# Optimizing a Trainium2 kernel written in Bass

```python
import numpy as np
import jax
import jax.numpy as jnp

def _softmax(x, axis=-1):
    return jax.nn.softmax(x, axis=axis)

def _gelu(x):
    return jax.nn.gelu(x, approximate=True)

def _silu(x):
    return jax.nn.silu(x)

def _sigmoid(x):
    return jax.nn.sigmoid(x)

def _layernorm(x, axis=-1, eps=1e-05):
    m = jnp.mean(x, axis=axis, keepdims=True)
    v = jnp.var(x, axis=axis, keepdims=True)
    return (x - m) / jnp.sqrt(v + eps)

def _scatter_add(tgt, idx, src, axis=0):
    return tgt.at[idx].add(src)

def _segment_sum(src, seg, n):
    return jax.ops.segment_sum(src, seg, n)
kernel_name = 'mk_gnn_ffn_d1_gnn_r16_9a5b85'

def setup_inputs(seed: int=0):
    np.random.seed(seed)
    _w = jnp.asarray

    def _rec_inputs():
        import jax
        import jax.numpy as jnp
        _gk = jax.random.key(seed)
        x = -0.0003713 + 1 * jax.random.normal(jax.random.fold_in(_gk, 1), (3125, 256), jnp.float32)
        _s = jax.random.randint(jax.random.fold_in(_gk, 2), (50000,), 0, 3125, jnp.int32)
        _d = jax.random.randint(jax.random.fold_in(_gk, 3), (50000,), 0, 3125, jnp.int32)
        _loop = jnp.arange(3125, dtype=jnp.int32)
        src = jnp.concatenate([_s, _d, _loop])
        dst = jnp.concatenate([_d, _s, _loop])
        _o = jnp.argsort(dst, stable=True)
        src = src[_o]
        dst = dst[_o]
        return (x, src, dst)
    x, src, dst = _rec_inputs()

    def _L0_gnn_setup():
        import jax, jax.numpy as jnp
        import numpy as np
        N_NODES = 3125
        N_EDGES = 50000
        D_IN = 256
        D_HID = 256
        D_OUT = 256
        GAMMA = 0.0
        K_STEPS = 6

        def _spmm(h, src, dst, inv_deg):
            msg = h[src]
            agg = jax.ops.segment_sum(msg, dst, num_segments=h.shape[0])
            return agg * inv_deg[:, None]

        def _linear_diffusion(h, src, dst, gamma=GAMMA, k=K_STEPS):
            n = h.shape[0]
            deg = jax.ops.segment_sum(jnp.ones((src.shape[0],), h.dtype), dst, num_segments=n)
            inv_deg = 1.0 / jnp.clip(deg, 1.0)
            out = h
            term = h
            for i in range(1, k + 1):
                term = (_spmm(term, src, dst, inv_deg) + gamma * term) / float(i)
                out = out + term
            return out
        key = jax.random.key(seed)
        ks = jax.random.split(key, 8)
        h = jax.random.normal(ks[0], (N_NODES, D_IN), dtype=jnp.float32)
        src = jax.random.randint(ks[1], (N_EDGES,), 0, N_NODES, dtype=jnp.int64)
        dst = jax.random.randint(ks[2], (N_EDGES,), 0, N_NODES, dtype=jnp.int64)
        s_in = 1.0 / np.sqrt(D_IN)
        s_hid = 1.0 / np.sqrt(D_HID)
        W_in = jax.random.uniform(ks[3], (D_HID, D_IN), jnp.float32, -s_in, s_in)
        b_in = jax.random.uniform(ks[4], (D_HID,), jnp.float32, -s_in, s_in)
        W_out = jax.random.uniform(ks[5], (D_OUT, D_HID), jnp.float32, -s_hid, s_hid)
        b_out = jax.random.uniform(ks[6], (D_OUT,), jnp.float32, -s_hid, s_hid)
        return {'h': h, 'src': src, 'dst': dst, 'W_in': W_in, 'b_in': b_in, 'W_out': W_out, 'b_out': b_out}
    _L0_gnn_all = _L0_gnn_setup()
    _L0_gnn_in = {k: v for k, v in _L0_gnn_all.items() if k in ('W_in', 'b_in', 'W_out', 'b_out')}
    del _L0_gnn_all

    def _L0_ffn_setup():
        import jax, jax.numpy as jnp
        import numpy as np
        E = 8
        K = 2
        D = 256
        H = 512
        DOUT = 256
        EPS = 1e-05
        key = jax.random.key(seed)
        ks = jax.random.split(key, 9)
        s = 0.02
        return {'x': jax.random.normal(ks[0], (4, 512, D), jnp.float32), 'gamma': 1.0 + 0.05 * jax.random.normal(ks[1], (D,), jnp.float32), 'beta': 0.05 * jax.random.normal(ks[2], (D,), jnp.float32), 'Wr': 0.01 * jax.random.normal(ks[3], (D, E), jnp.float32), 'br': jnp.zeros((E,), jnp.float32), 'W1': s * jax.random.normal(ks[4], (E, D, H), jnp.float32), 'b1': s * jax.random.normal(ks[5], (E, H), jnp.float32), 'W2': s * jax.random.normal(ks[6], (E, H, DOUT), jnp.float32), 'b2': s * jax.random.normal(ks[7], (E, DOUT), jnp.float32)}
    _L0_ffn_all = _L0_ffn_setup()
    _L0_ffn_in = {k: v for k, v in _L0_ffn_all.items() if k in ('gamma', 'beta', 'Wr', 'br', 'W1', 'b1', 'W2', 'b2')}
    del _L0_ffn_all
    return {'x': x, 'src': src, 'dst': dst, 'L0_gnn_W_in': _L0_gnn_in['W_in'], 'L0_gnn_b_in': _L0_gnn_in['b_in'], 'L0_gnn_W_out': _L0_gnn_in['W_out'], 'L0_gnn_b_out': _L0_gnn_in['b_out'], 'L0_ffn_gamma': _L0_ffn_in['gamma'], 'L0_ffn_beta': _L0_ffn_in['beta'], 'L0_ffn_Wr': _L0_ffn_in['Wr'], 'L0_ffn_br': _L0_ffn_in['br'], 'L0_ffn_W1': _L0_ffn_in['W1'], 'L0_ffn_b1': _L0_ffn_in['b1'], 'L0_ffn_W2': _L0_ffn_in['W2'], 'L0_ffn_b2': _L0_ffn_in['b2']}

def reference(x, src, dst, L0_gnn_W_in, L0_gnn_b_in, L0_gnn_W_out, L0_gnn_b_out, L0_ffn_gamma, L0_ffn_beta, L0_ffn_Wr, L0_ffn_br, L0_ffn_W1, L0_ffn_b1, L0_ffn_W2, L0_ffn_b2):
    import jax
    import jax.numpy as jnp

    def _L0_gnn_ref(h, src, dst, W_in, b_in, W_out, b_out):
        import jax, jax.numpy as jnp
        import numpy as np
        N_NODES = 3125
        N_EDGES = 50000
        D_IN = 256
        D_HID = 256
        D_OUT = 256
        GAMMA = 0.0
        K_STEPS = 6

        def _spmm(h, src, dst, inv_deg):
            msg = h[src]
            agg = jax.ops.segment_sum(msg, dst, num_segments=h.shape[0])
            return agg * inv_deg[:, None]

        def _linear_diffusion(h, src, dst, gamma=GAMMA, k=K_STEPS):
            n = h.shape[0]
            deg = jax.ops.segment_sum(jnp.ones((src.shape[0],), h.dtype), dst, num_segments=n)
            inv_deg = 1.0 / jnp.clip(deg, 1.0)
            out = h
            term = h
            for i in range(1, k + 1):
                term = (_spmm(term, src, dst, inv_deg) + gamma * term) / float(i)
                out = out + term
            return out
        x = h @ W_in.T + b_in
        x = jax.nn.silu(x)
        x = _linear_diffusion(x, src, dst)
        x = x @ W_out.T + b_out
        return x

    def _L0_ffn_ref(x, gamma, beta, Wr, br, W1, b1, W2, b2):
        import jax, jax.numpy as jnp
        import numpy as np
        E = 8
        K = 2
        D = 256
        H = 512
        DOUT = 256
        EPS = 1e-05
        mu = jnp.mean(x, axis=-1, keepdims=True)
        var = jnp.mean(jnp.square(x - mu), axis=-1, keepdims=True)
        xn = (x - mu) * jax.lax.rsqrt(var + EPS) * gamma + beta
        logits = jnp.einsum('bsd,de->bse', xn, Wr) + br
        top_vals, top_idx = jax.lax.top_k(logits, K)
        w = jax.nn.softmax(top_vals, axis=-1)
        w_full = jnp.einsum('bsk,bske->bse', w, jax.nn.one_hot(top_idx, E, dtype=w.dtype))
        y = jnp.zeros(x.shape[:-1] + (DOUT,), x.dtype)
        for e in range(E):
            h = jax.nn.gelu(jnp.einsum('bsd,dh->bsh', xn, W1[e]) + b1[e], approximate=False)
            y_e = jnp.einsum('bsh,hd->bsd', h, W2[e]) + b2[e]
            y = y + y_e * w_full[..., e, None]
        return y
    x = x + _L0_gnn_ref(_layernorm(x, axis=-1), src, dst, L0_gnn_W_in, L0_gnn_b_in, L0_gnn_W_out, L0_gnn_b_out)
    x = x + _L0_ffn_ref(_layernorm(x, axis=-1)[None], L0_ffn_gamma, L0_ffn_beta, L0_ffn_Wr, L0_ffn_br, L0_ffn_W1, L0_ffn_b1, L0_ffn_W2, L0_ffn_b2)[0]
    return x

_drawn_inputs = setup_inputs


def setup_inputs(seed=0):
    import zlib

    import numpy as np

    out = dict(_drawn_inputs(seed))
    spreads = {'L0_ffn_br': (0.0, 0.1)}
    factors = {'L0_ffn_gamma': 6.525, 'L0_ffn_beta': 5.26, 'L0_ffn_b1': 8.0, 'L0_ffn_b2': 4.369}
    for name, (base, spread) in spreads.items():
        noise = np.random.default_rng([zlib.crc32(name.encode()), seed]).standard_normal(out[name].shape)
        drawn = base * np.exp(spread * noise) if base else spread * noise
        out[name] = jnp.asarray(drawn.astype(out[name].dtype))
    for name, factor in factors.items():
        out[name] = (out[name] * factor).astype(out[name].dtype)
    return out
```

```python
from contextlib import ExitStack

import concourse.bass as bass
from concourse import mybir

F32 = mybir.dt.float32
F16 = mybir.dt.float16
I32 = mybir.dt.int32
ALU = mybir.AluOpType
ACT = mybir.ActivationFunctionType
AX = mybir.AxisListType

ROUND = 1.5 * 2.0**23


def gnn_ffn(nc, x, src, dst, W_in, b_in, W_out, b_out, gamma, beta, Wr, br, W1, b1, W2, b2, out):
    N, D = x.shape
    E = src.shape[0]
    NP = 125
    T = N // NP
    DK = D // 128
    WIN = 5
    NR = T // WIN
    Q = WIN * T
    SL = 2
    SLOTS = SL * NP
    GRAN = 25
    ROWS = (E - SLOTS) // GRAN + 1
    COARSE = E // GRAN // NP
    STEPS = 6
    C = WIN * SL
    NB = T // WIN
    assert N == NP * T and E % (GRAN * NP) == 0 and (E - SLOTS) % GRAN == 0

    NE, _, H = W1.shape
    HK = H // 128
    TOP = 2
    FT = (TOP * N + NE * 127) // 128
    FU = 8
    FR = 4
    LEAD = 4
    assert FT % FU == 0

    EC = E // NP
    EU = 5
    PARTS = ((0, (T + 1) // 2), ((T + 1) // 2, T // 2))
    assert EC % EU == 0 and PARTS[0][1] * D <= 7 * 512
    term_dram = nc.dram_tensor("term_dram", (N, D), F32, kind="Internal").ap()
    xs_dram = nc.dram_tensor("xs_dram", (N, 2 * D), F16, kind="Internal").ap()
    y_dram = nc.dram_tensor("y_dram", (TOP * N, D), F32, kind="Internal").ap()
    xs_v = xs_dram.rearrange("(p t) f -> p t f", t=T)
    y_v = y_dram.rearrange("(k p t) f -> k p t f", k=TOP, t=T)
    out_v = out.rearrange("(p t) f -> p t f", t=T)
    edge_rows = nc.dram_tensor("edge_rows", (ROWS, 2 * SLOTS), I32, kind="Internal").ap()
    h_dram = nc.dram_tensor("h_dram", (N, D), F32, kind="Internal").ap()
    x_v = x.rearrange("(p t) f -> p t f", t=T)
    h_v = h_dram.rearrange("(p t) f -> p t f", t=T)
    term_v = term_dram.rearrange("(p t) f -> p t f", t=T)

    with ExitStack() as ctx:
        def sb(name, shape, dt):
            return ctx.enter_context(nc.sbuf_tensor(name, shape, dt))

        def sem(name):
            return ctx.enter_context(nc.semaphore(name))

        ADJ = T * T * NP
        REG = 3126
        adj = sb("adj", [128, T * REG], F16)
        v_a = sb("v_a", [128, T * 2 * D], F16)
        v_b = sb("v_b", [128, T * 2 * D], F16)
        ps = ctx.enter_context(nc.psum_tensor("ps", [128, 8, 512], F32))

        def over(buf, at, n, dt, parts=128):
            size = 4 if dt in (F32, I32) else 2
            v = buf[0:parts, at // 2:at // 2 + n * size // 2]
            return v if dt == F16 else v.bitcast(dt)

        adj_w = adj[0:NP, 0:ADJ].rearrange("b (r q p) -> b r q p", r=NR, q=Q)
        adj_t = adj[0:NP, 0:ADJ].rearrange("b (t a p) -> b t a p", t=T, a=T)
        va = v_a[0:NP, :].rearrange("p (t f) -> p t f", t=T)
        vb = v_b[0:NP, :].rearrange("p (t f) -> p t f", t=T)

        cinv = sb("cinv", [128, STEPS, T], F32)
        h_ring = sb("h_ring", [128, 2, D], F32)
        t_hi = sb("t_hi", [128, D], F32)
        v_f = sb("v_f", [128, D], F32)
        scale = sb("scale", [128, 2], F32)

        in_windows = sb("in_windows", [128, 1], F32)
        covered = sb("covered", [1, 1], I32)

        at = (T - WIN) * T * NP * 2
        x_all = over(adj, at, T * D, F32, NP).rearrange("p (t f) -> p t f", t=T)
        at = 0

        def take(n, dt, parts=128):
            nonlocal at
            v = over(adj, at, n, dt, parts)
            at += (n * (4 if dt in (F32, I32) else 2) + 3) // 4 * 4
            return v

        dst_all = take(E // NP, I32, NP)
        above = take(COARSE * N // WIN, F16, NP).rearrange("p (j g) -> p j g", j=COARSE)
        iota_g = take(N // WIN, F16)
        key = take(COARSE, F32)
        key_t = take(COARSE, F32)
        ones16 = take(2, F16)
        starts = take(NR, F32)
        start_row = take(NR, I32)
        g_edges = take(NR * 2 * SLOTS, I32, NP).rearrange("p (r s) -> p r s", r=NR)
        e_src = take(NR * SLOTS, F32, NP).rearrange("p (r s) -> p r s", r=NR)
        e_b = take(NR * SLOTS, F32, NP).rearrange("p (r s) -> p r s", r=NR)
        e_q = take(NR * SLOTS, F32, NP).rearrange("p (r s) -> p r s", r=NR)
        e_d = take(NR * SLOTS, F32, NP).rearrange("p (r s) -> p r s", r=NR)
        win_base = take(NR, F32)
        dl_eq = take(WIN * SLOTS, F32, NP).rearrange("p (d s) -> p d s", d=WIN)
        dl25 = take(WIN, F32)
        deg = take(T, F32)
        degc = take(T, F32)
        iota_row = take(128, F32)
        iota_col = take(1, F32)
        ident = take(128, F32)
        ones32 = take(128, F32)
        w_raw = take(DK * D, F32).rearrange("o (b k) -> o b k", b=DK)
        w_sq = take(DK * D, F32).rearrange("o (b k) -> o b k", b=DK)
        w_inT = take(DK * D, F32).rearrange("k (b o) -> k b o", b=DK)
        b_row = take(D, F32)
        b_col = take(DK, F32)
        b_sq = take(DK, F32)
        bound = take(DK, F32)
        bmax = take(1, F32)
        ball = take(1, F32)
        exp_i = take(1, I32)
        exp_j = take(2, I32)
        stats = take(T * 6, F32).rearrange("p (t s) -> p t s", s=6)
        mv = take(T * 2, F32).rearrange("p (t s) -> p t s", s=2)
        rstd = take(T, F32)
        rtmp = take(T, F32)
        ve = take(T, F32)
        xT = [take(DK * NP, F32).rearrange("k (b p) -> k b p", b=DK) for _ in range(3)]
        x_n = [take(D, F32, NP) for _ in range(WIN)]
        h_f = [take(D, F32) for _ in range(3)]
        h_s = [take(D, F32) for _ in range(3)]
        assert at <= (T - WIN) * T * NP * 2, at

        at = 0

        def take_b(n, dt):
            nonlocal at
            v = over(v_b, at, n, dt, NP)
            at += n * 2
            return v

        iota_x = take_b(NP * C, F16).rearrange("e (x c) -> e x c", c=C)
        key_b = take_b(NP * C, F16).rearrange("e (r i k j) -> e r i k j", r=NR, k=SL, j=WIN)
        key_q = take_b(NP * C, F16).rearrange("e (r i k j) -> e r i k j", r=NR, k=SL, j=WIN)
        oh_b = [take_b(NP * C, F16).rearrange("e (x c) -> e x c", c=C) for _ in range(3)]
        oh_q = [take_b(NP * C, F16).rearrange("e (x c) -> e x c", c=C) for _ in range(3)]
        assert at <= T * 2 * D * 2

        x1 = adj[0:NP, :].bitcast(F32).rearrange("p (t r) -> p t r", t=T)[:, :, 0:D]
        XW = 2 * D
        EW = DK * H
        ex16 = adj[:, 0:3 * NE * REG].rearrange("p (e r) -> p e r", e=NE)
        ex32 = adj[:, 0:3 * NE * REG].bitcast(F32).rearrange("p (e r) -> p e r", e=NE)
        w1h, w1l = ex16[:, :, XW:XW + EW], ex16[:, :, XW + EW:XW + 2 * EW]
        w2h, w2l = ex16[:, :, REG + XW:REG + XW + EW], ex16[:, :, REG + XW + EW:REG + XW + 2 * EW]
        b2_bc = ex32[:, :, (XW + 2 * EW) // 2:(XW + 2 * EW) // 2 + D]
        w_f32 = ex32[:, :, (2 * REG + XW) // 2:(2 * REG + XW) // 2 + EW]
        assert EW == HK * D and XW + 2 * EW + 2 * D <= REG

        def taker(buf):
            used = [0]

            def take(n, dt, parts=128):
                v = over(buf, used[0], n, dt, parts)
                used[0] += (n * (4 if dt in (F32, I32) else 2) + 3) // 4 * 4
                assert used[0] <= (T * REG * 2 if buf is adj else T * 2 * D * 2), used
                return v
            return take

        fa = taker(v_a)
        ident2 = fa(128, F32)
        ident16 = fa(128, F16)
        ones2 = fa(128, F32)
        w_outT = fa(DK * D, F32).rearrange("k (b o) -> k b o", b=DK)
        bo_bc, ga_bc, be_bc = fa(D, F32), fa(D, F32), fa(D, F32)
        wr_sb = fa(DK * NE, F32).rearrange("k (b e) -> k b e", b=DK)
        br_bc = fa(NE, F32)
        lg = fa(T * NE, F32, NP).rearrange("p (t e) -> p t e", t=T)
        stats2 = fa(6, F32, NP)
        mv_t = fa(2, F32, NP)
        mv2 = fa(2 * T, F32, NP).rearrange("p (t s) -> p t s", s=2)
        ve2, sd2, rt2, r1 = (fa(WIN, F32, NP) for _ in range(4))
        rr = fa(T, F32, NP)
        gb_max = fa(2, F32)
        gb_sq = fa(2, F32)
        xn_sq = fa(2, F32)
        xs_scale = fa(2, F32)
        pow_i = fa(NE, I32)
        pow_j = fa(NE, I32)
        s1, s2, sh, i1, i2, ih, g1, g2 = (fa(NE, F32) for _ in range(8))
        w_max = fa(NE * (DK + HK), F32)
        w_sq2 = fa(NE * (DK + HK + HK), F32)
        w_sums = fa(NE * 3, F32).rearrange("p (a e) -> p a e", e=NE)
        b1T = fa(NE * HK, F32)
        tri = fa(NP, F32, NP)
        iota_e8 = fa(NE, F32, NP)
        iota_pos = fa(128, F16, NP)
        iota_tile = fa(FT, F16, NP)
        tile_row = fa(FT, F32)
        p_plus1 = fa(1, F32)
        ta_b = fa(T * TOP, F32)
        w_top1, w_top2 = fa(T, F32, NP), fa(T, F32, NP)
        idx_g, idx_s = fa(FT, I32), fa(FT, I32)
        exp_of = over(v_a, T * 2 * D * 2 - T * TOP * 2 * FT * 2 - 16 * (FT + LEAD), FT + LEAD, I32)
        vfin = [fa(D, F32, NP) for _ in range(3)]
        vT = fa(DK * NP, F32).rearrange("k (b p) -> k b p", b=DK)
        x_i = [fa(D, F32, NP) for _ in range(3)]
        xn2 = [fa(D, F32, NP) for _ in range(3)]
        xnT = fa(DK * NP, F32).rearrange("k (b p) -> k b p", b=DK)
        xs_f = fa(3 * 2 * D, F16)
        xs_r = [xs_f[0:NP, j * 2 * D:(j + 1) * 2 * D] for j in range(3)]
        w_oraw = xs_f[:, 0:2 * DK * D].bitcast(F32).rearrange("o (b k) -> o b k", b=DK)
        fb = taker(v_b)
        b1_rows = fb(128, F32, NE * HK)
        oh1, oh2, tmp1, tmp2, both, sum_a, sum_b, pos = (fb(T * NE, F32, NP).rearrange("p (t e) -> p t e", t=T) for _ in range(8))
        m1, m2, n1, slot1, slot2, ex2, den = (fb(T, F32, NP) for _ in range(7))
        per_p = fb(NE, F32, NP)
        totals, tiles_a, tiles_b, tiles_c = (fb(NE, F32) for _ in range(4))
        slot_base = fb(NE, F32, NP)
        s_all, s_tile, s_pin = (fb(T * TOP, F32, NP) for _ in range(3))
        tok_p, tok_b, dest, empty = (fb(FT, F32) for _ in range(4))
        le_tiles = fb(FT * NE, F32).rearrange("p (j e) -> p j e", e=NE)
        oh_pos = fb(T * TOP * 128, F16, NP).rearrange("p (c x) -> p c x", x=128)
        PL = 2 * FT
        planes = over(v_a, T * 2 * D * 2 - T * TOP * PL * 2, T * TOP * PL, F16, NP).rearrange("p (c y) -> p c y", y=PL)
        fc = taker(v_b)
        x_g = [fc(2 * D, F16) for _ in range(FU)]
        xT16 = [fc(2 * D, F16).rearrange("k (b s) -> k b s", b=2 * DK) for _ in range(2)]
        h_g = [fc(H, F32) for _ in range(2)]
        h_hi = [fc(H, F16).rearrange("h (b s) -> h b s", b=HK) for _ in range(FR)]
        h_lo = [fc(H, F16).rearrange("h (b s) -> h b s", b=HK) for _ in range(FR)]
        at_y = ((T - 1) * REG + XW) * 2
        y_sb = [over(adj, at_y + r * D * 4, D, F32) for r in range(FR)]
        ig = [fc(1, I32) for _ in range(FU)]
        isc = [fc(1, I32) for _ in range(FR)]
        fd = taker(v_b)
        y_in = [[fd(WIN * D, F32, NP).rearrange("p (t f) -> p t f", t=WIN) for _ in range(TOP)] for _ in range(2)]

        fe = taker(adj)
        src_e, dst_i = fe(EC, I32, NP), fe(EC, I32, NP)
        dst_e = fe(EC, F32, NP)
        node = fe(N, F32, NP).rearrange("e (t p) -> e t p", t=T)
        oh_e = [fe(PARTS[0][1] * NP, F32, NP).rearrange("e (t p) -> e t p", p=NP) for _ in range(EU)]
        rows_e = [fe(D, F32, NP) for _ in range(EU)]
        src_col = [fe(1, I32, NP) for _ in range(EU)]
        ones_e, zeros_e = fe(1, F32, NP), fe(512, F32, 1)
        k_inv = fe(STEPS, F32, NP)
        deg_e = fe(T, F32, NP)
        term_e = fe(T * D, F32, NP).rearrange("p (t f) -> p t f", t=T)
        h_e = fe(T * D, F32, NP).rearrange("p (t f) -> p t f", t=T)

        names = """rows_made dst_in x_in w_in_in iotas ident_ok key_ok above_ok count_ok start_ok
            keys_ok keyT_ps keyT_ok stats_ok std_ok rstd_ok wT_ps wT_ok bound_ok ball_ok scale_ok xn_ok xT_ps xT_ok
            h_ps h_act v_ready oh_ready win_ps win_out tile_ps hi_ok psum_read h_used
            f_const pool_const bo_mat w_oT_ps w_oT_ok vfin_ok vT_ps vT_ok y_ps xb_ok x1_ok ve_ok sd_ok z_ok xn2_ok xnT_ps xnT_ok
            lg_ps lg_ok xhi_ok xs_ok b1_in b1T_ps b1T_ok w_sq_ok w_sum_ps w1_hi w1_lo w2_hi w2_lo wsc_ok
            ex_in ex_ok cnt_in cnt_ok rt_done tok_ps idx_ok
            pool_turn cover_sum cover_ps cover_ok term_ok e_const e_in e_col e_oh e_mm e_acc e_read e_term e_rows
            ig_ok is_ok xg_T xgT_ok ffn_h gelu_ok hs_ok ffn_y y_ok y_free comb_ok""".split()
        S = {n: sem(n) for n in names}
        gathered = [sem(f"gathered{r}") for r in range(NR)]
        h_in = [sem(f"h_in{r}") for r in range(2)]
        h_out = [sem(f"h_out{r}") for r in range(3)]
        xs_out = [sem(f"xs_out{r}") for r in range(3)]
        xi_in = [sem(f"xi_in{r}") for r in range(3)]
        w1_in = sem("w1_in")
        w2_in = [sem(f"w2_in{e}") for e in range(NE)]
        g_in = [sem(f"g_in{r}") for r in range(FU)]
        y_out = [sem(f"y_out{r}") for r in range(FR)]
        yc_in = [sem(f"yc_in{r}") for r in range(2)]
        out_sem = sem("out_sem")
        e_gathered = [sem(f"e_gathered{r}") for r in range(EU)]

        block = ctx.enter_context(nc.Block())
        RB = [0, 1, 2, 0, 1]
        PRIOR = [(2, 0), (2, 0), (1, 0), (2, 1), (2, 1)]
        LAST = (STEPS - 1) * T

        def ring(d, u):
            return RB[(u - d) % WIN]

        def uses(i, u, d):
            w = (u - d) % WIN
            group = i + (u - d - w) // WIN
            return PRIOR[w][0] * group + PRIOR[w][1]

        def need(eng, s, value):
            if not (isinstance(value, int) and value <= 0):
                eng.wait_ge(s, value)

        def experts(i, eng):
            _, es = nc.values_load_multi_w_load_instructions(
                exp_of[0:1, bass.ds(FU * i, LEAD + FU)], engines=[eng.engine], min_val=0, max_val=NE - 1,
                skip_runtime_bounds_check_because="a minimum with NE - 1 of a count made exp_of")
            return es

        def last_step(eng, body):
            def peeled(i):
                for u in range(WIN):
                    body(i, u, lambda d: 0 <= WIN * i + u - d < T)
            peeled(0)
            peeled(1)
            with eng.Fori(2, NB) as i:
                for u in range(WIN):
                    body(i, u, lambda d: True)
            peeled(NB)
            peeled(NB + 1)

        @block.sync
        def _(sp):
            sp.dma_start(dst_all, dst.rearrange("(p e) -> p e", p=NP)).then_inc(S["dst_in"], 16)
            for half, a in enumerate((src, dst)):
                rows = bass.AP(a.tensor, 0, [[GRAN, ROWS], [1, SLOTS]])
                sp.dma_start(edge_rows[:, half * SLOTS:(half + 1) * SLOTS], rows).then_inc(S["rows_made"], 16)
            with sp.Fori(0, NB) as i:
                for u in range(WIN):
                    sp.wait_ge(S["v_ready"], 5 * i + u + 1)
                    sp.dma_start(h_v[:, bass.ds(5 * i + u, 1), :].rearrange("p a f -> p (a f)"), h_s[RB[u]][0:NP, :]).then_inc(h_out[RB[u]], 16)
            for slot, per in enumerate((2, 2, 1)):
                sp.wait_ge(h_out[slot], 16 * per * NB)

            def step(n0):
                with sp.Fori(0, NB) as i:
                    for u in range(WIN):
                        n = n0 + 5 * i + u
                        if u == 0:
                            sp.wait_ge(S["h_used"], n + 2)
                        elif u > 1:
                            sp.wait_ge(S["h_used"], n + 1)
                        sp.dma_start(h_ring[0:NP, u % 2, :],
                                     h_v[:, bass.ds(5 * i + u, 1), :].rearrange("p a f -> p (a f)")).then_inc(h_in[u % 2], 16)
            for s in range(STEPS - 1):
                step(s * T)
            sp.wait_ge(S["term_ok"], 1)

            def bc(v, n):
                return bass.AP(v.tensor, 0, [[0, 128], [1, n]])
            sp.dma_start(w_oraw, W_out.rearrange("(b o) k -> o b k", o=128)).then_inc(S["f_const"], 16)
            sp.dma_start(bo_bc, bc(b_out, D)).then_inc(S["f_const"], 16)
            sp.dma_start(ga_bc, bc(gamma, D)).then_inc(S["f_const"], 16)
            sp.dma_start(be_bc, bc(beta, D)).then_inc(S["f_const"], 16)
            sp.dma_start(wr_sb, Wr.rearrange("(b k) e -> k b e", k=128)).then_inc(S["f_const"], 16)
            sp.dma_start(br_bc, bc(br, NE)).then_inc(S["f_const"], 16)

            def body(i, u, has):
                m = 5 * i + u
                n = LAST + m
                if has(0):
                    if u == 0:
                        sp.wait_ge(S["h_used"], n + 2)
                    elif u > 1:
                        sp.wait_ge(S["h_used"], n + 1)
                    sp.dma_start(h_ring[0:NP, u % 2, :],
                                 h_v[:, bass.ds(m, 1), :].rearrange("p a f -> p (a f)")).then_inc(h_in[u % 2], 16)
                    need(sp, S["x1_ok"], m - 1)
                    sp.dma_start(x_i[RB[u]], x_v[:, bass.ds(m, 1), :].rearrange("p a f -> p (a f)")).then_inc(xi_in[RB[u]], 16)
                if has(8):
                    sp.wait_ge(S["xs_ok"], m - 7)
                    sp.dma_start(xs_v[:, bass.ds(m - 8, 1), :].rearrange("p a f -> p (a f)"), xs_r[ring(8, u)]).then_inc(xs_out[ring(8, u)], 16)
            last_step(sp, body)
            sp.dma_start(b1_rows, b1.rearrange("e (b h) -> (e b) h", h=128)).then_inc(S["b1_in"], 16)
            for b in range(DK):
                sp.dma_start(w_f32[:, :, b * H:(b + 1) * H], W1[:, b * 128:(b + 1) * 128, :].rearrange("e k h -> k e h")).then_inc(w1_in, 16)
            sp.dma_start(b2_bc, bass.AP(b2.tensor, 0, [[0, 128], [D, NE], [1, D]])).then_inc(S["b1_in"], 16)
            for e in range(NE):
                sp.wait_ge(S["w1_lo"], e + 1)
                sp.dma_start(w_f32[:, e, :].rearrange("h (b d) -> h b d", b=HK),
                             W2[e].rearrange("(b h) d -> h b d", h=128)).then_inc(w2_in[e], 16)
            for r in range(FR):
                sp.wait_ge(y_out[r], 16 * (FT // FR))
            for i in range(NB):
                if i >= 2:
                    sp.wait_ge(S["comb_ok"], i - 1)
                for k in range(TOP):
                    sp.dma_start(y_in[i % 2][k], y_v[k, :, i * WIN:(i + 1) * WIN, :]).then_inc(yc_in[i % 2], 16)
            for i in range(NB):
                sp.wait_ge(S["comb_ok"], i + 1)
                sp.dma_start(out_v[:, i * WIN:(i + 1) * WIN, :], x1[:, i * WIN:(i + 1) * WIN, :]).then_inc(out_sem, 16)
            sp.wait_ge(out_sem, 16 * NB)

        @block.gpsimd
        def _(pool):
            g = nc.gpsimd
            g.iota(iota_g, [[1, N // WIN]], base=0, channel_multiplier=0, allow_small_or_imprecise_dtypes=True)
            g.memset(ones16, 1.0).then_inc(S["iotas"], 1)
            g.iota(iota_row, [[1, 128]], base=0, channel_multiplier=0, allow_small_or_imprecise_dtypes=True)
            g.iota(iota_col, [[0, 1]], base=0, channel_multiplier=1, allow_small_or_imprecise_dtypes=True)
            g.iota(win_base, [[T * WIN, NR]], base=0, channel_multiplier=T * T, allow_small_or_imprecise_dtypes=True)
            g.iota(dl25, [[T, WIN]], base=0, channel_multiplier=0, allow_small_or_imprecise_dtypes=True)
            g.memset(ones32, 1.0).then_inc(S["iotas"], 1)
            g.iota(iota_x, [[1, NP], [0, C]], base=0, channel_multiplier=0,
                   allow_small_or_imprecise_dtypes=True).then_inc(S["iotas"], 1)
            pool.wait_ge(S["rows_made"], 32)
            pool.wait_ge(S["start_ok"], 1)
            for r in range(NR):
                g.indirect_dma_start(g_edges[:, r, :], None, edge_rows,
                                     bass.IndirectOffsetOnAxis(ap=start_row[0:NP, r:r + 1], axis=0),
                                     ).then_inc(gathered[r], 16)
            pool.wait_ge(S["bound_ok"], 1)
            g.partition_all_reduce(ball, bmax, 128, bass.bass_isa.ReduceOp.max).then_inc(S["ball_ok"], 1)
            pool.wait_ge(S["cover_ok"], 1)
            fast = pool.value_load(covered[:, :], min_val=0, max_val=1)
            with pool.If(fast == 0):
                pool.wait_ge(S["v_ready"], T * STEPS)
                for slot, per in enumerate((2, 2, 1)):
                    pool.wait_ge(h_out[slot], 16 * per * NB)
                g.dma_start(src_e, src.rearrange("(p e) -> p e", p=NP)).then_inc(S["e_in"], 16)
                g.dma_start(dst_i, dst.rearrange("(p e) -> p e", p=NP)).then_inc(S["e_in"], 16)
                g.dma_start(h_e, h_v).then_inc(S["e_in"], 16)
                g.dma_start(term_v, h_v).then_inc(S["e_rows"], 16)
                g.iota(node, [[1, T], [T, NP]], base=0, channel_multiplier=0, allow_small_or_imprecise_dtypes=True)
                g.memset(ones_e, 1.0)
                for s in range(STEPS):
                    g.memset(k_inv[:, s:s + 1], 1.0 / (STEPS - s))
                g.memset(zeros_e, 0.0).then_inc(S["e_const"], 1)
                pool.wait_ge(S["e_in"], 48)
                with pool.Fori(0, STEPS) as s:
                    pool.wait_ge(S["e_rows"], s * 16 + 16)
                    pool.sem_inc(S["pool_turn"], 1)
                    for part in range(2):
                        with pool.Fori(0, EC // EU) as i:
                            for u in range(EU):
                                n = s * (2 * EC) + i * EU + (part * EC + u)
                                pool.wait_ge(S["e_mm"], n + 1)
                                pool.sem_inc(S["pool_turn"], 1)
                                g.tensor_copy(src_col[u], src_e[:, bass.ds(i * EU + u, 1)]).then_inc(S["e_col"], 1)
                                pool.wait_ge(S["e_col"], n + 1)
                                pool.sem_inc(S["pool_turn"], 1)
                                g.indirect_dma_start(rows_e[u], None, term_dram,
                                                     bass.IndirectOffsetOnAxis(ap=src_col[u], axis=0)).then_inc(e_gathered[u], 16)
                    pool.wait_ge(S["e_term"], s + 1)
                    pool.sem_inc(S["pool_turn"], 1)
                    g.dma_start(term_v, term_e).then_inc(S["e_rows"], 16)
                pool.wait_ge(S["e_rows"], 16 * (STEPS + 1))
                g.dma_start(h_v, term_e).then_inc(S["e_rows"], 16)
            pool.wait_ge(S["term_ok"], 1)
            g.memset(ident2, 0.0)
            g.memset(ident16, 0.0)
            g.memset(ones2, 1.0)
            g.memset(tri, 1.0)
            g.iota(iota_e8, [[1, NE]], base=-NE, channel_multiplier=0, allow_small_or_imprecise_dtypes=True)
            g.iota(iota_pos, [[1, 128]], base=0, channel_multiplier=0, allow_small_or_imprecise_dtypes=True)
            g.iota(iota_tile, [[1, FT]], base=0, channel_multiplier=0, allow_small_or_imprecise_dtypes=True)
            g.iota(tile_row, [[1, FT]], base=0, channel_multiplier=0, allow_small_or_imprecise_dtypes=True)
            g.iota(p_plus1, [[0, 1]], base=1, channel_multiplier=1, allow_small_or_imprecise_dtypes=True)
            g.iota(ta_b, [[1, T * TOP]], base=0, channel_multiplier=0, allow_small_or_imprecise_dtypes=True).then_inc(S["bo_mat"], 1)
            pool.wait_ge(S["bo_mat"], 1)
            g.affine_select(out=ident2, in_=ident2, compare_op=ALU.not_equal, fill=1.0, base=0, pattern=[[-1, 128]], channel_multiplier=1)
            g.affine_select(out=ident16, in_=ident16, compare_op=ALU.not_equal, fill=1.0, base=0, pattern=[[-1, 128]], channel_multiplier=1)
            g.affine_select(out=tri, in_=tri, compare_op=ALU.is_gt, fill=0.0, base=0, pattern=[[1, NP]],
                            channel_multiplier=-1).then_inc(S["pool_const"], 1)
            pool.wait_ge(S["f_const"], 96)

            def body(i, u, has):
                m = 5 * i + u
                if has(7):
                    pool.wait_ge(S["z_ok"], m - 6)
                    g.tensor_tensor(xn2[ring(7, u)], xn2[ring(7, u)], be_bc[0:NP, :], ALU.add).then_inc(S["xn2_ok"], 1)
                if has(0):
                    pool.wait_ge(xi_in[RB[u]], 16 * (uses(i, u, 0) + 1))
                    g.tensor_tensor(x_i[RB[u]], x_i[RB[u]], bo_bc[0:NP, :], ALU.add).then_inc(S["xb_ok"], 1)
            last_step(pool, body)
            for r, per in enumerate((2, 2, 1)):
                pool.wait_ge(xs_out[r], 16 * per * NB)
            pool.wait_ge(S["idx_ok"], 1)

            def gather(i, u):
                j = FU * i + u
                need(pool, g_in[u], 16 * i)
                pool.sem_inc(S["pool_turn"], 1)
                g.tensor_copy(ig[u], idx_g[:, bass.ds(j, 1)]).then_inc(S["ig_ok"], 1)
                need(pool, S["xg_T"], j - FU + 1)
                pool.wait_ge(S["ig_ok"], j + 1)
                pool.sem_inc(S["pool_turn"], 1)
                g.indirect_dma_start(x_g[u], None, xs_dram, bass.IndirectOffsetOnAxis(ap=ig[u], axis=0)).then_inc(g_in[u], 16)

            def scatter(i, u):
                j = FU * i + u
                r = u % FR
                need(pool, y_out[r], 16 * (FU // FR * i + u // FR))
                pool.sem_inc(S["pool_turn"], 1)
                g.tensor_copy(isc[r], idx_s[:, bass.ds(j, 1)]).then_inc(S["is_ok"], 1)
                pool.wait_ge(S["y_ok"], j + 1)
                pool.wait_ge(S["is_ok"], j + 1)
                pool.sem_inc(S["pool_turn"], 1)
                g.indirect_dma_start(y_dram, bass.IndirectOffsetOnAxis(ap=isc[r], axis=0), y_sb[r], None,
                                     bounds_check=TOP * N - 1, oob_is_err=False).then_inc(y_out[r], 16)

            def tiles(i, last):
                for u in range(FU):
                    if not (last and u):
                        gather(i + (u + FU - 1) // FU, (u + FU - 1) % FU)
                    scatter(i, u)
            for u in range(FU - 1):
                gather(0, u)
            tiles(0, False)
            with pool.Fori(1, FT // FU - 1) as i:
                tiles(i, False)
            tiles(FT // FU - 1, True)

        @block.scalar
        def _(act):
            a = nc.scalar
            act.dma_start(x_all, x_v).then_inc(S["x_in"], 16)
            act.dma_start(w_raw, W_in.rearrange("(b o) k -> o b k", o=128)).then_inc(S["w_in_in"], 16)
            act.dma_start(b_row[0:1, :], b_in[None, :]).then_inc(S["w_in_in"], 16)
            act.dma_start(b_col, b_in.rearrange("(b o) -> o b", o=128), allow_slow_non_contiguous=True).then_inc(S["w_in_in"], 16)
            act.wait_ge(S["wT_ps"], 1)
            a.activation(w_inT, ps[:, 6, :].rearrange("k (b o) -> k b o", b=DK), ACT.Copy).then_inc(S["wT_ok"], 1)
            act.wait_ge(S["stats_ok"], 1)
            a.activation(rstd[0:NP, :], ve[0:NP, :], ACT.Sqrt).then_inc(S["std_ok"], 1)

            def features(i):
                for u in range(WIN):
                    n = WIN * i + u
                    act.wait_ge(S["xT_ps"], n + 1)
                    a.activation(xT[RB[u]], ps[:, RB[u], 0:DK * 128].rearrange("k (b p) -> k b p", b=DK)[:, :, 0:NP],
                                 ACT.Copy).then_inc(S["xT_ok"], 1)
                    act.wait_ge(S["h_ps"], n + 1)
                    need(act, S["v_ready"], n if u == 0 else n - 1)
                    a.activation(h_f[RB[u]][0:NP, :], ps[0:NP, 3 + RB[u], 0:D], ACT.Silu).then_inc(S["h_act"], 1)
            features(0)
            with act.Fori(1, NB) as i:
                features(i)
            for slot, per in enumerate((2, 2, 1)):
                act.wait_ge(h_out[slot], 16 * per * NB)
            with act.Fori(0, NR) as r:
                with act.Fori(0, NB) as i:
                    for u in range(WIN):
                        bt = 25 * r + 5 * i + u
                        act.wait_ge(S["win_ps"], bt + 1 + 2)
                        sl = RB[u]
                        cells = ps[0:NP, 2 * sl:2 * sl + 2, :].rearrange("b k (c q) -> b (k c) q", q=128)[:, 0:WIN, 0:Q]
                        a.activation(adj_w[:, bass.ds(r, 1), :, bass.ds(25 * i + 5 * u, WIN)].rearrange("b o q p -> b (o q) p"),
                                     cells.rearrange("b c q -> b q c"), ACT.Copy).then_inc(S["win_out"], 1)

            def step(n0, s):
                with act.Fori(0, NB) as i:
                    for u in range(WIN):
                        n = n0 + 5 * i + u
                        act.wait_ge(S["tile_ps"], n + 1)
                        act.wait_ge(S["psum_read"], n + 5)
                        a.activation(t_hi[0:NP, :], ps[0:NP, u, 0:D], ACT.Copy,
                                     scale=cinv[0:NP, s, bass.ds(5 * i + u, 1)]).then_inc(S["hi_ok"], 1)
            for s in range(STEPS - 1):
                step(s * T, s)
            act.wait_ge(S["w_oT_ps"], 1)
            a.activation(w_outT, ps[:, 7, :].rearrange("k (b o) -> k b o", b=DK), ACT.Copy).then_inc(S["w_oT_ok"], 1)

            def body(i, u, has):
                m = 5 * i + u
                n = LAST + m
                if u == 2 and has(7):
                    for k in range(2):
                        act.wait_ge(S["ve_ok"], 2 * i + k - 1)
                        a.activation(sd2, ve2, ACT.Sqrt).then_inc(S["sd_ok"], 1)
                if has(7):
                    act.wait_ge(S["xn2_ok"], m - 6)
                    need(act, xs_out[ring(7, u)], 16 * uses(i, u, 7))
                    a.activation(xs_r[ring(7, u)][:, 0:D], xn2[ring(7, u)], ACT.Copy, scale=xs_scale[0:NP, 0:1]).then_inc(S["xhi_ok"], 1)
                if has(0):
                    act.wait_ge(S["tile_ps"], n + 1)
                    act.wait_ge(S["psum_read"], n + 5)
                    a.activation(t_hi[0:NP, :], ps[0:NP, RB[u], 0:D], ACT.Copy,
                                 scale=cinv[0:NP, STEPS - 1, bass.ds(m, 1)]).then_inc(S["hi_ok"], 1)
                if has(7):
                    act.wait_ge(S["xnT_ps"], m - 6)
                    need(act, S["lg_ps"], m - 7)
                    a.activation(xnT, ps[:, 4, 0:DK * 128].rearrange("k (b p) -> k b p", b=DK)[:, :, 0:NP], ACT.Copy).then_inc(S["xnT_ok"], 1)
                if has(1):
                    act.wait_ge(S["vT_ps"], m)
                    need(act, S["y_ps"], m - 1)
                    a.activation(vT, ps[:, 3, 0:DK * 128].rearrange("k (b p) -> k b p", b=DK)[:, :, 0:NP], ACT.Copy).then_inc(S["vT_ok"], 1)
            last_step(act, body)
            act.wait_ge(S["b1T_ps"], 1)
            a.activation(b1T, ps[:, 5, 0:NE * HK], ACT.Copy).then_inc(S["b1T_ok"], 1)
            act.wait_ge(S["ex_in"], 1)
            a.activation(ex2, m2, ACT.Exp).then_inc(S["ex_ok"], 1)
            act.wait_ge(S["wsc_ok"], 1)
            for e in range(NE):
                a.activation(w1h[:, e, :], w_f32[:, e, :], ACT.Copy, scale=s1[:, e:e + 1]).then_inc(S["w1_hi"], 1)
            act.wait_ge(S["wsc_ok"], 2)
            for e in range(NE):
                a.activation(w2h[:, e, :], w_f32[:, e, :], ACT.Copy, scale=s2[:, e:e + 1]).then_inc(S["w2_hi"], 1)
            act.wait_ge(S["wsc_ok"], 3)
            act.wait_ge(S["idx_ok"], 1)

            def tile(i, u, e):
                j = FU * i + u
                r = u % 2
                act.wait_ge(S["ffn_h"], j + 1)
                need(act, S["hs_ok"], j - 1)
                for b in range(HK):
                    last = a.activation(h_g[r][:, b * 128:(b + 1) * 128], ps[:, 2 + r, b * 128:(b + 1) * 128], ACT.Gelu,
                                        bias=b1T[:, bass.ds(e * HK + b, 1)], scale=g1[:, bass.ds(e, 1)])
                last.then_inc(S["gelu_ok"], 1)
            def group(i):
                es = experts(i, act)
                for u in range(FU):
                    tile(i, u, es[LEAD + u])
            group(0)
            with act.Fori(1, FT // FU) as i:
                group(i)

        @block.vector
        def _(dve):
            v = nc.vector
            dve.wait_ge(S["dst_in"], 16)
            v.tensor_scalar(key_t[0:NP, :], dst_all.rearrange("p (j g) -> p j g", g=GRAN)[:, :, 0], 1.0 / WIN, 0.5 / WIN - 0.5,
                            ALU.mult, ALU.add)
            v.drain()
            v.tensor_scalar(key[0:NP, :], key_t[0:NP, :], ROUND, ROUND, ALU.add, ALU.subtract)
            v.drain()
            dve.wait_ge(S["iotas"], 1)
            for j in range(COARSE):
                last = v.tensor_scalar(above[:, j, :], iota_g[0:NP, :], key[0:NP, j:j + 1], None, ALU.is_gt)
            last.then_inc(S["above_ok"], 1)
            dve.wait_ge(S["iotas"], 2)
            v.tensor_scalar(ident, iota_row, iota_col, None, ALU.is_equal).then_inc(S["ident_ok"], 1)
            dve.wait_ge(S["w_in_in"], 48)
            v.tensor_tensor(w_sq, w_raw, w_raw, ALU.mult)
            v.tensor_tensor(b_sq, b_col, b_col, ALU.mult)
            v.drain()
            v.tensor_reduce(bound, w_sq, AX.X, ALU.add)
            v.drain()
            v.scalar_tensor_tensor(bound, bound, float(D), b_sq, ALU.mult, ALU.add)
            v.drain()
            v.tensor_reduce(bmax, bound, AX.X, ALU.max).then_inc(S["bound_ok"], 1)
            dve.wait_ge(S["count_ok"], 1)
            v.tensor_scalar(starts[0:NP, :], ps[0:NP, 7, 0:NR], -1.0, 0.0, ALU.add, ALU.max)
            v.drain()
            v.tensor_scalar(start_row[0:NP, :], starts[0:NP, :], float(ROWS - 1), None, ALU.min).then_inc(S["start_ok"], 1)
            dve.wait_ge(S["x_in"], 16)
            for t in range(T):
                v.bn_stats(stats[0:NP, t, :], x_all[:, t, :])
            v.drain()
            for t in range(T):
                v.bn_aggr(mv[0:NP, t, :], stats[0:NP, t, :])
            v.drain()
            v.tensor_scalar(ve[0:NP, :], mv[0:NP, :, 1], 1e-5, None, ALU.add).then_inc(S["stats_ok"], 1)
            dve.wait_ge(S["ball_ok"], 1)
            v.tensor_scalar(bmax, ball, 2.0, None, ALU.mult)
            v.drain()
            v.tensor_scalar(exp_i, bmax.bitcast(I32), 24, None, ALU.logical_shift_right)
            v.drain()
            v.tensor_scalar(exp_j[:, 0:1], exp_i, -1.0, 202.0, ALU.mult, ALU.add)
            v.tensor_scalar(exp_j[:, 1:2], exp_i, 52.0, None, ALU.add)
            v.drain()
            v.tensor_scalar(scale[:, :].bitcast(I32), exp_j, 23, None, ALU.logical_shift_left)
            dve.wait_ge(S["std_ok"], 1)
            newton(v, rstd[0:NP, :], ve[0:NP, :], rtmp[0:NP, :])
            for r in range(NR):
                dve.wait_ge(gathered[r], 16)
            gs, gd = g_edges[:, :, 0:SLOTS], g_edges[:, :, SLOTS:2 * SLOTS]
            v.tensor_copy(e_src, gs)
            v.tensor_scalar(e_d, gs, 1.0 / T, 0.5 / T - 0.5, ALU.mult, ALU.add)
            v.drain()
            v.tensor_scalar(e_b, e_d, ROUND, ROUND, ALU.add, ALU.subtract)
            v.drain()
            for r in range(NR):
                v.tensor_scalar(e_d[:, r, :], gd[:, r, :], float(T), win_base[0:NP, r:r + 1], ALU.mult, ALU.subtract)
            flat = "p r s -> p (r s)"
            v.scalar_tensor_tensor(e_q.rearrange(flat), e_b.rearrange(flat), -float(T), e_src.rearrange(flat), ALU.mult, ALU.add)
            v.drain()
            v.tensor_tensor(e_q, e_q, e_d, ALU.add).then_inc(S["keys_ok"], 1)
            for r in range(NR):
                for k in range(SL):
                    dve.wait_ge(S["keyT_ps"], r * SL + k + 1)
                    tb = ps[0:NP, 2 * (k % 2), 0:NP].rearrange("e (i j) -> e i j", j=WIN)
                    tq = ps[0:NP, 2 * (k % 2) + 1, 0:NP].rearrange("e (i j) -> e i j", j=WIN)
                    v.tensor_copy(key_b[:, r, :, k, :], tb)
                    v.tensor_scalar(key_q[:, r, :, k, :], tq, -1.0, float(Q), ALU.max, ALU.min).then_inc(S["keyT_ok"], 1)
            for r in range(NR):
                v.tensor_tensor(dl_eq, e_d[:, r:r + 1, :].broadcast_to([NP, WIN, SLOTS]),
                                dl25[0:NP, :, None].broadcast_to([NP, WIN, SLOTS]), ALU.is_equal)
                v.drain()
                v.tensor_reduce(deg[0:NP, r * WIN:(r + 1) * WIN], dl_eq, AX.X, ALU.add)
                v.drain()
            v.tensor_scalar(degc[0:NP, :], deg[0:NP, :], 1.0, None, ALU.max)
            v.drain()
            v.reciprocal(degc[0:NP, :], degc[0:NP, :])
            v.drain()
            for s in range(STEPS):
                v.tensor_scalar(cinv[0:NP, s, :], degc[0:NP, :], 1.0 / (STEPS - s), None, ALU.mult)
            v.tensor_reduce(in_windows[0:NP, :], deg[0:NP, :], AX.X, ALU.add).then_inc(S["cover_sum"], 1)
            def normalise(i, u):
                n = 5 * i + u
                v.tensor_scalar(x_n[u], x_all[:, bass.ds(n, 1), :].rearrange("p a f -> p (a f)"),
                                mv[0:NP, bass.ds(n, 1), 0], rstd[0:NP, bass.ds(n, 1)],
                                ALU.subtract, ALU.mult).then_inc(S["xn_ok"], 1)

            def split(i, u):
                n = 5 * i + u
                dve.wait_ge(S["h_act"], n + 1)
                need(dve, h_out[RB[u]], 16 * (i if u == 2 else 2 * i + u // 3))
                hi = va[:, bass.ds(n, 1), 0:D].rearrange("p a f -> p (a f)")
                lo = va[:, bass.ds(n, 1), D:2 * D].rearrange("p a f -> p (a f)")
                v.tensor_scalar(h_s[RB[u]][0:NP, :], h_f[RB[u]][0:NP, :], scale[0:NP, 0:1], None, ALU.mult)
                v.tensor_scalar(hi, h_f[RB[u]][0:NP, :], scale[0:NP, 0:1], None, ALU.mult)
                v.drain()
                v.tensor_tensor(lo, h_s[RB[u]][0:NP, :], hi, ALU.subtract).then_inc(S["v_ready"], 1)

            for u in range(WIN):
                normalise(0, u)
            for u in range(WIN):
                split(0, u)
                normalise(1, u)
            with dve.Fori(1, NB - 1) as i:
                for u in range(WIN):
                    split(i, u)
                    normalise(i + 1, u)
            for u in range(WIN):
                split(NB - 1, u)
            kb = key_b.rearrange("e r i k j -> e (r i) (k j)")
            kq = key_q.rearrange("e r i k j -> e (r i) (k j)")
            dve.wait_ge(S["iotas"], 3)
            v.drain()
            with dve.Fori(0, NR * NB) as i:
                for u in range(WIN):
                    bt = 5 * i + u
                    dve.wait_ge(S["win_ps"], bt + 1)
                    v.tensor_tensor(oh_b[RB[u]], iota_x, kb[:, bass.ds(bt, 1), :].broadcast_to([NP, NP, C]), ALU.is_equal)
                    v.tensor_tensor(oh_q[RB[u]], iota_x, kq[:, bass.ds(bt, 1), :].broadcast_to([NP, NP, C]),
                                    ALU.is_equal).then_inc(S["oh_ready"], 1)

            def step(n0, s, dest):
                with dve.Fori(0, NB) as i:
                    for u in range(WIN):
                        t = 5 * i + u
                        n = n0 + t
                        dve.wait_ge(S["hi_ok"], n + 1)
                        v.scalar_tensor_tensor(v_f[0:NP, :], ps[0:NP, u, D:2 * D], cinv[0:NP, s, bass.ds(t, 1)], t_hi[0:NP, :],
                                               ALU.mult, ALU.add).then_inc(S["psum_read"], 1)
                        v.drain()
                        if u % 2 == 0:
                            dve.wait_ge(h_in[0], 16 * (3 * (s * NB + i) + u // 2 + 1))
                        else:
                            dve.wait_ge(h_in[1], 16 * (2 * (s * NB + i) + u // 2 + 1))
                        hi = dest[:, bass.ds(t, 1), 0:D].rearrange("p a f -> p (a f)")
                        lo = dest[:, bass.ds(t, 1), D:2 * D].rearrange("p a f -> p (a f)")
                        v.tensor_tensor(v_f[0:NP, :], v_f[0:NP, :], h_ring[0:NP, u % 2, :], ALU.add).then_inc(S["h_used"], 1)
                        v.drain()
                        v.tensor_copy(hi, v_f[0:NP, :])
                        v.drain()
                        v.tensor_tensor(lo, v_f[0:NP, :], hi, ALU.subtract).then_inc(S["v_ready"], 1)
                        v.drain()
            dve.sem_inc(S["psum_read"], 5)
            dve.sem_inc(S["h_used"], 2)
            dve.wait_ge(S["cover_ps"], 1)
            v.tensor_scalar(covered[:, :], ps[0:1, 7, 0:1], float(E), None, ALU.is_equal)
            v.drain().then_inc(S["cover_ok"], 1)
            for s in range(STEPS - 1):
                step(s * T, s, vb if s % 2 == 0 else va)
            fast = dve.value_load(covered[:, :], min_val=0, max_val=1)
            with dve.If(fast == 0):
                dve.wait_ge(S["e_const"], 1)
                dve.wait_ge(S["e_in"], 48)
                v.tensor_copy(dst_e, dst_i)
                v.drain()
                with dve.Fori(0, STEPS) as s:
                    for part, (t0, count) in enumerate(PARTS):
                        with dve.Fori(0, EC // EU) as i:
                            for u in range(EU):
                                dve.wait_ge(S["e_mm"], s * (2 * EC) + i * EU + (part * EC + u + 1))
                                v.tensor_scalar(oh_e[u][:, 0:count, :], node[:, t0:t0 + count, :], dst_e[:, bass.ds(i * EU + u, 1)], None,
                                                ALU.is_equal).then_inc(S["e_oh"], 1)
                        dve.wait_ge(S["e_acc"], 2 * s + (part + 1))
                        dve.wait_ge(S["e_rows"], s * 16 + 16)
                        v.tensor_scalar(deg_e[:, t0:t0 + count], ps[0:NP, 7, 0:count], 1.0, None, ALU.max)
                        v.drain()
                        v.reciprocal(deg_e[:, t0:t0 + count], deg_e[:, t0:t0 + count])
                        v.drain()
                        v.tensor_scalar(deg_e[:, t0:t0 + count], deg_e[:, t0:t0 + count], k_inv[:, bass.ds(s, 1)], None, ALU.mult)
                        v.drain()
                        for t in range(count):
                            v.scalar_tensor_tensor(term_e[:, t0 + t, :], ps[0:NP, t // 2, t % 2 * D:(t % 2 + 1) * D],
                                                   deg_e[:, t0 + t:t0 + t + 1], h_e[:, t0 + t, :], ALU.mult, ALU.add)
                        v.drain().then_inc(S["e_read"], 1)
                    dve.sem_inc(S["e_term"], 1)
                dve.wait_ge(S["e_rows"], 16 * (STEPS + 2))
                v.memset(adj[:, :], 0.0)
                v.memset(v_b[:, :], 0.0)
                v.memset(cinv[:, STEPS - 1, :], 0.0)
                v.drain()
            v.drain().then_inc(S["term_ok"], 1)
            def pow2(scale_out, inv_out, square, pi, pj):
                v.tensor_scalar(pi, square.bitcast(I32), 24, None, ALU.logical_shift_right)
                v.drain()
                v.tensor_scalar(pj, pi, -1.0, 203.0, ALU.mult, ALU.add)
                v.tensor_scalar(pi, pi, 51.0, None, ALU.add)
                v.drain()
                v.tensor_scalar(scale_out.bitcast(I32), pj, 23, None, ALU.logical_shift_left)
                v.tensor_scalar(inv_out.bitcast(I32), pi, 23, None, ALU.logical_shift_left)
                v.drain()

            dve.wait_ge(S["f_const"], 96)
            v.tensor_reduce(gb_max[:, 0:1], ga_bc, AX.X, ALU.max, apply_absolute_value=True)
            v.tensor_reduce(gb_max[:, 1:2], be_bc, AX.X, ALU.max, apply_absolute_value=True)
            v.drain()
            v.tensor_tensor(gb_sq, gb_max, gb_max, ALU.mult)
            v.drain()
            v.tensor_scalar(xn_sq[:, 0:1], gb_sq[:, 0:1], float(D), gb_sq[:, 1:2], ALU.mult, ALU.add)
            v.tensor_tensor(xn_sq[:, 1:2], gb_sq[:, 0:1], gb_sq[:, 1:2], ALU.add)
            v.drain()
            v.tensor_scalar(xn_sq[:, 0:1], xn_sq[:, 0:1], 2.0, None, ALU.mult)
            v.tensor_scalar(xn_sq[:, 1:2], xn_sq[:, 1:2], 2.0 * D, None, ALU.mult)
            v.drain()
            pow2(xs_scale[:, 0:1], xs_scale[:, 1:2], xn_sq[:, 0:1], pow_i[:, 0:1], pow_j[:, 0:1])

            def root(k, i):
                v.drain().then_inc(S["ve_ok"], 1)
                dve.wait_ge(S["sd_ok"], 2 * i + k - 1)
                newton(v, sd2, ve2, rt2)

            def body(i, u, has):
                m = 5 * i + u
                n = LAST + m
                if u == 2 and has(7):
                    gv = mv2[:, bass.ds(5 * (i - 1), WIN), 1]
                    v.tensor_scalar(ve2, gv, 1e-5, None, ALU.add)
                    root(0, i)
                    v.tensor_copy(r1, sd2)
                    v.tensor_tensor(ve2, sd2, sd2, ALU.mult)
                    v.drain()
                    v.tensor_tensor(ve2, ve2, gv, ALU.mult)
                    v.drain()
                    v.tensor_scalar(ve2, ve2, 1e-5, None, ALU.add)
                    root(1, i)
                    v.tensor_tensor(rr[:, bass.ds(5 * (i - 1), WIN)], r1, sd2, ALU.mult)
                    v.drain()
                if has(7):
                    w = m - 7
                    v.drain()
                    need(dve, S["xnT_ps"], w - 1)
                    need(dve, S["xhi_ok"], w - 1)
                    v.tensor_scalar(xn2[ring(7, u)], x1[:, bass.ds(w, 1), :].rearrange("p a f -> p (a f)"),
                                    mv2[:, bass.ds(w, 1), 0], rr[:, bass.ds(w, 1)], ALU.subtract, ALU.mult)
                    v.drain()
                    v.tensor_tensor(xn2[ring(7, u)], xn2[ring(7, u)], ga_bc[0:NP, :], ALU.mult).then_inc(S["z_ok"], 1)
                if has(0):
                    dve.wait_ge(S["hi_ok"], n + 1)
                    v.scalar_tensor_tensor(v_f[0:NP, :], ps[0:NP, RB[u], D:2 * D], cinv[0:NP, STEPS - 1, bass.ds(m, 1)], t_hi[0:NP, :],
                                           ALU.mult, ALU.add).then_inc(S["psum_read"], 1)
                    v.drain()
                    if u % 2 == 0:
                        dve.wait_ge(h_in[0], 16 * (3 * ((STEPS - 1) * NB + i) + u // 2 + 1))
                    else:
                        dve.wait_ge(h_in[1], 16 * (2 * ((STEPS - 1) * NB + i) + u // 2 + 1))
                    need(dve, S["vT_ps"], m - 1)
                    v.tensor_tensor(vfin[RB[u]], v_f[0:NP, :], h_ring[0:NP, u % 2, :], ALU.add).then_inc(S["h_used"], 1)
                    v.drain().then_inc(S["vfin_ok"], 1)
                if has(2):
                    xt = x1[:, bass.ds(m - 2, 1), :].rearrange("p a f -> p (a f)")
                    dve.wait_ge(S["y_ps"], m - 1)
                    dve.wait_ge(S["xb_ok"], m - 1)
                    v.scalar_tensor_tensor(xt, ps[0:NP, 5, 0:D], scale[0:NP, 1:2], x_i[ring(2, u)], ALU.mult, ALU.add).then_inc(S["x1_ok"], 1)
                    v.drain()
                    v.bn_stats(stats2, xt)
                    v.drain()
                    v.bn_aggr(mv_t, stats2)
                    v.drain()
                    v.tensor_copy(mv2[:, bass.ds(m - 2, 1), :].rearrange("p a f -> p (a f)"), mv_t)
                    v.drain()
                if has(8):
                    w = m - 8
                    dve.wait_ge(S["lg_ps"], w + 1)
                    v.tensor_tensor(lg[:, bass.ds(w, 1), :].rearrange("p a e -> p (a e)"), ps[0:NP, 6, 0:NE], br_bc[0:NP, :],
                                    ALU.add).then_inc(S["lg_ok"], 1)
                    dve.wait_ge(S["xhi_ok"], w + 1)
                    xs = xs_r[ring(8, u)]
                    v.scalar_tensor_tensor(xs[:, D:2 * D], xn2[ring(8, u)], xs_scale[0:NP, 0:1], xs[:, 0:D],
                                           ALU.mult, ALU.subtract).then_inc(S["xs_ok"], 1)
            last_step(dve, body)
            v.drain()
            bte = [NP, T, NE]
            e8 = iota_e8[:, None, :].broadcast_to(bte)
            v.tensor_reduce(m1, lg, AX.X, ALU.max)
            v.drain()

            def one_hot(out_, logits, m):
                v.tensor_tensor(tmp1, logits, m[:, :, None].broadcast_to(bte), ALU.is_equal)
                v.drain()
                v.tensor_tensor(tmp1, tmp1, e8, ALU.mult)
                v.drain()
                v.tensor_reduce(n1, tmp1, AX.X, ALU.min)
                v.drain()
                v.tensor_tensor(out_, e8, n1[:, :, None].broadcast_to(bte), ALU.is_equal)
                v.drain()
            one_hot(oh1, lg, m1)
            v.scalar_tensor_tensor(tmp2, oh1, -3e38, lg, ALU.mult, ALU.add)
            v.drain()
            v.tensor_reduce(m2, tmp2, AX.X, ALU.max)
            v.drain()
            one_hot(oh2, tmp2, m2)
            v.tensor_tensor(m2, m2, m1, ALU.subtract)
            v.drain().then_inc(S["ex_in"], 1)
            v.tensor_tensor(both, oh1, oh2, ALU.add)
            v.drain()
            v.tensor_reduce(per_p, both.rearrange("p t e -> p e t"), AX.X, ALU.add).then_inc(S["cnt_in"], 1)
            src_, d = both, 1
            bufs = [sum_a, sum_b]
            while d < T:
                dst_ = bufs[0]
                v.tensor_tensor(dst_[:, d:T, :], src_[:, d:T, :], src_[:, 0:T - d, :], ALU.add)
                v.tensor_copy(dst_[:, 0:d, :], src_[:, 0:d, :])
                v.drain()
                src_, d = dst_, 2 * d
                bufs = bufs[::-1]
            v.tensor_tensor(pos, src_, both, ALU.subtract)
            dve.wait_ge(S["ex_ok"], 1)
            v.tensor_scalar(den, ex2, 1.0, None, ALU.add)
            v.drain()
            v.reciprocal(w_top1, den)
            v.drain()
            v.tensor_tensor(w_top2, ex2, w_top1, ALU.mult)
            dve.wait_ge(S["cnt_ok"], 1)
            v.tensor_scalar(totals, ps[:, 7, 8:8 + NE], 127.0, 1.0 / 128, ALU.add, ALU.mult)
            v.drain()
            v.tensor_scalar(totals, totals, 1.0 / 256 - 0.5, None, ALU.add)
            v.drain()
            v.tensor_scalar(tiles_a, totals, ROUND, ROUND, ALU.add, ALU.subtract)
            v.drain()
            src_, d = tiles_a, 1
            bufs = [tiles_b, tiles_c]
            while d < NE:
                dst_ = bufs[0]
                v.tensor_tensor(dst_[:, d:NE], src_[:, d:NE], src_[:, 0:NE - d], ALU.add)
                v.tensor_copy(dst_[:, 0:d], src_[:, 0:d])
                v.drain()
                src_, d = dst_, 2 * d
                bufs = bufs[::-1]
            ends = src_
            v.tensor_tensor(totals, ends, tiles_a, ALU.subtract)
            v.drain()
            v.scalar_tensor_tensor(slot_base, totals[0:NP, :], 128.0, ps[0:NP, 7, 0:NE], ALU.mult, ALU.add)
            v.drain()
            v.tensor_tensor(pos, pos, slot_base[:, None, :].broadcast_to(bte), ALU.add)
            v.drain()
            for k, (oh, slot) in enumerate(((oh1, slot1), (oh2, slot2))):
                v.tensor_tensor(tmp1, oh, pos, ALU.mult)
                v.drain()
                v.tensor_reduce(s_all[:, k * T:(k + 1) * T], tmp1, AX.X, ALU.add)
                v.drain()
            v.tensor_scalar(s_tile, s_all, 1.0 / 128, 1.0 / 256 - 0.5, ALU.mult, ALU.add)
            v.drain()
            v.tensor_scalar(s_tile, s_tile, ROUND, ROUND, ALU.add, ALU.subtract)
            v.drain()
            v.scalar_tensor_tensor(s_pin, s_tile, -128.0, s_all, ALU.mult, ALU.add)
            v.tensor_tensor(le_tiles, tile_row[:, :, None].broadcast_to([128, FT, NE]),
                            ends[:, None, :].broadcast_to([128, FT, NE]), ALU.is_ge)
            v.drain()
            v.tensor_reduce(empty, le_tiles, AX.X, ALU.add)
            v.drain()
            v.memset(exp_of[:, 0:LEAD], 0)
            v.tensor_scalar(exp_of[:, LEAD:], empty, float(NE - 1), None, ALU.min)
            for c in range(T * TOP):
                v.tensor_scalar(oh_pos[:, c, :], iota_pos, s_pin[:, c:c + 1], None, ALU.is_equal)
                v.tensor_scalar(planes[:, c, 0:FT], iota_tile, s_tile[:, c:c + 1], p_plus1[0:NP, :], ALU.is_equal, ALU.mult)
                v.tensor_scalar(planes[:, c, FT:PL], iota_tile, s_tile[:, c:c + 1], float(c), ALU.is_equal, ALU.mult)
            v.drain().then_inc(S["rt_done"], 1)
            dve.wait_ge(w1_in, 16 * DK)
            v.tensor_reduce(w_max[:, 0:NE * DK].rearrange("p (e b) -> p e b", e=NE),
                            w_f32.rearrange("p e (b h) -> p e b h", b=DK), AX.X, ALU.max, apply_absolute_value=True)
            v.drain()
            v.tensor_tensor(w_sq2[:, 0:NE * DK], w_max[:, 0:NE * DK], w_max[:, 0:NE * DK], ALU.mult)
            dve.wait_ge(S["b1T_ok"], 1)
            v.tensor_tensor(w_sq2[:, NE * DK:NE * (DK + HK)], b1T, b1T, ALU.mult)
            v.drain().then_inc(S["w_sq_ok"], 1)
            dve.wait_ge(S["w_sum_ps"], 1)
            v.tensor_reduce(w_sums[:, 0, :], ps[:, 5, 0:NE * DK].rearrange("p (e b) -> p e b", e=NE), AX.X, ALU.add)
            v.tensor_reduce(w_sums[:, 2, :], ps[:, 5, NE * DK:NE * (DK + HK)].rearrange("p (e b) -> p e b", e=NE), AX.X, ALU.add)
            v.drain()
            pow2(s1, i1, w_sums[:, 0, :], pow_i, pow_j)
            v.tensor_scalar(g1, i1, xs_scale[:, 1:2], None, ALU.mult).then_inc(S["wsc_ok"], 1)
            v.scalar_tensor_tensor(w_sums[:, 2, :], w_sums[:, 0, :], xn_sq[:, 1:2], w_sums[:, 2, :], ALU.mult, ALU.add)
            v.drain()
            v.tensor_scalar(w_sums[:, 2, :], w_sums[:, 2, :], 2.0, None, ALU.mult)
            v.drain()
            pow2(sh, ih, w_sums[:, 2, :], pow_i, pow_j)
            for e in range(NE):
                dve.wait_ge(S["w1_hi"], e + 1)
                v.scalar_tensor_tensor(w1l[:, e, :], w_f32[:, e, :], s1[:, e:e + 1], w1h[:, e, :], ALU.mult, ALU.subtract).then_inc(S["w1_lo"], 1)
            for e in range(NE):
                dve.wait_ge(w2_in[e], 16)
                v.tensor_reduce(w_max[:, NE * DK + e * HK:NE * DK + (e + 1) * HK],
                                w_f32[:, e, :].rearrange("p (b d) -> p b d", b=HK), AX.X, ALU.max, apply_absolute_value=True)
            v.drain()
            v.tensor_tensor(w_sq2[:, 0:NE * HK], w_max[:, NE * DK:], w_max[:, NE * DK:], ALU.mult)
            v.drain().then_inc(S["w_sq_ok"], 1)
            dve.wait_ge(S["w_sum_ps"], 2)
            v.tensor_reduce(w_sums[:, 1, :], ps[:, 5, 0:NE * HK].rearrange("p (e b) -> p e b", e=NE), AX.X, ALU.add)
            v.drain()
            pow2(s2, i2, w_sums[:, 1, :], pow_i, pow_j)
            v.tensor_tensor(g2, ih, i2, ALU.mult).then_inc(S["wsc_ok"], 1)
            for e in range(NE):
                dve.wait_ge(S["w2_hi"], e + 1)
                v.scalar_tensor_tensor(w2l[:, e, :], w_f32[:, e, :], s2[:, e:e + 1], w2h[:, e, :], ALU.mult, ALU.subtract).then_inc(S["w2_lo"], 1)
            dve.wait_ge(S["tok_ps"], 1)
            v.tensor_scalar(tok_p, ps[:, 0, 0:FT], -1.0, float(T), ALU.add, ALU.mult)
            v.tensor_scalar(empty, ps[:, 0, 0:FT], 0.0, 4.0 * TOP * N, ALU.is_equal, ALU.mult)
            v.tensor_copy(tok_b, ps[:, 0, FT:PL])
            v.drain()
            v.tensor_tensor(tok_p, tok_p, tok_b, ALU.add)
            v.tensor_scalar(tok_b, tok_b, float(T), None, ALU.is_ge)
            v.drain()
            v.scalar_tensor_tensor(tok_p, tok_b, -float(T), tok_p, ALU.mult, ALU.add)
            v.drain()
            v.scalar_tensor_tensor(dest, tok_b, float(N), tok_p, ALU.mult, ALU.add)
            v.tensor_scalar(idx_g, tok_p, 0.0, None, ALU.max)
            v.drain()
            v.tensor_tensor(dest, dest, empty, ALU.add)
            v.drain()
            v.tensor_copy(idx_s, dest)
            v.drain().then_inc(S["idx_ok"], 1)
            dve.sem_inc(S["wsc_ok"], 1)

            def transposed(i, u):
                j = FU * i + u
                r = u % 2
                dve.wait_ge(S["xg_T"], j + 1)
                need(dve, S["ffn_h"], j - 1)
                v.tensor_copy(xT16[r], ps[:, r, :].bitcast(F16)[:, 0:2 * D].rearrange("k (b s) -> k b s", b=2 * DK)).then_inc(S["xgT_ok"], 1)

            def hidden(i, u, e):
                j = FU * i + u
                r = u % 2
                dve.wait_ge(S["gelu_ok"], j + 1)
                need(dve, S["ffn_y"], j - FR + 1)
                hh, hl = h_hi[u % FR].rearrange("h b s -> h (b s)"), h_lo[u % FR].rearrange("h b s -> h (b s)")
                v.tensor_scalar(hh, h_g[r], sh[:, bass.ds(e, 1)], None, ALU.mult)
                v.drain()
                v.scalar_tensor_tensor(hl, h_g[r], sh[:, bass.ds(e, 1)], hh, ALU.mult, ALU.subtract).then_inc(S["hs_ok"], 1)

            def result(i, u, e):
                j = FU * i + u
                r = u % 2
                dve.wait_ge(S["ffn_y"], j + 1)
                need(dve, y_out[u % FR], 16 * (FU // FR * i + u // FR))
                v.scalar_tensor_tensor(y_sb[u % FR], ps[:, 4 + r, 0:D], g2[:, bass.ds(e, 1)], b2_bc[:, bass.ds(e, 1), :].rearrange("p a f -> p (a f)"),
                                       ALU.mult, ALU.add).then_inc(S["y_ok"], 1)
            ffn_tiles(dve, FT, FU, LEAD, experts, transposed, hidden, result)
            for i in range(NB):
                dve.wait_ge(yc_in[i % 2], 32 * (i // 2 + 1))
                for k, wk in enumerate((w_top1, w_top2)):
                    v.drain()
                    for t in range(WIN):
                        n = i * WIN + t
                        last = v.scalar_tensor_tensor(x1[:, n, :], y_in[i % 2][k][:, t, :], wk[:, n:n + 1], x1[:, n, :], ALU.mult, ALU.add)
                v.drain().then_inc(S["comb_ok"], 1)

        @block.tensor
        def _(pe):
            te = nc.tensor
            pe.wait_ge(S["ident_ok"], 1)
            pe.wait_ge(S["w_in_in"], 48)
            for kb in range(DK):
                for ob in range(DK):
                    last = te.transpose(ps[:, 6, (kb * DK + ob) * 128:(kb * DK + ob + 1) * 128],
                                        w_raw[:, ob, kb * 128:(kb + 1) * 128], ident)
            last.then_inc(S["wT_ps"], 1)
            pe.wait_ge(S["above_ok"], 1)
            for r in range(NR):
                for j in range(COARSE):
                    last = te.matmul(ps[0:NP, 7, r:r + 1], above[:, j, :].rearrange("p (g r) -> p g r", r=NR)[:, :, r],
                                     ones16[0:NP, 0:1], start=(j == 0), stop=(j == COARSE - 1))
            last.then_inc(S["count_ok"], 1)
            pe.wait_ge(S["keys_ok"], 1)
            for r in range(NR):
                for k in range(SL):
                    n = r * SL + k
                    if n >= 2:
                        pe.wait_ge(S["keyT_ok"], n - 1)
                    te.transpose(ps[0:NP, 2 * (k % 2), 0:NP], e_b[:, r, k * NP:(k + 1) * NP], ident[0:NP, 0:NP])
                    te.transpose(ps[0:NP, 2 * (k % 2) + 1, 0:NP], e_q[:, r, k * NP:(k + 1) * NP],
                                 ident[0:NP, 0:NP]).then_inc(S["keyT_ps"], 1)
            pe.wait_ge(S["keyT_ok"], NR * SL)
            pe.wait_ge(S["wT_ok"], 1)

            def features(i):
                for u in range(WIN):
                    n = WIN * i + u
                    pe.wait_ge(S["xn_ok"], n + 1)
                    for b in range(DK):
                        last = te.transpose(ps[:, RB[u], b * 128:b * 128 + NP],
                                            x_n[u][:, b * 128:(b + 1) * 128],
                                            ident[0:NP, 0:NP])
                    last.then_inc(S["xT_ps"], 1)
                    pe.wait_ge(S["xT_ok"], n + 1)
                    need(pe, S["h_act"], n if u == 0 else n - 1)
                    te.matmul(ps[0:NP, 3 + RB[u], 0:D], ones32[0:1, 0:NP], b_row[0:1, :], start=True, stop=False)
                    for b in range(DK):
                        last = te.matmul(ps[0:NP, 3 + RB[u], 0:D], xT[RB[u]][:, b, :], w_inT[:, b, :],
                                         start=False, stop=(b == DK - 1))
                    last.then_inc(S["h_ps"], 1)
            features(0)
            with pe.Fori(1, NB) as i:
                features(i)
            pe.wait_ge(S["h_act"], T)
            pe.wait_ge(S["cover_sum"], 1)
            te.matmul(ps[0:1, 7, 0:1], in_windows[0:NP, :], ones32[0:NP, 0:1], start=True, stop=True).then_inc(S["cover_ps"], 1)
            pe.sem_inc(S["win_ps"], 2)

            def windows(i):
                for u in range(WIN):
                    bt = WIN * i + u
                    pe.wait_ge(S["oh_ready"], bt + 1)
                    need(pe, S["win_out"], bt if u == 0 else bt - 1)
                    for j in range(WIN):
                        cell = ps[0:NP, 2 * RB[u] + j // 4, (j % 4) * 128:(j % 4) * 128 + Q]
                        for k in range(SL):
                            last = te.matmul(cell, oh_b[RB[u]][:, :, k * WIN + j], oh_q[RB[u]][:, :, k * WIN + j],
                                             start=(k == 0), stop=(k == SL - 1))
                    last.then_inc(S["win_ps"], 1)
            windows(0)
            with pe.Fori(1, NR * NB) as i:
                windows(i)
            pe.wait_ge(S["win_out"], NP)

            def step(n0, s, source):
                with pe.Fori(0, NB) as i:
                    for u in range(WIN):
                        t = 5 * i + u
                        n = n0 + t
                        pe.wait_ge(S["psum_read"], n + 1)
                        pe.wait_ge(S["v_ready"], T * (s + 1) - 1)
                        for a in range(T):
                            if a == T - 1:
                                pe.wait_ge(S["v_ready"], T * (s + 1))
                            last = te.matmul(ps[0:NP, u, :], adj_t[:, bass.ds(t, 1), a, :].rearrange("b t p -> b (t p)"),
                                             source[:, a, :], start=(a == 0), stop=(a == T - 1))
                        last.then_inc(S["tile_ps"], 1)
            for s in range(STEPS - 1):
                step(s * T, s, va if s % 2 == 0 else vb)
            pe.wait_ge(S["cover_ok"], 1)
            fast = pe.value_load(covered[:, :], min_val=0, max_val=1)
            with pe.If(fast == 0):
                pe.wait_ge(S["psum_read"], LAST + 5)
                pe.wait_ge(S["e_const"], 1)
                pe.sem_inc(S["e_mm"], EU)
                pe.sem_inc(S["e_read"], 1)
                with pe.Fori(0, STEPS) as s:
                    for part, (t0, count) in enumerate(PARTS):
                        banks = [(b, min(512, count * D - b * 512)) for b in range((count + 1) // 2)] + [(7, count)]
                        pe.wait_ge(S["e_read"], 2 * s + (part + 1))
                        for b, n in banks:
                            te.matmul(ps[0:NP, b, 0:n], zeros_e[:, 0:NP], zeros_e[:, 0:n], start=True, stop=False)
                        with pe.Fori(0, EC // EU) as i:
                            for u in range(EU):
                                pe.wait_ge(S["e_oh"], s * (2 * EC) + i * EU + (part * EC + u + 1))
                                pe.wait_ge(e_gathered[u], s * (32 * EC // EU) + i * 16 + (part * 16 * EC // EU + 16))
                                for t in range(count):
                                    te.matmul(ps[0:NP, t // 2, t % 2 * D:(t % 2 + 1) * D], oh_e[u][:, t, :], rows_e[u], start=False, stop=False)
                                    last = te.matmul(ps[0:NP, 7, t:t + 1], oh_e[u][:, t, :], ones_e, start=False, stop=False)
                                last.then_inc(S["e_mm"], 1)
                        for b, n in banks:
                            last = te.matmul(ps[0:NP, b, 0:n], zeros_e[:, 0:NP], zeros_e[:, 0:n], start=False, stop=True)
                        last.then_inc(S["e_acc"], 1)
            pe.wait_ge(S["term_ok"], 1)
            pe.wait_ge(S["f_const"], 96)
            pe.wait_ge(S["pool_const"], 1)
            pe.wait_ge(S["psum_read"], LAST + 5)
            for kb in range(DK):
                for ob in range(DK):
                    last = te.transpose(ps[:, 7, (kb * DK + ob) * 128:(kb * DK + ob + 1) * 128],
                                        w_oraw[:, ob, kb * 128:(kb + 1) * 128], ident2)
            last.then_inc(S["w_oT_ps"], 1)
            pe.wait_ge(S["v_ready"], T * STEPS)

            def body(i, u, has):
                m = 5 * i + u
                n = LAST + m
                if has(0):
                    pe.wait_ge(S["psum_read"], n + 4)
                    for a in range(T):
                        last = te.matmul(ps[0:NP, RB[u], :], adj_t[:, bass.ds(m, 1), a, :].rearrange("b t p -> b (t p)"),
                                         vb[:, a, :], start=(a == 0), stop=(a == T - 1))
                    last.then_inc(S["tile_ps"], 1)
                if has(7):
                    pe.wait_ge(S["xn2_ok"], m - 6)
                    need(pe, S["xnT_ok"], m - 7)
                    for b in range(DK):
                        last = te.transpose(ps[:, 4, b * 128:b * 128 + NP], xn2[ring(7, u)][:, b * 128:(b + 1) * 128], ident2[0:NP, 0:NP])
                    last.then_inc(S["xnT_ps"], 1)
                if has(8):
                    pe.wait_ge(S["xnT_ok"], m - 7)
                    need(pe, S["lg_ok"], m - 8)
                    for b in range(DK):
                        last = te.matmul(ps[0:NP, 6, 0:NE], xnT[:, b, :], wr_sb[:, b, :], start=(b == 0), stop=(b == DK - 1))
                    last.then_inc(S["lg_ps"], 1)
                if has(2):
                    pe.wait_ge(S["vT_ok"], m - 1)
                    if isinstance(i, int) and m == 2:
                        pe.wait_ge(S["w_oT_ok"], 1)
                    need(pe, S["x1_ok"], m - 2)
                    for b in range(DK):
                        last = te.matmul(ps[0:NP, 5, 0:D], vT[:, b, :], w_outT[:, b, :], start=(b == 0), stop=(b == DK - 1))
                    last.then_inc(S["y_ps"], 1)
                if has(1):
                    pe.wait_ge(S["vfin_ok"], m)
                    need(pe, S["vT_ok"], m - 1)
                    for b in range(DK):
                        last = te.transpose(ps[:, 3, b * 128:b * 128 + NP], vfin[ring(1, u)][:, b * 128:(b + 1) * 128], ident2[0:NP, 0:NP])
                    last.then_inc(S["vT_ps"], 1)
            last_step(pe, body)
            pe.wait_ge(S["b1_in"], 32)
            pe.wait_ge(S["x1_ok"], T)
            te.transpose(ps[:, 5, 0:NE * HK], b1_rows, ident2[0:NE * HK, 0:NE * HK]).then_inc(S["b1T_ps"], 1)
            pe.wait_ge(S["cnt_in"], 1)
            te.matmul(ps[0:NP, 7, 0:NE], tri, per_p, start=True, stop=True)
            te.matmul(ps[:, 7, 8:8 + NE], ones2[0:NP, :], per_p, start=True, stop=True).then_inc(S["cnt_ok"], 1)
            pe.wait_ge(S["rt_done"], 1)
            for c in range(T * TOP):
                last = te.matmul(ps[:, 0, 0:PL], oh_pos[:, c, :], planes[:, c, :], start=(c == 0), stop=(c == T * TOP - 1))
            last.then_inc(S["tok_ps"], 1)
            pe.wait_ge(S["w_sq_ok"], 1)
            te.matmul(ps[:, 5, 0:NE * (DK + HK)], ones2, w_sq2[:, 0:NE * (DK + HK)], start=True, stop=True).then_inc(S["w_sum_ps"], 1)
            pe.wait_ge(S["w_sq_ok"], 2)
            te.matmul(ps[:, 5, 0:NE * HK], ones2, w_sq2[:, 0:NE * HK], start=True, stop=True).then_inc(S["w_sum_ps"], 1)
            pe.wait_ge(S["idx_ok"], 1)
            pe.wait_ge(S["w2_lo"], NE)

            def transposed(i, u):
                j = FU * i + u
                r = u % 2
                pe.wait_ge(g_in[u], 16 * (i + 1))
                need(pe, S["xgT_ok"], j - 1)
                for b in range(2 * DK):
                    last = te.transpose(ps[:, r, :].bitcast(F16)[:, b * 128:(b + 1) * 128], x_g[u][:, b * 128:(b + 1) * 128], ident16)
                last.then_inc(S["xg_T"], 1)

            def hidden(i, u, e):
                j = FU * i + u
                r = u % 2
                pe.wait_ge(S["xgT_ok"], j + 1)
                need(pe, S["gelu_ok"], j - 1)
                for b in range(HK):
                    for n, (w, part) in enumerate(((w1h, 0), (w1h, 1), (w1l, 0))):
                        for k in range(DK):
                            at = k * H + b * 128
                            last = te.matmul(ps[:, 2 + r, b * 128:(b + 1) * 128],
                                             w[:, bass.ds(e, 1), at:at + 128].rearrange("k a h -> k (a h)"),
                                             xT16[r][:, part * DK + k, :], start=(n == 0 and k == 0), stop=(n == 2 and k == DK - 1))
                last.then_inc(S["ffn_h"], 1)

            def result(i, u, e):
                j = FU * i + u
                r = u % 2
                pe.wait_ge(S["hs_ok"], j + 1)
                need(pe, S["y_ok"], j - 1)
                for b in range(HK):
                    for n, (hp, w) in enumerate(((h_hi, w2h), (h_hi, w2l), (h_lo, w2h))):
                        last = te.matmul(ps[:, 4 + r, 0:D], hp[u % FR][:, b, :],
                                         w[:, bass.ds(e, 1), b * D:(b + 1) * D].rearrange("h a d -> h (a d)"),
                                         start=(b == 0 and n == 0), stop=(b == HK - 1 and n == 2))
                last.then_inc(S["ffn_y"], 1)
            ffn_tiles(pe, FT, FU, LEAD, experts, transposed, hidden, result)


def ffn_tiles(eng, count, unroll, lead, experts, transposed, hidden, result):
    groups = count // unroll

    def group(i, first, last):
        es = experts(i, eng)
        for u in range(unroll):
            if not (last and u == unroll - 1):
                transposed(i + (u + 1) // unroll, (u + 1) % unroll)
            hidden(i, u, es[lead + u])
            if not (first and u < 2):
                result(i + (u - 2) // unroll, (u - 2) % unroll, es[lead + u - 2])
        if last:
            for u in (unroll - 2, unroll - 1):
                result(i, u, es[lead + u])

    transposed(0, 0)
    group(0, True, False)
    with eng.Fori(1, groups - 1) as i:
        group(i, False, False)
    group(groups - 1, False, True)


def newton(v, r, var, tmp):
    v.reciprocal(r, r)
    v.drain()
    v.tensor_tensor(tmp, r, r, ALU.mult)
    v.drain()
    v.tensor_tensor(tmp, tmp, var, ALU.mult)
    v.drain()
    v.tensor_scalar(tmp, tmp, -0.5, 1.5, ALU.mult, ALU.add)
    v.drain()
    v.tensor_tensor(r, r, tmp, ALU.mult)
    v.drain()


_INS = ["x", "src", "dst", "L0_gnn_W_in", "L0_gnn_b_in", "L0_gnn_W_out", "L0_gnn_b_out", "L0_ffn_gamma", "L0_ffn_beta",
        "L0_ffn_Wr", "L0_ffn_br", "L0_ffn_W1", "L0_ffn_b1", "L0_ffn_W2", "L0_ffn_b2"]


def kernel(**inputs):
    import numpy as np
    import concourse.bacc as bacc
    from concourse.bass_utils import run_bass_kernel_spmd

    nc = bacc.Bacc("TRN2", target_bir_lowering=False, num_devices=1)
    arrays, args = {}, []
    for name in _INS:
        a = np.ascontiguousarray(inputs[name])
        arrays[name] = a
        args.append(nc.dram_tensor(name, a.shape, mybir.dt.from_np(a.dtype), kind="ExternalInput").ap())
    out = nc.dram_tensor("out", inputs["x"].shape, F32, kind="ExternalOutput").ap()
    gnn_ffn(nc, *args, out)
    return run_bass_kernel_spmd(nc, [arrays], core_ids=[0]).results[0]["out"]
```

```python
from contextlib import ExitStack

import concourse.bass as bass
from concourse import mybir

F32 = mybir.dt.float32
F16 = mybir.dt.float16
I32 = mybir.dt.int32
I16 = mybir.dt.int16
ALU = mybir.AluOpType
ACT = mybir.ActivationFunctionType
AX = mybir.AxisListType

ROUND = 1.5 * 2.0**23


def gnn_ffn(nc, x, src, dst, W_in, b_in, W_out, b_out, gamma, beta, Wr, br, W1, b1, W2, b2, out):
    N, D = x.shape
    E = src.shape[0]
    NP = 125
    T = N // NP
    DK = D // 128
    WIN = 5
    NR = T // WIN
    Q = WIN * T
    SL = 2
    SLOTS = SL * NP
    GRAN = 25
    ROWS = (E - SLOTS) // GRAN + 1
    COARSE = E // GRAN // NP
    STEPS = 6
    XS = 2.0**11
    C = WIN * SL
    NB = T // WIN
    EARLY = T - WIN
    EC = E // NP
    TAIL = SLOTS - GRAN
    assert N < 2**15 and EC % GRAN == 0
    assert N == NP * T and E % (GRAN * NP) == 0 and (E - SLOTS) % GRAN == 0

    NE, _, H = W1.shape
    HK = H // 128
    TOP = 2
    FT = (TOP * N + NE * 127) // 128
    FU = 8
    FR = 4
    LEAD = 4
    assert FT % FU == 0

    EU = 5
    PARTS = ((0, (T + 1) // 2), ((T + 1) // 2, T // 2))
    assert EC % EU == 0 and PARTS[0][1] * D <= 7 * 512
    term_dram = nc.dram_tensor("term_dram", (N, D), F32, kind="Internal").ap()
    xs_dram = nc.dram_tensor("xs_dram", (N, 2 * D), F16, kind="Internal").ap()
    y_dram = nc.dram_tensor("y_dram", (TOP * N, D), F32, kind="Internal").ap()
    xs_v = xs_dram.rearrange("(p t) f -> p t f", t=T)
    y_v = y_dram.rearrange("(k p t) f -> k p t f", k=TOP, t=T)
    out_v = out.rearrange("(p t) f -> p t f", t=T)
    edge_rows = nc.dram_tensor("edge_rows", (ROWS, 2 * SLOTS), I16, kind="Internal").ap()
    early_dram = nc.dram_tensor("early_dram", (N, 2 * D), F16, kind="Internal").ap()
    h_dram = nc.dram_tensor("h_dram", (N, D), F32, kind="Internal").ap()
    x_v = x.rearrange("(p t) f -> p t f", t=T)
    h_v = h_dram.rearrange("(p t) f -> p t f", t=T)
    early_v = early_dram.rearrange("(p t) f -> p t f", t=T)
    term_v = term_dram.rearrange("(p t) f -> p t f", t=T)

    with ExitStack() as ctx:
        def sb(name, shape, dt):
            return ctx.enter_context(nc.sbuf_tensor(name, shape, dt))

        def sem(name):
            return ctx.enter_context(nc.semaphore(name))

        ADJ = T * T * NP
        REG = 3126
        adj = sb("adj", [128, T * REG], F16)
        v_a = sb("v_a", [128, T * 2 * D], F16)
        v_b = sb("v_b", [128, T * 2 * D], F16)
        ps = ctx.enter_context(nc.psum_tensor("ps", [128, 8, 512], F32))

        def over(buf, at, n, dt, parts=128):
            size = 4 if dt in (F32, I32) else 2
            assert at % size == 0
            v = buf[0:parts, at // 2:at // 2 + n * size // 2]
            return v if dt == F16 else v.bitcast(dt)

        adj_w = adj[0:NP, 0:ADJ].rearrange("b (r q p) -> b r q p", r=NR, q=Q)
        adj_t = adj[0:NP, 0:ADJ].rearrange("b (t a p) -> b t a p", t=T, a=T)
        va = v_a[0:NP, :].rearrange("p (t f) -> p t f", t=T)
        vb = v_b[0:NP, :].rearrange("p (t f) -> p t f", t=T)

        cinv = sb("cinv", [128, STEPS, T], F32)
        h_ring = sb("h_ring", [128, 2, D], F32)
        t_hi = sb("t_hi", [128, D], F32)
        v_f = sb("v_f", [128, D], F32)
        scale = sb("scale", [128, 2], F32)

        in_windows = sb("in_windows", [128, 1], F32)
        ones_col = sb("ones_col", [128, 1], F32)
        covered = sb("covered", [1, 1], I32)

        at = (T - WIN) * T * NP * 2
        x_all = over(adj, at, T * D, F32, NP).rearrange("p (t f) -> p t f", t=T)
        at = 0
        def take(n, dt, parts=128):
            nonlocal at
            v = over(adj, at, n, dt, parts)
            at += (n * (4 if dt in (F32, I32) else 2) + 3) // 4 * 4
            return v

        src_i = take(EC + TAIL, I32, NP)
        dst_i32 = take(EC + TAIL, I32, NP)
        edges = take((EC + TAIL) * 2, F16, NP).bitcast(I16).rearrange("p (e k) -> p e k", k=2)
        w_raw = take(DK * D, F32).rearrange("o (b k) -> o b k", b=DK)
        w_sq = take(DK * D, F32).rearrange("o (b k) -> o b k", b=DK)
        x_n = [take(D, F32, NP) for _ in range(WIN)]
        assert at <= WIN * T * NP * 2
        at = (WIN * T * NP * 2 + 3) // 4 * 4
        above = take(COARSE * N // WIN, F16, NP).rearrange("p (j g) -> p j g", j=COARSE)
        iota_g = take(N // WIN, F16)
        key = take(COARSE, F32)
        key_t = take(COARSE, F32)
        ones16 = take(256 + 8, F16)
        starts = take(NR, F32)
        start_row = take(NR, I32)
        g_edges = take(NR * 2 * SLOTS, F16, NP).bitcast(I16).rearrange("p (r s k) -> p r s k", r=NR, k=2)
        e_b = take(NR * SLOTS, F32, NP).rearrange("p (r s) -> p r s", r=NR)
        e_q = take(NR * SLOTS, F32, NP).rearrange("p (r s) -> p r s", r=NR)
        e_d = take(NR * SLOTS, F32, NP).rearrange("p (r s) -> p r s", r=NR)
        win_base = take(NR, F32)
        dl_eq = take(T * SLOTS, F16, NP).rearrange("p (r d s) -> p r d s", r=NR, d=WIN)
        deg = take(T, F32)
        degc = take(T, F32)
        iota_row = take(128, F32)
        iota_col = take(1, F32)
        ident = take(128, F32)
        w_inH = take(DK * D, F16)
        w_inL = take(DK * D, F16)
        b_row = take(D, F32)
        b_hi = take(D, F16)
        b_lo = take(D, F16)
        b_col = take(DK, F32)
        b_abs = take(DK, F32)
        b_sq = take(DK, F32)
        bound = take(DK, F32)
        bmax = take(2, F32)
        ball = take(2, F32)
        w_scale = take(1, F32)
        w_unscale = take(1, F32)
        exp_i = take(1, I32)
        exp_j = take(2, I32)
        exp_w = take(3, I32)
        stats = take(T * 6, F32).rearrange("p (t s) -> p t s", s=6)
        mv = take(T * 2, F32).rearrange("p (t s) -> p t s", s=2)
        rstd = take(T, F32)
        rtmp = take(T, F32)
        ve = take(T, F32)
        xT_hi = [take(DK * NP, F16).rearrange("k (b p) -> k b p", b=DK) for _ in range(3)]
        xT_lo = [take(DK * NP, F16).rearrange("k (b p) -> k b p", b=DK) for _ in range(3)]
        h_f = [take(D, F32) for _ in range(3)]
        h_s = [take(D, F32) for _ in range(3)]
        assert at <= (T - WIN) * T * NP * 2, at

        at = 0

        def take_b(n, dt):
            nonlocal at
            v = over(v_b, at, n, dt, NP)
            at += n * 2
            return v

        iota_x = take_b(NP * C, F16).rearrange("e (x c) -> e x c", c=C)
        key_b = take_b(NP * C, F16).rearrange("e (r i k j) -> e r i k j", r=NR, k=SL, j=WIN)
        key_q = take_b(NP * C, F16).rearrange("e (r i k j) -> e r i k j", r=NR, k=SL, j=WIN)
        oh_b = [take_b(NP * C, F16).rearrange("e (x c) -> e x c", c=C) for _ in range(3)]
        oh_q = [take_b(NP * C, F16).rearrange("e (x c) -> e x c", c=C) for _ in range(3)]
        v_early = [take_b(2 * D, F16) for _ in range(3)]
        assert at <= T * 2 * D * 2

        x1 = adj[0:NP, :].bitcast(F32).rearrange("p (t r) -> p t r", t=T)[:, :, 0:D]
        XW = 2 * D
        EW = DK * H
        ex16 = adj[:, 0:3 * NE * REG].rearrange("p (e r) -> p e r", e=NE)
        ex32 = adj[:, 0:3 * NE * REG].bitcast(F32).rearrange("p (e r) -> p e r", e=NE)
        w1h, w1l = ex16[:, :, XW:XW + EW], ex16[:, :, XW + EW:XW + 2 * EW]
        w2h, w2l = ex16[:, :, REG + XW:REG + XW + EW], ex16[:, :, REG + XW + EW:REG + XW + 2 * EW]
        b2_bc = ex32[:, :, (XW + 2 * EW) // 2:(XW + 2 * EW) // 2 + D]
        w_f32 = ex32[:, :, (2 * REG + XW) // 2:(2 * REG + XW) // 2 + EW]
        assert EW == HK * D and XW + 2 * EW + 2 * D <= REG

        def taker(buf):
            used = [0]

            def take(n, dt, parts=128):
                v = over(buf, used[0], n, dt, parts)
                used[0] += (n * (4 if dt in (F32, I32) else 2) + 3) // 4 * 4
                assert used[0] <= (T * REG * 2 if buf is adj else T * 2 * D * 2), used
                return v
            return take

        fa = taker(v_a)
        ident2 = fa(128, F32)
        ident16 = fa(128, F16)
        ones2 = fa(128, F32)
        w_outT = fa(DK * D, F32).rearrange("k (b o) -> k b o", b=DK)
        bo_bc, ga_bc, be_bc = fa(D, F32), fa(D, F32), fa(D, F32)
        wr_sb = fa(DK * NE, F32).rearrange("k (b e) -> k b e", b=DK)
        br_bc = fa(NE, F32)
        lg = fa(T * NE, F32, NP).rearrange("p (t e) -> p t e", t=T)
        stats2 = fa(6, F32, NP)
        mv_t = fa(2, F32, NP)
        mv2 = fa(2 * T, F32, NP).rearrange("p (t s) -> p t s", s=2)
        ve2, sd2, rt2, r1 = (fa(WIN, F32, NP) for _ in range(4))
        rr = fa(T, F32, NP)
        gb_max = fa(2, F32)
        gb_sq = fa(2, F32)
        xn_sq = fa(2, F32)
        xs_scale = fa(2, F32)
        pow_i = fa(NE, I32)
        pow_j = fa(NE, I32)
        s1, s2, sh, i1, i2, ih, g1, g2 = (fa(NE, F32) for _ in range(8))
        w_max = fa(NE * (DK + HK), F32)
        w_sq2 = fa(NE * (DK + HK + HK), F32)
        w_sums = fa(NE * 3, F32).rearrange("p (a e) -> p a e", e=NE)
        b1T = fa(NE * HK, F32)
        tri = fa(NP, F32, NP)
        iota_e8 = fa(NE, F32, NP)
        iota_pos = fa(128, F16, NP)
        iota_tile = fa(FT, F16, NP)
        tile_row = fa(FT, F32)
        p_plus1 = fa(1, F32)
        ta_b = fa(T * TOP, F32)
        w_top1, w_top2 = fa(T, F32, NP), fa(T, F32, NP)
        idx_g, idx_s = fa(FT, I32), fa(FT, I32)
        exp_of = over(v_a, T * 2 * D * 2 - T * TOP * 2 * FT * 2 - 16 * (FT + LEAD), FT + LEAD, I32)
        vfin = [fa(D, F32, NP) for _ in range(3)]
        vT = fa(DK * NP, F32).rearrange("k (b p) -> k b p", b=DK)
        x_i = [fa(D, F32, NP) for _ in range(3)]
        xn2 = [fa(D, F32, NP) for _ in range(3)]
        xnT = fa(DK * NP, F32).rearrange("k (b p) -> k b p", b=DK)
        xs_f = fa(3 * 2 * D, F16)
        xs_r = [xs_f[0:NP, j * 2 * D:(j + 1) * 2 * D] for j in range(3)]
        w_oraw = xs_f[:, 0:2 * DK * D].bitcast(F32).rearrange("o (b k) -> o b k", b=DK)
        fb = taker(v_b)
        b1_rows = fb(128, F32, NE * HK)
        oh1, oh2, tmp1, tmp2, both, sum_a, sum_b, pos = (fb(T * NE, F32, NP).rearrange("p (t e) -> p t e", t=T) for _ in range(8))
        m1, m2, n1, slot1, slot2, ex2, den = (fb(T, F32, NP) for _ in range(7))
        per_p = fb(NE, F32, NP)
        totals, tiles_a, tiles_b, tiles_c = (fb(NE, F32) for _ in range(4))
        slot_base = fb(NE, F32, NP)
        s_all, s_tile, s_pin = (fb(T * TOP, F32, NP) for _ in range(3))
        tok_p, tok_b, dest, empty = (fb(FT, F32) for _ in range(4))
        le_tiles = fb(FT * NE, F32).rearrange("p (j e) -> p j e", e=NE)
        oh_pos = fb(T * TOP * 128, F16, NP).rearrange("p (c x) -> p c x", x=128)
        PL = 2 * FT
        planes = over(v_a, T * 2 * D * 2 - T * TOP * PL * 2, T * TOP * PL, F16, NP).rearrange("p (c y) -> p c y", y=PL)
        fc = taker(v_b)
        x_g = [fc(2 * D, F16) for _ in range(FU)]
        xT16 = [fc(2 * D, F16).rearrange("k (b s) -> k b s", b=2 * DK) for _ in range(2)]
        h_g = [fc(H, F32) for _ in range(2)]
        h_hi = [fc(H, F16).rearrange("h (b s) -> h b s", b=HK) for _ in range(FR)]
        h_lo = [fc(H, F16).rearrange("h (b s) -> h b s", b=HK) for _ in range(FR)]
        at_y = ((T - 1) * REG + XW) * 2
        y_sb = [over(adj, at_y + r * D * 4, D, F32) for r in range(FR)]
        ig = [fc(1, I32) for _ in range(FU)]
        isc = [fc(1, I32) for _ in range(FR)]
        fd = taker(v_b)
        y_in = [[fd(WIN * D, F32, NP).rearrange("p (t f) -> p t f", t=WIN) for _ in range(TOP)] for _ in range(2)]

        fe = taker(adj)
        src_e, dst_i = fe(EC, I32, NP), fe(EC, I32, NP)
        dst_e = fe(EC, F32, NP)
        node = fe(N, F32, NP).rearrange("e (t p) -> e t p", t=T)
        oh_e = [fe(PARTS[0][1] * NP, F32, NP).rearrange("e (t p) -> e t p", p=NP) for _ in range(EU)]
        rows_e = [fe(D, F32, NP) for _ in range(EU)]
        src_col = [fe(1, I32, NP) for _ in range(EU)]
        ones_e, zeros_e = fe(1, F32, NP), fe(512, F32, 1)
        k_inv = fe(STEPS, F32, NP)
        deg_e = fe(T, F32, NP)
        term_e = fe(T * D, F32, NP).rearrange("p (t f) -> p t f", t=T)
        h_e = fe(T * D, F32, NP).rearrange("p (t f) -> p t f", t=T)

        names = """rows_made src_in dst_in edges_ok w_in_in iotas ident_ok above_ok count_ok start_ok
            deg_ok wscale_ok whi_ok xlo_ok b_ok early_back
            keys_ok keyT_ps keyT_ok stats_ok std_ok rstd_ok wT_ps wT_ok bound_ok ball_ok scale_ok xn_ok xT_ps xT_ok
            h_ps h_act v_ready oh_ready win_ps win_out tile_ps hi_ok psum_read h_used
            f_const pool_const bo_mat w_oT_ps w_oT_ok vfin_ok vT_ps vT_ok y_ps xb_ok x1_ok ve_ok sd_ok z_ok xn2_ok xnT_ps xnT_ok
            lg_ps lg_ok xhi_ok xs_ok b1_in b1T_ps b1T_ok w_sq_ok w_sum_ps w1_hi w1_lo w2_hi w2_lo wsc_ok
            ex_in ex_ok cnt_in cnt_ok rt_done tok_ps idx_ok
            pool_turn cover_sum cover_ps cover_ok term_ok e_const e_in e_col e_oh e_mm e_acc e_read e_term e_rows
            ig_ok is_ok xg_T xgT_ok ffn_h gelu_ok hs_ok ffn_y y_ok y_free comb_ok""".split()
        S = {n: sem(n) for n in names}
        gathered = [sem(f"gathered{r}") for r in range(NR)]
        h_in = [sem(f"h_in{r}") for r in range(2)]
        h_out = [sem(f"h_out{r}") for r in range(3)]
        x_in = [sem(f"x_in{i}") for i in range(NB)]
        early_out = [sem(f"early_out{r}") for r in range(3)]
        xs_out = [sem(f"xs_out{r}") for r in range(3)]
        xi_in = [sem(f"xi_in{r}") for r in range(3)]
        w1_in = sem("w1_in")
        w2_in = [sem(f"w2_in{e}") for e in range(NE)]
        g_in = [sem(f"g_in{r}") for r in range(FU)]
        y_out = [sem(f"y_out{r}") for r in range(FR)]
        yc_in = [sem(f"yc_in{r}") for r in range(2)]
        out_sem = sem("out_sem")
        e_gathered = [sem(f"e_gathered{r}") for r in range(EU)]

        block = ctx.enter_context(nc.Block())
        RB = [0, 1, 2, 0, 1]
        AGE = [2, 2, 5, 3, 3]
        PRIOR = [(2, 0), (2, 0), (1, 0), (2, 1), (2, 1)]
        LAST = (STEPS - 1) * T

        def ring(d, u):
            return RB[(u - d) % WIN]

        def uses(i, u, d):
            w = (u - d) % WIN
            group = i + (u - d - w) // WIN
            return PRIOR[w][0] * group + PRIOR[w][1]

        def need(eng, s, value):
            if not (isinstance(value, int) and value <= 0):
                eng.wait_ge(s, value)

        def experts(i, eng):
            _, es = nc.values_load_multi_w_load_instructions(
                exp_of[0:1, bass.ds(FU * i, LEAD + FU)], engines=[eng.engine], min_val=0, max_val=NE - 1,
                skip_runtime_bounds_check_because="a minimum with NE - 1 of a count made exp_of")
            return es

        def win_cells(slot):
            return ps[0:NP, 2 * slot:2 * slot + 2, :].rearrange("b k c -> b (k c)")[:, 0:WIN * 128]

        def early_bank(w):
            return 6 + w % WIN % 2

        def with_lag(eng, lag, body):
            def group(i):
                for u in range(WIN if i is not NB else lag):
                    body(i, u, lambda d: not isinstance(i, int) or 0 <= WIN * i + u - d < T)
            group(0)
            with eng.Fori(1, NB) as i:
                group(i)
            group(NB)

        def feature_tiles(eng, transposed, features):
            def tile(i, u, has):
                if has(0):
                    transposed(i, u)
                if has(2):
                    features(i + (u - 2) // WIN, (u - 2) % WIN)
            with_lag(eng, 2, tile)

        def loop(eng, first, end, body):
            if end - first == 1:
                body(first)
            else:
                with eng.Fori(first, end) as i:
                    body(i)

        def early_step(eng, body):
            def group(i):
                for u in range(WIN):
                    body(i, u, lambda d: not isinstance(i, int) or 0 <= WIN * i + u - d < EARLY)
            group(0)
            with eng.Fori(1, EARLY // WIN) as i:
                group(i)
            group(EARLY // WIN)

        def last_step(eng, body):
            def peeled(i):
                for u in range(WIN):
                    body(i, u, lambda d: 0 <= WIN * i + u - d < T)
            peeled(0)
            peeled(1)
            with eng.Fori(2, NB) as i:
                for u in range(WIN):
                    body(i, u, lambda d: True)
            peeled(NB)
            peeled(NB + 1)

        @block.sync
        def _(sp):
            for a, on_chip, s in ((dst, dst_i32, "dst_in"), (src, src_i, "src_in")):
                sp.dma_start(on_chip[0:NP - 1, :], bass.AP(a.tensor, 0, [[EC, NP - 1], [1, EC + TAIL]])).then_inc(S[s], 16)
                sp.dma_start(on_chip[NP - 1:NP, 0:EC], bass.AP(a.tensor, (NP - 1) * EC, [[EC, 1], [1, EC]])).then_inc(S[s], 16)
            sp.wait_ge(S["edges_ok"], 1)
            whole = (NP - 1) * COARSE
            flat = edges.rearrange("p e k -> p (e k)")

            def rows(parts, count):
                v = flat[parts, 0:2 * SLOTS]
                return bass.AP(v.tensor, v.offset, [list(v.ap[0]), [2 * GRAN, count], [1, 2 * SLOTS]])
            sp.dma_start(edge_rows[0:whole, :].rearrange("(p j) s -> p j s", j=COARSE),
                         rows(slice(0, NP - 1), COARSE)).then_inc(S["rows_made"], 16)
            sp.dma_start(edge_rows[whole:ROWS, :].rearrange("(p j) s -> p j s", p=1),
                         rows(slice(NP - 1, NP), ROWS - whole)).then_inc(S["rows_made"], 16)
            with sp.Fori(0, NB) as i:
                for u in range(WIN):
                    sp.wait_ge(S["v_ready"], 5 * i + u + 1)
                    sp.dma_start(h_v[:, bass.ds(5 * i + u, 1), :].rearrange("p a f -> p (a f)"), h_s[RB[u]][0:NP, :]).then_inc(h_out[RB[u]], 16)
            for slot, per in enumerate((2, 2, 1)):
                sp.wait_ge(h_out[slot], 16 * per * NB)

            def step(n0, t0, t1):
                def tiles(i):
                    for u in range(WIN):
                        n = n0 - t0 + WIN * i + u
                        if u == 0:
                            sp.wait_ge(S["h_used"], n + 2)
                        elif u > 1:
                            sp.wait_ge(S["h_used"], n + 1)
                        sp.dma_start(h_ring[0:NP, u % 2, :],
                                     h_v[:, bass.ds(5 * i + u, 1), :].rearrange("p a f -> p (a f)")).then_inc(h_in[u % 2], 16)
                loop(sp, t0 // WIN, t1 // WIN, tiles)

            def early(i, u, has):
                n = WIN * i + u
                if has(0):
                    if u == 0:
                        sp.wait_ge(S["h_used"], n + 2)
                    elif u > 1:
                        sp.wait_ge(S["h_used"], n + 1)
                    sp.dma_start(h_ring[0:NP, u % 2, :],
                                 h_v[:, bass.ds(n, 1), :].rearrange("p a f -> p (a f)")).then_inc(h_in[u % 2], 16)
                if has(2):
                    sp.wait_ge(S["v_ready"], T + n - 1)
                    sp.dma_start(early_v[:, bass.ds(n - 2, 1), :].rearrange("p a f -> p (a f)"),
                                 v_early[ring(2, u)]).then_inc(early_out[ring(2, u)], 16)
            early_step(sp, early)
            for r, per in enumerate((2, 2, 1)):
                sp.wait_ge(early_out[r], 16 * per * (EARLY // WIN))
            sp.wait_ge(S["win_ps"], NR * T + 2)
            sp.dma_start(vb[:, 0:EARLY, :], early_v[:, 0:EARLY, :]).then_inc(S["early_back"], 16)
            step(EARLY, EARLY, T)
            for s in range(1, STEPS - 1):
                step(s * T, 0, T)
            sp.wait_ge(S["term_ok"], 1)

            def bc(v, n):
                return bass.AP(v.tensor, 0, [[0, 128], [1, n]])
            sp.dma_start(w_oraw, W_out.rearrange("(b o) k -> o b k", o=128)).then_inc(S["f_const"], 16)
            sp.dma_start(bo_bc, bc(b_out, D)).then_inc(S["f_const"], 16)
            sp.dma_start(ga_bc, bc(gamma, D)).then_inc(S["f_const"], 16)
            sp.dma_start(be_bc, bc(beta, D)).then_inc(S["f_const"], 16)
            sp.dma_start(wr_sb, Wr.rearrange("(b k) e -> k b e", k=128)).then_inc(S["f_const"], 16)
            sp.dma_start(br_bc, bc(br, NE)).then_inc(S["f_const"], 16)

            def body(i, u, has):
                m = 5 * i + u
                n = LAST + m
                if has(0):
                    if u == 0:
                        sp.wait_ge(S["h_used"], n + 2)
                    elif u > 1:
                        sp.wait_ge(S["h_used"], n + 1)
                    sp.dma_start(h_ring[0:NP, u % 2, :],
                                 h_v[:, bass.ds(m, 1), :].rearrange("p a f -> p (a f)")).then_inc(h_in[u % 2], 16)
                    need(sp, S["x1_ok"], m - 1)
                    sp.dma_start(x_i[RB[u]], x_v[:, bass.ds(m, 1), :].rearrange("p a f -> p (a f)")).then_inc(xi_in[RB[u]], 16)
                if has(8):
                    sp.wait_ge(S["xs_ok"], m - 7)
                    sp.dma_start(xs_v[:, bass.ds(m - 8, 1), :].rearrange("p a f -> p (a f)"), xs_r[ring(8, u)]).then_inc(xs_out[ring(8, u)], 16)
            last_step(sp, body)
            sp.dma_start(b1_rows, b1.rearrange("e (b h) -> (e b) h", h=128)).then_inc(S["b1_in"], 16)
            for b in range(DK):
                sp.dma_start(w_f32[:, :, b * H:(b + 1) * H], W1[:, b * 128:(b + 1) * 128, :].rearrange("e k h -> k e h")).then_inc(w1_in, 16)
            sp.dma_start(b2_bc, bass.AP(b2.tensor, 0, [[0, 128], [D, NE], [1, D]])).then_inc(S["b1_in"], 16)
            for e in range(NE):
                sp.wait_ge(S["w1_lo"], e + 1)
                sp.dma_start(w_f32[:, e, :].rearrange("h (b d) -> h b d", b=HK),
                             W2[e].rearrange("(b h) d -> h b d", h=128)).then_inc(w2_in[e], 16)
            for r in range(FR):
                sp.wait_ge(y_out[r], 16 * (FT // FR))
            for i in range(NB):
                if i >= 2:
                    sp.wait_ge(S["comb_ok"], i - 1)
                for k in range(TOP):
                    sp.dma_start(y_in[i % 2][k], y_v[k, :, i * WIN:(i + 1) * WIN, :]).then_inc(yc_in[i % 2], 16)
            for i in range(NB):
                sp.wait_ge(S["comb_ok"], i + 1)
                sp.dma_start(out_v[:, i * WIN:(i + 1) * WIN, :], x1[:, i * WIN:(i + 1) * WIN, :]).then_inc(out_sem, 16)
            sp.wait_ge(out_sem, 16 * NB)

        @block.gpsimd
        def _(pool):
            g = nc.gpsimd
            g.iota(iota_g, [[1, N // WIN]], base=0, channel_multiplier=0, allow_small_or_imprecise_dtypes=True)
            g.iota(iota_row, [[1, 128]], base=0, channel_multiplier=0, allow_small_or_imprecise_dtypes=True)
            g.iota(iota_col, [[0, 1]], base=0, channel_multiplier=1, allow_small_or_imprecise_dtypes=True)
            g.memset(ones_col[:, :], 1.0)
            g.memset(ones16[:, 0:128], 1.0)
            g.memset(ones16[:, 256:264], 0.0)
            g.memset(ones16[:, 128:256], XS).then_inc(S["iotas"], 1)
            g.iota(win_base, [[T * WIN, NR]], base=0, channel_multiplier=T * T, allow_small_or_imprecise_dtypes=True)
            g.iota(iota_x, [[1, NP], [0, C]], base=0, channel_multiplier=0,
                   allow_small_or_imprecise_dtypes=True).then_inc(S["iotas"], 1)
            pool.wait_ge(S["bound_ok"], 1)
            g.partition_all_reduce(ball, bmax, 128, bass.bass_isa.ReduceOp.max).then_inc(S["ball_ok"], 1)
            pool.wait_ge(S["rows_made"], 32)
            pool.wait_ge(S["start_ok"], 1)
            for r in range(NR):
                g.indirect_dma_start(g_edges[:, r, :, :].rearrange("p s k -> p (s k)"), None, edge_rows,
                                     bass.IndirectOffsetOnAxis(ap=start_row[0:NP, r:r + 1], axis=0),
                                     ).then_inc(gathered[r], 16)
            pool.wait_ge(S["keys_ok"], 1)
            for d in range(WIN):
                last = g.tensor_scalar(dl_eq[:, :, d, :], e_d, float(T * d), None, ALU.is_equal)
            last.then_inc(S["deg_ok"], 1)
            pool.wait_ge(S["cover_ok"], 1)
            fast = pool.value_load(covered[:, :], min_val=0, max_val=1)
            with pool.If(fast == 0):
                pool.wait_ge(S["v_ready"], T * STEPS)
                for slot, per in enumerate((2, 2, 1)):
                    pool.wait_ge(h_out[slot], 16 * per * NB)
                g.dma_start(src_e, src.rearrange("(p e) -> p e", p=NP)).then_inc(S["e_in"], 16)
                g.dma_start(dst_i, dst.rearrange("(p e) -> p e", p=NP)).then_inc(S["e_in"], 16)
                g.dma_start(h_e, h_v).then_inc(S["e_in"], 16)
                g.dma_start(term_v, h_v).then_inc(S["e_rows"], 16)
                g.iota(node, [[1, T], [T, NP]], base=0, channel_multiplier=0, allow_small_or_imprecise_dtypes=True)
                g.memset(ones_e, 1.0)
                for s in range(STEPS):
                    g.memset(k_inv[:, s:s + 1], 1.0 / (STEPS - s))
                g.memset(zeros_e, 0.0).then_inc(S["e_const"], 1)
                pool.wait_ge(S["e_in"], 48)
                with pool.Fori(0, STEPS) as s:
                    pool.wait_ge(S["e_rows"], s * 16 + 16)
                    pool.sem_inc(S["pool_turn"], 1)
                    for part in range(2):
                        with pool.Fori(0, EC // EU) as i:
                            for u in range(EU):
                                n = s * (2 * EC) + i * EU + (part * EC + u)
                                pool.wait_ge(S["e_mm"], n + 1)
                                pool.sem_inc(S["pool_turn"], 1)
                                g.tensor_copy(src_col[u], src_e[:, bass.ds(i * EU + u, 1)]).then_inc(S["e_col"], 1)
                                pool.wait_ge(S["e_col"], n + 1)
                                pool.sem_inc(S["pool_turn"], 1)
                                g.indirect_dma_start(rows_e[u], None, term_dram,
                                                     bass.IndirectOffsetOnAxis(ap=src_col[u], axis=0)).then_inc(e_gathered[u], 16)
                    pool.wait_ge(S["e_term"], s + 1)
                    pool.sem_inc(S["pool_turn"], 1)
                    g.dma_start(term_v, term_e).then_inc(S["e_rows"], 16)
                pool.wait_ge(S["e_rows"], 16 * (STEPS + 1))
                g.dma_start(h_v, term_e).then_inc(S["e_rows"], 16)
            pool.wait_ge(S["term_ok"], 1)
            g.memset(ident2, 0.0)
            g.memset(ident16, 0.0)
            g.memset(ones2, 1.0)
            g.memset(tri, 1.0)
            g.iota(iota_e8, [[1, NE]], base=-NE, channel_multiplier=0, allow_small_or_imprecise_dtypes=True)
            g.iota(iota_pos, [[1, 128]], base=0, channel_multiplier=0, allow_small_or_imprecise_dtypes=True)
            g.iota(iota_tile, [[1, FT]], base=0, channel_multiplier=0, allow_small_or_imprecise_dtypes=True)
            g.iota(tile_row, [[1, FT]], base=0, channel_multiplier=0, allow_small_or_imprecise_dtypes=True)
            g.iota(p_plus1, [[0, 1]], base=1, channel_multiplier=1, allow_small_or_imprecise_dtypes=True)
            g.iota(ta_b, [[1, T * TOP]], base=0, channel_multiplier=0, allow_small_or_imprecise_dtypes=True).then_inc(S["bo_mat"], 1)
            pool.wait_ge(S["bo_mat"], 1)
            g.affine_select(out=ident2, in_=ident2, compare_op=ALU.not_equal, fill=1.0, base=0, pattern=[[-1, 128]], channel_multiplier=1)
            g.affine_select(out=ident16, in_=ident16, compare_op=ALU.not_equal, fill=1.0, base=0, pattern=[[-1, 128]], channel_multiplier=1)
            g.affine_select(out=tri, in_=tri, compare_op=ALU.is_gt, fill=0.0, base=0, pattern=[[1, NP]],
                            channel_multiplier=-1).then_inc(S["pool_const"], 1)
            pool.wait_ge(S["f_const"], 96)

            def body(i, u, has):
                m = 5 * i + u
                if has(7):
                    pool.wait_ge(S["z_ok"], m - 6)
                    g.tensor_tensor(xn2[ring(7, u)], xn2[ring(7, u)], be_bc[0:NP, :], ALU.add).then_inc(S["xn2_ok"], 1)
                if has(0):
                    pool.wait_ge(xi_in[RB[u]], 16 * (uses(i, u, 0) + 1))
                    g.tensor_tensor(x_i[RB[u]], x_i[RB[u]], bo_bc[0:NP, :], ALU.add).then_inc(S["xb_ok"], 1)
            last_step(pool, body)
            for r, per in enumerate((2, 2, 1)):
                pool.wait_ge(xs_out[r], 16 * per * NB)
            pool.wait_ge(S["idx_ok"], 1)

            def gather(i, u):
                j = FU * i + u
                need(pool, g_in[u], 16 * i)
                pool.sem_inc(S["pool_turn"], 1)
                g.tensor_copy(ig[u], idx_g[:, bass.ds(j, 1)]).then_inc(S["ig_ok"], 1)
                need(pool, S["xg_T"], j - FU + 1)
                pool.wait_ge(S["ig_ok"], j + 1)
                pool.sem_inc(S["pool_turn"], 1)
                g.indirect_dma_start(x_g[u], None, xs_dram, bass.IndirectOffsetOnAxis(ap=ig[u], axis=0)).then_inc(g_in[u], 16)

            def scatter(i, u):
                j = FU * i + u
                r = u % FR
                need(pool, y_out[r], 16 * (FU // FR * i + u // FR))
                pool.sem_inc(S["pool_turn"], 1)
                g.tensor_copy(isc[r], idx_s[:, bass.ds(j, 1)]).then_inc(S["is_ok"], 1)
                pool.wait_ge(S["y_ok"], j + 1)
                pool.wait_ge(S["is_ok"], j + 1)
                pool.sem_inc(S["pool_turn"], 1)
                g.indirect_dma_start(y_dram, bass.IndirectOffsetOnAxis(ap=isc[r], axis=0), y_sb[r], None,
                                     bounds_check=TOP * N - 1, oob_is_err=False).then_inc(y_out[r], 16)

            def tiles(i, last):
                for u in range(FU):
                    if not (last and u):
                        gather(i + (u + FU - 1) // FU, (u + FU - 1) % FU)
                    scatter(i, u)
            for u in range(FU - 1):
                gather(0, u)
            tiles(0, False)
            with pool.Fori(1, FT // FU - 1) as i:
                tiles(i, False)
            tiles(FT // FU - 1, True)

        @block.scalar
        def _(act):
            a = nc.scalar
            act.dma_start(w_raw, W_in.rearrange("(b o) k -> o b k", o=128)).then_inc(S["w_in_in"], 16)
            act.dma_start(b_row[0:1, :], b_in[None, :]).then_inc(S["w_in_in"], 16)
            act.dma_start(b_col, b_in.rearrange("(b o) -> o b", o=128), allow_slow_non_contiguous=True).then_inc(S["w_in_in"], 16)
            for i in range(NB):
                act.dma_start(x_all[:, i * WIN:(i + 1) * WIN, :], x_v[:, i * WIN:(i + 1) * WIN, :]).then_inc(x_in[i], 16)
            act.wait_ge(S["wT_ps"], 1)
            act.wait_ge(S["wscale_ok"], 1)
            a.activation(w_inH, ps[:, 7, :], ACT.Copy, scale=w_scale[:, 0:1])
            a.activation(b_hi[0:1, :], b_row[0:1, :], ACT.Copy, scale=w_scale[0:1, 0:1]).then_inc(S["whi_ok"], 1)
            act.wait_ge(S["stats_ok"], 1)
            a.activation(rstd[0:NP, :], ve[0:NP, :], ACT.Sqrt).then_inc(S["std_ok"], 1)

            def transposed(i, u):
                n = WIN * i + u
                act.wait_ge(S["xT_ps"], n + 1)
                need(act, S["h_ps"], n - AGE[u] + 1)
                a.activation(xT_hi[RB[u]], ps[:, RB[u], 0:DK * 128].rearrange("k (b p) -> k b p", b=DK)[:, :, 0:NP],
                             ACT.Copy).then_inc(S["xT_ok"], 1)

            def features(i, u):
                n = WIN * i + u
                act.wait_ge(S["h_ps"], n + 1)
                need(act, S["v_ready"], n - AGE[u] + 1)
                a.activation(h_f[RB[u]][0:NP, :], ps[0:NP, 3 + RB[u], 0:D], ACT.Silu, scale=w_unscale[0:NP, 0:1])
                a.drain()
                a.activation(va[:, bass.ds(n, 1), 0:D].rearrange("p a f -> p (a f)"), h_f[RB[u]][0:NP, :], ACT.Copy,
                             scale=scale[0:NP, 0:1]).then_inc(S["h_act"], 1)
            feature_tiles(act, transposed, features)

            def window(r, i, u):
                bt = T * r + WIN * i + u
                act.wait_ge(S["win_ps"], bt + 1 + 2)
                cells = win_cells(RB[u]).rearrange("b (c q) -> b c q", q=128)[:, :, 0:Q]
                row = bass.ds(r, 1) if not isinstance(r, int) else slice(r, r + 1)
                a.activation(adj_w[:, row, :, bass.ds(T * i + WIN * u, WIN)].rearrange("b o q p -> b (o q) p"),
                             cells.rearrange("b c q -> b q c"), ACT.Copy).then_inc(S["win_out"], 1)

            def high(n0, s, i, u, bank):
                n = n0 + WIN * i + u
                act.wait_ge(S["tile_ps"], n + 1)
                act.wait_ge(S["psum_read"], n + 5)
                a.activation(t_hi[0:NP, :], ps[0:NP, bank, 0:D], ACT.Copy,
                             scale=cinv[0:NP, s, bass.ds(WIN * i + u, 1)]).then_inc(S["hi_ok"], 1)
            with act.Fori(0, NB) as i:
                for u in range(WIN):
                    window(0, i, u)
            for slot, per in enumerate((2, 2, 1)):
                act.wait_ge(h_out[slot], 16 * per * NB)

            def group(r):
                for w in range(WIN):
                    if not (isinstance(r, int) and r == 1 and w == 0):
                        high(0, 0, r - 1 + (w - 1) // WIN, (w - 1) % WIN, early_bank(w - 1))
                    for u in range(WIN):
                        window(r, w, u)
            group(1)
            with act.Fori(2, NR) as r:
                group(r)
            high(0, 0, NR - 2, WIN - 1, early_bank(-1))

            def step(n0, s, t0, t1):
                def tiles(i):
                    for u in range(WIN):
                        high(n0, s, i, u, u)
                loop(act, t0 // WIN, t1 // WIN, tiles)
            step(0, 0, EARLY, T)
            for s in range(1, STEPS - 1):
                step(s * T, s, 0, T)
            act.wait_ge(S["w_oT_ps"], 1)
            a.activation(w_outT, ps[:, 7, :].rearrange("k (b o) -> k b o", b=DK), ACT.Copy).then_inc(S["w_oT_ok"], 1)

            def body(i, u, has):
                m = 5 * i + u
                n = LAST + m
                if u == 2 and has(7):
                    for k in range(2):
                        act.wait_ge(S["ve_ok"], 2 * i + k - 1)
                        a.activation(sd2, ve2, ACT.Sqrt).then_inc(S["sd_ok"], 1)
                if has(7):
                    act.wait_ge(S["xn2_ok"], m - 6)
                    need(act, xs_out[ring(7, u)], 16 * uses(i, u, 7))
                    a.activation(xs_r[ring(7, u)][:, 0:D], xn2[ring(7, u)], ACT.Copy, scale=xs_scale[0:NP, 0:1]).then_inc(S["xhi_ok"], 1)
                if has(0):
                    act.wait_ge(S["tile_ps"], n + 1)
                    act.wait_ge(S["psum_read"], n + 5)
                    a.activation(t_hi[0:NP, :], ps[0:NP, RB[u], 0:D], ACT.Copy,
                                 scale=cinv[0:NP, STEPS - 1, bass.ds(m, 1)]).then_inc(S["hi_ok"], 1)
                if has(7):
                    act.wait_ge(S["xnT_ps"], m - 6)
                    need(act, S["lg_ps"], m - 7)
                    a.activation(xnT, ps[:, 4, 0:DK * 128].rearrange("k (b p) -> k b p", b=DK)[:, :, 0:NP], ACT.Copy).then_inc(S["xnT_ok"], 1)
                if has(1):
                    act.wait_ge(S["vT_ps"], m)
                    need(act, S["y_ps"], m - 1)
                    a.activation(vT, ps[:, 3, 0:DK * 128].rearrange("k (b p) -> k b p", b=DK)[:, :, 0:NP], ACT.Copy).then_inc(S["vT_ok"], 1)
            last_step(act, body)
            act.wait_ge(S["b1T_ps"], 1)
            a.activation(b1T, ps[:, 5, 0:NE * HK], ACT.Copy).then_inc(S["b1T_ok"], 1)
            act.wait_ge(S["ex_in"], 1)
            a.activation(ex2, m2, ACT.Exp).then_inc(S["ex_ok"], 1)
            act.wait_ge(S["wsc_ok"], 1)
            for e in range(NE):
                a.activation(w1h[:, e, :], w_f32[:, e, :], ACT.Copy, scale=s1[:, e:e + 1]).then_inc(S["w1_hi"], 1)
            act.wait_ge(S["wsc_ok"], 2)
            for e in range(NE):
                a.activation(w2h[:, e, :], w_f32[:, e, :], ACT.Copy, scale=s2[:, e:e + 1]).then_inc(S["w2_hi"], 1)
            act.wait_ge(S["wsc_ok"], 3)
            act.wait_ge(S["idx_ok"], 1)

            def tile(i, u, e):
                j = FU * i + u
                r = u % 2
                act.wait_ge(S["ffn_h"], j + 1)
                need(act, S["hs_ok"], j - 1)
                for b in range(HK):
                    last = a.activation(h_g[r][:, b * 128:(b + 1) * 128], ps[:, 2 + r, b * 128:(b + 1) * 128], ACT.Gelu,
                                        bias=b1T[:, bass.ds(e * HK + b, 1)], scale=g1[:, bass.ds(e, 1)])
                last.then_inc(S["gelu_ok"], 1)
            def group(i):
                es = experts(i, act)
                for u in range(FU):
                    tile(i, u, es[LEAD + u])
            group(0)
            with act.Fori(1, FT // FU) as i:
                group(i)

        @block.vector
        def _(dve):
            v = nc.vector
            dve.wait_ge(S["dst_in"], 32)
            v.tensor_scalar(key_t[0:NP, :], dst_i32[:, 0:EC].rearrange("p (j g) -> p j g", g=GRAN)[:, :, 0], 1.0 / WIN, 0.5 / WIN - 0.5,
                            ALU.mult, ALU.add)
            v.drain()
            v.tensor_scalar(key[0:NP, :], key_t[0:NP, :], ROUND, ROUND, ALU.add, ALU.subtract)
            dve.wait_ge(S["src_in"], 32)
            for k, ids in enumerate((src_i, dst_i32)):
                v.tensor_copy(edges[:, 0:EC, k], ids[:, 0:EC])
                v.tensor_copy(edges[0:NP - 1, EC:EC + TAIL, k], ids[0:NP - 1, EC:EC + TAIL])
            v.drain().then_inc(S["edges_ok"], 1)
            dve.wait_ge(S["iotas"], 1)
            v.drain()
            for j in range(COARSE):
                v.tensor_scalar(above[:, j, :], iota_g[0:NP, :], key[0:NP, j:j + 1], None, ALU.is_gt).then_inc(S["above_ok"], 1)
            v.tensor_scalar(ident, iota_row, iota_col, None, ALU.is_equal).then_inc(S["ident_ok"], 1)
            dve.wait_ge(S["w_in_in"], 48)
            v.tensor_tensor(w_sq, w_raw, w_raw, ALU.mult)
            v.tensor_tensor(b_sq, b_col, b_col, ALU.mult)
            v.tensor_reduce(b_abs, w_raw, AX.X, ALU.max, apply_absolute_value=True)
            v.drain()
            v.tensor_reduce(bound, w_sq, AX.X, ALU.add)
            v.tensor_tensor(b_abs, b_abs, b_abs, ALU.mult)
            v.drain()
            v.tensor_tensor(b_abs, b_abs, b_sq, ALU.max)
            v.scalar_tensor_tensor(bound, bound, float(D), b_sq, ALU.mult, ALU.add)
            v.drain()
            v.tensor_reduce(bmax[:, 1:2], b_abs, AX.X, ALU.max)
            v.tensor_reduce(bmax[:, 0:1], bound, AX.X, ALU.max)
            v.drain().then_inc(S["bound_ok"], 1)
            for t in range(T):
                if t % WIN == 0:
                    dve.wait_ge(x_in[t // WIN], 16)
                v.bn_stats(stats[0:NP, t, :], x_all[:, t, :])
            v.drain()
            for t in range(T):
                v.bn_aggr(mv[0:NP, t, :], stats[0:NP, t, :])
            v.drain()
            v.tensor_scalar(ve[0:NP, :], mv[0:NP, :, 1], 1e-5, None, ALU.add).then_inc(S["stats_ok"], 1)
            dve.wait_ge(S["count_ok"], 1)
            v.tensor_scalar(starts[0:NP, :], ps[0:NP, 6, 0:NR], -1.0, 0.0, ALU.add, ALU.max)
            v.drain()
            v.tensor_scalar(start_row[0:NP, :], starts[0:NP, :], float(ROWS - 1), None, ALU.min).then_inc(S["start_ok"], 1)
            dve.wait_ge(S["ball_ok"], 1)
            v.tensor_scalar(bmax, ball, 2.0, None, ALU.mult)
            v.drain()
            v.tensor_scalar(exp_i, bmax.bitcast(I32)[:, 0:1], 24, None, ALU.logical_shift_right)
            v.tensor_scalar(exp_w[:, 0:1], bmax.bitcast(I32)[:, 1:2], 24, None, ALU.logical_shift_right)
            v.drain()
            v.tensor_scalar(exp_j[:, 0:1], exp_i, -1.0, 202.0, ALU.mult, ALU.add)
            v.tensor_scalar(exp_j[:, 1:2], exp_i, 52.0, None, ALU.add)
            v.tensor_scalar(exp_w[:, 1:2], exp_w[:, 0:1], -1.0, 203.0, ALU.mult, ALU.add)
            v.tensor_scalar(exp_w[:, 2:3], exp_w[:, 0:1], 51.0, None, ALU.add)
            v.drain()
            v.tensor_scalar(scale[:, :].bitcast(I32), exp_j, 23, None, ALU.logical_shift_left)
            v.tensor_scalar(w_scale.bitcast(I32), exp_w[:, 1:2], 23, None, ALU.logical_shift_left)
            v.tensor_scalar(w_unscale.bitcast(I32), exp_w[:, 2:3], 23, None, ALU.logical_shift_left)
            v.drain()
            v.tensor_scalar(w_unscale, w_unscale, 1.0 / XS, None, ALU.mult)
            v.drain().then_inc(S["wscale_ok"], 1)
            dve.wait_ge(S["whi_ok"], 1)
            v.scalar_tensor_tensor(w_inL, ps[:, 7, :], w_scale[:, 0:1], w_inH, ALU.mult, ALU.subtract)
            v.scalar_tensor_tensor(b_lo[0:1, :], b_row[0:1, :], w_scale[0:1, 0:1], b_hi[0:1, :], ALU.mult, ALU.subtract)
            v.drain().then_inc(S["b_ok"], 1)
            dve.wait_ge(S["std_ok"], 1)
            newton(v, rstd[0:NP, :], ve[0:NP, :], rtmp[0:NP, :])
            v.tensor_scalar(rstd[0:NP, :], rstd[0:NP, :], XS, None, ALU.mult)
            v.drain()

            def normalise(i, u):
                n = WIN * i + u
                v.tensor_scalar(x_n[u], x_all[:, bass.ds(n, 1), :].rearrange("p a f -> p (a f)"),
                                mv[0:NP, bass.ds(n, 1), 0], rstd[0:NP, bass.ds(n, 1)],
                                ALU.subtract, ALU.mult).then_inc(S["xn_ok"], 1)

            def transposed(i, u):
                n = WIN * i + u
                dve.wait_ge(S["xT_ok"], n + 1)
                v.tensor_tensor(xT_lo[RB[u]], ps[:, RB[u], 0:DK * 128].rearrange("k (b p) -> k b p", b=DK)[:, :, 0:NP],
                                xT_hi[RB[u]], ALU.subtract).then_inc(S["xlo_ok"], 1)

            def features(i, u):
                n = WIN * i + u
                dve.wait_ge(S["h_act"], n + 1)
                need(dve, h_out[RB[u]], 16 * uses(i, u, 0))
                hi = va[:, bass.ds(n, 1), 0:D].rearrange("p a f -> p (a f)")
                lo = va[:, bass.ds(n, 1), D:2 * D].rearrange("p a f -> p (a f)")
                v.tensor_scalar(h_s[RB[u]][0:NP, :], h_f[RB[u]][0:NP, :], scale[0:NP, 0:1], None, ALU.mult)
                v.scalar_tensor_tensor(lo, h_f[RB[u]][0:NP, :], scale[0:NP, 0:1], hi, ALU.mult, ALU.subtract)
                v.drain().then_inc(S["v_ready"], 1)

            def tile(i, u, has):
                if has(0):
                    normalise(i, u)
                if has(3):
                    transposed(i + (u - 3) // WIN, (u - 3) % WIN)
                if has(5):
                    features(i - 1, u)
            with_lag(dve, 5, tile)

            for r in range(NR):
                dve.wait_ge(gathered[r], 16)
            gs, gd = g_edges[:, :, :, 0], g_edges[:, :, :, 1]
            dve.wait_ge(S["iotas"], 2)
            v.tensor_scalar(e_q, gs, 1.0 / T, 0.5 / T - 0.5, ALU.mult, ALU.add)
            for r in range(NR):
                v.tensor_scalar(e_d[:, r, :], gd[:, r, :], float(T), win_base[0:NP, r:r + 1], ALU.mult, ALU.subtract)
            v.drain()
            v.tensor_scalar(e_b, e_q, ROUND, ROUND, ALU.add, ALU.subtract)
            v.drain()
            v.scalar_tensor_tensor(e_q, e_b, -float(T), gs, ALU.mult, ALU.add)
            v.drain()
            v.tensor_tensor(e_q, e_q, e_d, ALU.add)
            v.drain().then_inc(S["keys_ok"], 1)
            for r in range(NR):
                for k in range(SL):
                    dve.wait_ge(S["keyT_ps"], r * SL + k + 1)
                    tb = ps[0:NP, 2 * (k % 2), 0:NP].rearrange("e (i j) -> e i j", j=WIN)
                    tq = ps[0:NP, 2 * (k % 2) + 1, 0:NP].rearrange("e (i j) -> e i j", j=WIN)
                    v.tensor_copy(key_b[:, r, :, k, :], tb)
                    v.tensor_scalar(key_q[:, r, :, k, :], tq, -1.0, float(Q), ALU.max, ALU.min).then_inc(S["keyT_ok"], 1)
            v.drain()
            kb = key_b.rearrange("e r i k j -> e (r i) (k j)")
            kq = key_q.rearrange("e r i k j -> e (r i) (k j)")

            def one_hots(r, i, u):
                bt = T * r + WIN * i + u
                dve.wait_ge(S["win_ps"], bt + 1)
                v.tensor_tensor(oh_b[RB[u]], iota_x, kb[:, bass.ds(bt, 1), :].broadcast_to([NP, NP, C]), ALU.is_equal)
                v.tensor_tensor(oh_q[RB[u]], iota_x, kq[:, bass.ds(bt, 1), :].broadcast_to([NP, NP, C]),
                                ALU.is_equal).then_inc(S["oh_ready"], 1)

            def result(n0, s, i, u, bank, hi, lo):
                t = WIN * i + u
                n = n0 + t
                dve.wait_ge(S["hi_ok"], n + 1)
                v.scalar_tensor_tensor(v_f[0:NP, :], ps[0:NP, bank, D:2 * D], cinv[0:NP, s, bass.ds(t, 1)], t_hi[0:NP, :],
                                       ALU.mult, ALU.add).then_inc(S["psum_read"], 1)
                v.drain()
                if u % 2 == 0:
                    dve.wait_ge(h_in[0], 16 * (3 * (s * NB + i) + u // 2 + 1))
                else:
                    dve.wait_ge(h_in[1], 16 * (2 * (s * NB + i) + u // 2 + 1))
                v.tensor_tensor(v_f[0:NP, :], v_f[0:NP, :], h_ring[0:NP, u % 2, :], ALU.add).then_inc(S["h_used"], 1)
                v.drain()
                v.tensor_copy(hi, v_f[0:NP, :])
                v.drain()
                v.tensor_tensor(lo, v_f[0:NP, :], hi, ALU.subtract).then_inc(S["v_ready"], 1)
                v.drain()

            with dve.Fori(0, NB) as i:
                for u in range(WIN):
                    one_hots(0, i, u)
            dve.wait_ge(S["deg_ok"], 1)
            v.tensor_reduce(deg[0:NP, :].rearrange("p (r d) -> p r d", d=WIN), dl_eq, AX.X, ALU.add)
            v.drain()
            v.tensor_scalar(degc[0:NP, :], deg[0:NP, :], 1.0, None, ALU.max)
            v.tensor_reduce(in_windows[0:NP, :], deg[0:NP, :], AX.X, ALU.add)
            v.drain()
            v.reciprocal(degc[0:NP, :], degc[0:NP, :])
            v.drain()
            for s in range(STEPS):
                v.tensor_scalar(cinv[0:NP, s, :], degc[0:NP, :], 1.0 / (STEPS - s), None, ALU.mult)
            v.drain().then_inc(S["cover_sum"], 1)
            dve.sem_inc(S["psum_read"], 5)
            dve.sem_inc(S["h_used"], 2)

            def early(i, u):
                need(dve, early_out[RB[u]], 16 * uses(i, u, 0))
                result(0, 0, i, u, early_bank(u), v_early[RB[u]][:, 0:D], v_early[RB[u]][:, D:2 * D])

            def group(r):
                for w in range(WIN):
                    for u in range(WIN):
                        one_hots(r, w, u)
                        if u == 2 and not (isinstance(r, int) and r == 1 and w == 0):
                            early(r - 1 + (w - 1) // WIN, (w - 1) % WIN)
            group(1)
            with dve.Fori(2, NR) as r:
                group(r)
            early(NR - 2, WIN - 1)
            def step(n0, s, dest, t0, t1):
                def tiles(i):
                    for u in range(WIN):
                        t = WIN * i + u
                        result(n0, s, i, u, u, dest[:, bass.ds(t, 1), 0:D].rearrange("p a f -> p (a f)"),
                               dest[:, bass.ds(t, 1), D:2 * D].rearrange("p a f -> p (a f)"))
                loop(dve, t0 // WIN, t1 // WIN, tiles)
            dve.wait_ge(S["cover_ps"], 1)
            v.tensor_scalar(covered[:, :], ps[0:1, 7, 0:1], float(E), None, ALU.is_equal)
            v.drain().then_inc(S["cover_ok"], 1)
            for r, per in enumerate((2, 2, 1)):
                dve.wait_ge(early_out[r], 16 * per * (EARLY // WIN))
            step(0, 0, vb, EARLY, T)
            for s in range(1, STEPS - 1):
                step(s * T, s, vb if s % 2 == 0 else va, 0, T)
            fast = dve.value_load(covered[:, :], min_val=0, max_val=1)
            with dve.If(fast == 0):
                dve.wait_ge(S["e_const"], 1)
                dve.wait_ge(S["e_in"], 48)
                v.tensor_copy(dst_e, dst_i)
                v.drain()
                with dve.Fori(0, STEPS) as s:
                    for part, (t0, count) in enumerate(PARTS):
                        with dve.Fori(0, EC // EU) as i:
                            for u in range(EU):
                                dve.wait_ge(S["e_mm"], s * (2 * EC) + i * EU + (part * EC + u + 1))
                                v.tensor_scalar(oh_e[u][:, 0:count, :], node[:, t0:t0 + count, :], dst_e[:, bass.ds(i * EU + u, 1)], None,
                                                ALU.is_equal).then_inc(S["e_oh"], 1)
                        dve.wait_ge(S["e_acc"], 2 * s + (part + 1))
                        dve.wait_ge(S["e_rows"], s * 16 + 16)
                        v.tensor_scalar(deg_e[:, t0:t0 + count], ps[0:NP, 7, 0:count], 1.0, None, ALU.max)
                        v.drain()
                        v.reciprocal(deg_e[:, t0:t0 + count], deg_e[:, t0:t0 + count])
                        v.drain()
                        v.tensor_scalar(deg_e[:, t0:t0 + count], deg_e[:, t0:t0 + count], k_inv[:, bass.ds(s, 1)], None, ALU.mult)
                        v.drain()
                        for t in range(count):
                            v.scalar_tensor_tensor(term_e[:, t0 + t, :], ps[0:NP, t // 2, t % 2 * D:(t % 2 + 1) * D],
                                                   deg_e[:, t0 + t:t0 + t + 1], h_e[:, t0 + t, :], ALU.mult, ALU.add)
                        v.drain().then_inc(S["e_read"], 1)
                    dve.sem_inc(S["e_term"], 1)
                dve.wait_ge(S["e_rows"], 16 * (STEPS + 2))
                v.memset(adj[:, :], 0.0)
                v.memset(v_b[:, :], 0.0)
                v.memset(cinv[:, STEPS - 1, :], 0.0)
                v.drain()
            v.drain().then_inc(S["term_ok"], 1)
            def pow2(scale_out, inv_out, square, pi, pj):
                v.tensor_scalar(pi, square.bitcast(I32), 24, None, ALU.logical_shift_right)
                v.drain()
                v.tensor_scalar(pj, pi, -1.0, 203.0, ALU.mult, ALU.add)
                v.tensor_scalar(pi, pi, 51.0, None, ALU.add)
                v.drain()
                v.tensor_scalar(scale_out.bitcast(I32), pj, 23, None, ALU.logical_shift_left)
                v.tensor_scalar(inv_out.bitcast(I32), pi, 23, None, ALU.logical_shift_left)
                v.drain()

            dve.wait_ge(S["f_const"], 96)
            v.tensor_reduce(gb_max[:, 0:1], ga_bc, AX.X, ALU.max, apply_absolute_value=True)
            v.tensor_reduce(gb_max[:, 1:2], be_bc, AX.X, ALU.max, apply_absolute_value=True)
            v.drain()
            v.tensor_tensor(gb_sq, gb_max, gb_max, ALU.mult)
            v.drain()
            v.tensor_scalar(xn_sq[:, 0:1], gb_sq[:, 0:1], float(D), gb_sq[:, 1:2], ALU.mult, ALU.add)
            v.tensor_tensor(xn_sq[:, 1:2], gb_sq[:, 0:1], gb_sq[:, 1:2], ALU.add)
            v.drain()
            v.tensor_scalar(xn_sq[:, 0:1], xn_sq[:, 0:1], 2.0, None, ALU.mult)
            v.tensor_scalar(xn_sq[:, 1:2], xn_sq[:, 1:2], 2.0 * D, None, ALU.mult)
            v.drain()
            pow2(xs_scale[:, 0:1], xs_scale[:, 1:2], xn_sq[:, 0:1], pow_i[:, 0:1], pow_j[:, 0:1])

            def root(k, i):
                v.drain().then_inc(S["ve_ok"], 1)
                dve.wait_ge(S["sd_ok"], 2 * i + k - 1)
                newton(v, sd2, ve2, rt2)

            def body(i, u, has):
                m = 5 * i + u
                n = LAST + m
                if u == 2 and has(7):
                    gv = mv2[:, bass.ds(5 * (i - 1), WIN), 1]
                    v.tensor_scalar(ve2, gv, 1e-5, None, ALU.add)
                    root(0, i)
                    v.tensor_copy(r1, sd2)
                    v.tensor_tensor(ve2, sd2, sd2, ALU.mult)
                    v.drain()
                    v.tensor_tensor(ve2, ve2, gv, ALU.mult)
                    v.drain()
                    v.tensor_scalar(ve2, ve2, 1e-5, None, ALU.add)
                    root(1, i)
                    v.tensor_tensor(rr[:, bass.ds(5 * (i - 1), WIN)], r1, sd2, ALU.mult)
                    v.drain()
                if has(7):
                    w = m - 7
                    v.drain()
                    need(dve, S["xnT_ps"], w - 1)
                    need(dve, S["xhi_ok"], w - 1)
                    v.tensor_scalar(xn2[ring(7, u)], x1[:, bass.ds(w, 1), :].rearrange("p a f -> p (a f)"),
                                    mv2[:, bass.ds(w, 1), 0], rr[:, bass.ds(w, 1)], ALU.subtract, ALU.mult)
                    v.drain()
                    v.tensor_tensor(xn2[ring(7, u)], xn2[ring(7, u)], ga_bc[0:NP, :], ALU.mult).then_inc(S["z_ok"], 1)
                if has(0):
                    dve.wait_ge(S["hi_ok"], n + 1)
                    v.scalar_tensor_tensor(v_f[0:NP, :], ps[0:NP, RB[u], D:2 * D], cinv[0:NP, STEPS - 1, bass.ds(m, 1)], t_hi[0:NP, :],
                                           ALU.mult, ALU.add).then_inc(S["psum_read"], 1)
                    v.drain()
                    if u % 2 == 0:
                        dve.wait_ge(h_in[0], 16 * (3 * ((STEPS - 1) * NB + i) + u // 2 + 1))
                    else:
                        dve.wait_ge(h_in[1], 16 * (2 * ((STEPS - 1) * NB + i) + u // 2 + 1))
                    need(dve, S["vT_ps"], m - 1)
                    v.tensor_tensor(vfin[RB[u]], v_f[0:NP, :], h_ring[0:NP, u % 2, :], ALU.add).then_inc(S["h_used"], 1)
                    v.drain().then_inc(S["vfin_ok"], 1)
                if has(2):
                    xt = x1[:, bass.ds(m - 2, 1), :].rearrange("p a f -> p (a f)")
                    dve.wait_ge(S["y_ps"], m - 1)
                    dve.wait_ge(S["xb_ok"], m - 1)
                    v.scalar_tensor_tensor(xt, ps[0:NP, 5, 0:D], scale[0:NP, 1:2], x_i[ring(2, u)], ALU.mult, ALU.add).then_inc(S["x1_ok"], 1)
                    v.drain()
                    v.bn_stats(stats2, xt)
                    v.drain()
                    v.bn_aggr(mv_t, stats2)
                    v.drain()
                    v.tensor_copy(mv2[:, bass.ds(m - 2, 1), :].rearrange("p a f -> p (a f)"), mv_t)
                    v.drain()
                if has(8):
                    w = m - 8
                    dve.wait_ge(S["lg_ps"], w + 1)
                    v.tensor_tensor(lg[:, bass.ds(w, 1), :].rearrange("p a e -> p (a e)"), ps[0:NP, 6, 0:NE], br_bc[0:NP, :],
                                    ALU.add).then_inc(S["lg_ok"], 1)
                    dve.wait_ge(S["xhi_ok"], w + 1)
                    xs = xs_r[ring(8, u)]
                    v.scalar_tensor_tensor(xs[:, D:2 * D], xn2[ring(8, u)], xs_scale[0:NP, 0:1], xs[:, 0:D],
                                           ALU.mult, ALU.subtract).then_inc(S["xs_ok"], 1)
            last_step(dve, body)
            v.drain()
            bte = [NP, T, NE]
            e8 = iota_e8[:, None, :].broadcast_to(bte)
            v.tensor_reduce(m1, lg, AX.X, ALU.max)
            v.drain()

            def one_hot(out_, logits, m):
                v.tensor_tensor(tmp1, logits, m[:, :, None].broadcast_to(bte), ALU.is_equal)
                v.drain()
                v.tensor_tensor(tmp1, tmp1, e8, ALU.mult)
                v.drain()
                v.tensor_reduce(n1, tmp1, AX.X, ALU.min)
                v.drain()
                v.tensor_tensor(out_, e8, n1[:, :, None].broadcast_to(bte), ALU.is_equal)
                v.drain()
            one_hot(oh1, lg, m1)
            v.scalar_tensor_tensor(tmp2, oh1, -3e38, lg, ALU.mult, ALU.add)
            v.drain()
            v.tensor_reduce(m2, tmp2, AX.X, ALU.max)
            v.drain()
            one_hot(oh2, tmp2, m2)
            v.tensor_tensor(m2, m2, m1, ALU.subtract)
            v.drain().then_inc(S["ex_in"], 1)
            v.tensor_tensor(both, oh1, oh2, ALU.add)
            v.drain()
            v.tensor_reduce(per_p, both.rearrange("p t e -> p e t"), AX.X, ALU.add).then_inc(S["cnt_in"], 1)
            src_, d = both, 1
            bufs = [sum_a, sum_b]
            while d < T:
                dst_ = bufs[0]
                v.tensor_tensor(dst_[:, d:T, :], src_[:, d:T, :], src_[:, 0:T - d, :], ALU.add)
                v.tensor_copy(dst_[:, 0:d, :], src_[:, 0:d, :])
                v.drain()
                src_, d = dst_, 2 * d
                bufs = bufs[::-1]
            v.tensor_tensor(pos, src_, both, ALU.subtract)
            dve.wait_ge(S["ex_ok"], 1)
            v.tensor_scalar(den, ex2, 1.0, None, ALU.add)
            v.drain()
            v.reciprocal(w_top1, den)
            v.drain()
            v.tensor_tensor(w_top2, ex2, w_top1, ALU.mult)
            dve.wait_ge(S["cnt_ok"], 1)
            v.tensor_scalar(totals, ps[:, 7, 8:8 + NE], 127.0, 1.0 / 128, ALU.add, ALU.mult)
            v.drain()
            v.tensor_scalar(totals, totals, 1.0 / 256 - 0.5, None, ALU.add)
            v.drain()
            v.tensor_scalar(tiles_a, totals, ROUND, ROUND, ALU.add, ALU.subtract)
            v.drain()
            src_, d = tiles_a, 1
            bufs = [tiles_b, tiles_c]
            while d < NE:
                dst_ = bufs[0]
                v.tensor_tensor(dst_[:, d:NE], src_[:, d:NE], src_[:, 0:NE - d], ALU.add)
                v.tensor_copy(dst_[:, 0:d], src_[:, 0:d])
                v.drain()
                src_, d = dst_, 2 * d
                bufs = bufs[::-1]
            ends = src_
            v.tensor_tensor(totals, ends, tiles_a, ALU.subtract)
            v.drain()
            v.scalar_tensor_tensor(slot_base, totals[0:NP, :], 128.0, ps[0:NP, 7, 0:NE], ALU.mult, ALU.add)
            v.drain()
            v.tensor_tensor(pos, pos, slot_base[:, None, :].broadcast_to(bte), ALU.add)
            v.drain()
            for k, (oh, slot) in enumerate(((oh1, slot1), (oh2, slot2))):
                v.tensor_tensor(tmp1, oh, pos, ALU.mult)
                v.drain()
                v.tensor_reduce(s_all[:, k * T:(k + 1) * T], tmp1, AX.X, ALU.add)
                v.drain()
            v.tensor_scalar(s_tile, s_all, 1.0 / 128, 1.0 / 256 - 0.5, ALU.mult, ALU.add)
            v.drain()
            v.tensor_scalar(s_tile, s_tile, ROUND, ROUND, ALU.add, ALU.subtract)
            v.drain()
            v.scalar_tensor_tensor(s_pin, s_tile, -128.0, s_all, ALU.mult, ALU.add)
            v.tensor_tensor(le_tiles, tile_row[:, :, None].broadcast_to([128, FT, NE]),
                            ends[:, None, :].broadcast_to([128, FT, NE]), ALU.is_ge)
            v.drain()
            v.tensor_reduce(empty, le_tiles, AX.X, ALU.add)
            v.drain()
            v.memset(exp_of[:, 0:LEAD], 0)
            v.tensor_scalar(exp_of[:, LEAD:], empty, float(NE - 1), None, ALU.min)
            for c in range(T * TOP):
                v.tensor_scalar(oh_pos[:, c, :], iota_pos, s_pin[:, c:c + 1], None, ALU.is_equal)
                v.tensor_scalar(planes[:, c, 0:FT], iota_tile, s_tile[:, c:c + 1], p_plus1[0:NP, :], ALU.is_equal, ALU.mult)
                v.tensor_scalar(planes[:, c, FT:PL], iota_tile, s_tile[:, c:c + 1], float(c), ALU.is_equal, ALU.mult)
            v.drain().then_inc(S["rt_done"], 1)
            dve.wait_ge(w1_in, 16 * DK)
            v.tensor_reduce(w_max[:, 0:NE * DK].rearrange("p (e b) -> p e b", e=NE),
                            w_f32.rearrange("p e (b h) -> p e b h", b=DK), AX.X, ALU.max, apply_absolute_value=True)
            v.drain()
            v.tensor_tensor(w_sq2[:, 0:NE * DK], w_max[:, 0:NE * DK], w_max[:, 0:NE * DK], ALU.mult)
            dve.wait_ge(S["b1T_ok"], 1)
            v.tensor_tensor(w_sq2[:, NE * DK:NE * (DK + HK)], b1T, b1T, ALU.mult)
            v.drain().then_inc(S["w_sq_ok"], 1)
            dve.wait_ge(S["w_sum_ps"], 1)
            v.tensor_reduce(w_sums[:, 0, :], ps[:, 5, 0:NE * DK].rearrange("p (e b) -> p e b", e=NE), AX.X, ALU.add)
            v.tensor_reduce(w_sums[:, 2, :], ps[:, 5, NE * DK:NE * (DK + HK)].rearrange("p (e b) -> p e b", e=NE), AX.X, ALU.add)
            v.drain()
            pow2(s1, i1, w_sums[:, 0, :], pow_i, pow_j)
            v.tensor_scalar(g1, i1, xs_scale[:, 1:2], None, ALU.mult).then_inc(S["wsc_ok"], 1)
            v.scalar_tensor_tensor(w_sums[:, 2, :], w_sums[:, 0, :], xn_sq[:, 1:2], w_sums[:, 2, :], ALU.mult, ALU.add)
            v.drain()
            v.tensor_scalar(w_sums[:, 2, :], w_sums[:, 2, :], 2.0, None, ALU.mult)
            v.drain()
            pow2(sh, ih, w_sums[:, 2, :], pow_i, pow_j)
            for e in range(NE):
                dve.wait_ge(S["w1_hi"], e + 1)
                v.scalar_tensor_tensor(w1l[:, e, :], w_f32[:, e, :], s1[:, e:e + 1], w1h[:, e, :], ALU.mult, ALU.subtract).then_inc(S["w1_lo"], 1)
            for e in range(NE):
                dve.wait_ge(w2_in[e], 16)
                v.tensor_reduce(w_max[:, NE * DK + e * HK:NE * DK + (e + 1) * HK],
                                w_f32[:, e, :].rearrange("p (b d) -> p b d", b=HK), AX.X, ALU.max, apply_absolute_value=True)
            v.drain()
            v.tensor_tensor(w_sq2[:, 0:NE * HK], w_max[:, NE * DK:], w_max[:, NE * DK:], ALU.mult)
            v.drain().then_inc(S["w_sq_ok"], 1)
            dve.wait_ge(S["w_sum_ps"], 2)
            v.tensor_reduce(w_sums[:, 1, :], ps[:, 5, 0:NE * HK].rearrange("p (e b) -> p e b", e=NE), AX.X, ALU.add)
            v.drain()
            pow2(s2, i2, w_sums[:, 1, :], pow_i, pow_j)
            v.tensor_tensor(g2, ih, i2, ALU.mult).then_inc(S["wsc_ok"], 1)
            for e in range(NE):
                dve.wait_ge(S["w2_hi"], e + 1)
                v.scalar_tensor_tensor(w2l[:, e, :], w_f32[:, e, :], s2[:, e:e + 1], w2h[:, e, :], ALU.mult, ALU.subtract).then_inc(S["w2_lo"], 1)
            dve.wait_ge(S["tok_ps"], 1)
            v.tensor_scalar(tok_p, ps[:, 0, 0:FT], -1.0, float(T), ALU.add, ALU.mult)
            v.tensor_scalar(empty, ps[:, 0, 0:FT], 0.0, 4.0 * TOP * N, ALU.is_equal, ALU.mult)
            v.tensor_copy(tok_b, ps[:, 0, FT:PL])
            v.drain()
            v.tensor_tensor(tok_p, tok_p, tok_b, ALU.add)
            v.tensor_scalar(tok_b, tok_b, float(T), None, ALU.is_ge)
            v.drain()
            v.scalar_tensor_tensor(tok_p, tok_b, -float(T), tok_p, ALU.mult, ALU.add)
            v.drain()
            v.scalar_tensor_tensor(dest, tok_b, float(N), tok_p, ALU.mult, ALU.add)
            v.tensor_scalar(idx_g, tok_p, 0.0, None, ALU.max)
            v.drain()
            v.tensor_tensor(dest, dest, empty, ALU.add)
            v.drain()
            v.tensor_copy(idx_s, dest)
            v.drain().then_inc(S["idx_ok"], 1)
            dve.sem_inc(S["wsc_ok"], 1)

            def transposed(i, u):
                j = FU * i + u
                r = u % 2
                dve.wait_ge(S["xg_T"], j + 1)
                need(dve, S["ffn_h"], j - 1)
                v.tensor_copy(xT16[r], ps[:, r, :].bitcast(F16)[:, 0:2 * D].rearrange("k (b s) -> k b s", b=2 * DK)).then_inc(S["xgT_ok"], 1)

            def hidden(i, u, e):
                j = FU * i + u
                r = u % 2
                dve.wait_ge(S["gelu_ok"], j + 1)
                need(dve, S["ffn_y"], j - FR + 1)
                hh, hl = h_hi[u % FR].rearrange("h b s -> h (b s)"), h_lo[u % FR].rearrange("h b s -> h (b s)")
                v.tensor_scalar(hh, h_g[r], sh[:, bass.ds(e, 1)], None, ALU.mult)
                v.drain()
                v.scalar_tensor_tensor(hl, h_g[r], sh[:, bass.ds(e, 1)], hh, ALU.mult, ALU.subtract).then_inc(S["hs_ok"], 1)

            def result(i, u, e):
                j = FU * i + u
                r = u % 2
                dve.wait_ge(S["ffn_y"], j + 1)
                need(dve, y_out[u % FR], 16 * (FU // FR * i + u // FR))
                v.scalar_tensor_tensor(y_sb[u % FR], ps[:, 4 + r, 0:D], g2[:, bass.ds(e, 1)], b2_bc[:, bass.ds(e, 1), :].rearrange("p a f -> p (a f)"),
                                       ALU.mult, ALU.add).then_inc(S["y_ok"], 1)
            ffn_tiles(dve, FT, FU, LEAD, experts, transposed, hidden, result)
            for i in range(NB):
                dve.wait_ge(yc_in[i % 2], 32 * (i // 2 + 1))
                for k, wk in enumerate((w_top1, w_top2)):
                    v.drain()
                    for t in range(WIN):
                        n = i * WIN + t
                        last = v.scalar_tensor_tensor(x1[:, n, :], y_in[i % 2][k][:, t, :], wk[:, n:n + 1], x1[:, n, :], ALU.mult, ALU.add)
                v.drain().then_inc(S["comb_ok"], 1)

        @block.tensor
        def _(pe):
            te = nc.tensor
            pe.wait_ge(S["iotas"], 1)
            count = ps[0:NP, 6, 0:NR]
            te.matmul(count, ones16[0:NP, 0:NP], ones16[0:NP, 256:256 + NR], start=True, stop=False)
            for j in range(COARSE):
                pe.wait_ge(S["above_ok"], j + 1)
                for r in range(NR):
                    last = te.matmul(count[:, r:r + 1], above[:, j, :].rearrange("p (g r) -> p g r", r=NR)[:, :, r],
                                     ones16[0:NP, 0:1], start=False, stop=(j == COARSE - 1 and r == NR - 1))
            last.then_inc(S["count_ok"], 1)
            pe.wait_ge(S["ident_ok"], 1)
            pe.wait_ge(S["w_in_in"], 48)
            for kb in range(DK):
                for ob in range(DK):
                    last = te.transpose(ps[:, 7, (kb * DK + ob) * 128:(kb * DK + ob + 1) * 128],
                                        w_raw[:, ob, kb * 128:(kb + 1) * 128], ident)
            last.then_inc(S["wT_ps"], 1)
            pe.wait_ge(S["b_ok"], 1)

            def transposed(i, u):
                n = WIN * i + u
                pe.wait_ge(S["xn_ok"], n + 1)
                need(pe, S["xlo_ok"], n - AGE[u] + 1)
                for b in range(DK):
                    last = te.transpose(ps[:, RB[u], b * 128:b * 128 + NP], x_n[u][:, b * 128:(b + 1) * 128], ident[0:NP, 0:NP])
                last.then_inc(S["xT_ps"], 1)

            def features(i, u):
                n = WIN * i + u
                pe.wait_ge(S["xlo_ok"], n + 1)
                need(pe, S["h_act"], n - AGE[u] + 1)
                bank = ps[0:NP, 3 + RB[u], 0:D]
                te.matmul(bank, ones16[0:1, 128:128 + NP], b_hi[0:1, :], start=True, stop=False)
                te.matmul(bank, ones16[0:1, 128:128 + NP], b_lo[0:1, :], start=False, stop=False)
                for part, (xp, w) in enumerate(((xT_hi, w_inH), (xT_hi, w_inL), (xT_lo, w_inH))):
                    for b in range(DK):
                        last = te.matmul(bank, xp[RB[u]][:, b, :], w[:, b * D:(b + 1) * D],
                                         start=False, stop=(part == 2 and b == DK - 1))
                last.then_inc(S["h_ps"], 1)
            feature_tiles(pe, transposed, features)
            pe.wait_ge(S["h_act"], T)
            pe.wait_ge(S["keys_ok"], 1)
            for r in range(NR):
                for k in range(SL):
                    n = r * SL + k
                    if n >= 2:
                        pe.wait_ge(S["keyT_ok"], n - 1)
                    te.transpose(ps[0:NP, 2 * (k % 2), 0:NP], e_b[:, r, k * NP:(k + 1) * NP], ident[0:NP, 0:NP])
                    te.transpose(ps[0:NP, 2 * (k % 2) + 1, 0:NP], e_q[:, r, k * NP:(k + 1) * NP],
                                 ident[0:NP, 0:NP]).then_inc(S["keyT_ps"], 1)
            pe.wait_ge(S["keyT_ok"], NR * SL)
            pe.sem_inc(S["win_ps"], 2)

            def windows(r, i, u):
                bt = T * r + WIN * i + u
                pe.wait_ge(S["oh_ready"], bt + 1)
                need(pe, S["win_out"], bt - 1)
                cells = win_cells(RB[u])
                for j in range(WIN):
                    for k in range(SL):
                        last = te.matmul(cells[:, j * 128:j * 128 + Q], oh_b[RB[u]][:, :, k * WIN + j], oh_q[RB[u]][:, :, k * WIN + j],
                                         start=(k == 0), stop=(k == SL - 1))
                last.then_inc(S["win_ps"], 1)

            def windows_only(i):
                for u in range(WIN):
                    windows(0, i, u)
            windows_only(0)
            with pe.Fori(1, NB) as i:
                windows_only(i)
            pe.wait_ge(S["v_ready"], T)

            def group(r):
                for w in range(WIN):
                    n = WIN * (r - 1) + w
                    for u in range(WIN):
                        windows(r, w, u)
                        parts = (0, 0, 0, 8, 16, T) if w == 0 else (0, 5, 10, 15, 20, T)
                        if parts[u] == 0 and parts[u + 1] > 0:
                            if w == 0:
                                pe.wait_ge(S["win_out"], T * r)
                            pe.wait_ge(S["psum_read"], n + 5 if w == 0 else n + 4)
                        for a in range(parts[u], parts[u + 1]):
                            last = te.matmul(ps[0:NP, early_bank(w), :], adj_t[:, bass.ds(n, 1), a, :].rearrange("b t p -> b (t p)"),
                                             va[:, a, :], start=(a == 0), stop=(a == T - 1))
                    last.then_inc(S["tile_ps"], 1)
            group(1)
            with pe.Fori(2, NR) as r:
                group(r)
            pe.wait_ge(S["cover_sum"], 1)
            te.matmul(ps[0:1, 7, 0:1], in_windows[0:NP, :], ones_col[0:NP, :], start=True, stop=True).then_inc(S["cover_ps"], 1)
            pe.wait_ge(S["win_out"], NR * T)

            def step(n0, s, source, t0, t1):
                def tiles(i):
                    for u in range(WIN):
                        t = WIN * i + u
                        n = n0 + t
                        pe.wait_ge(S["psum_read"], n + 1)
                        pe.wait_ge(S["v_ready"], T * (s + 1) - 1)
                        for a in range(T):
                            if a == T - 1:
                                pe.wait_ge(S["v_ready"], T * (s + 1))
                            last = te.matmul(ps[0:NP, u, :], adj_t[:, bass.ds(t, 1), a, :].rearrange("b t p -> b (t p)"),
                                             source[:, a, :], start=(a == 0), stop=(a == T - 1))
                        last.then_inc(S["tile_ps"], 1)
                loop(pe, t0 // WIN, t1 // WIN, tiles)
            step(0, 0, va, EARLY, T)
            pe.wait_ge(S["early_back"], 16)
            for s in range(1, STEPS - 1):
                step(s * T, s, va if s % 2 == 0 else vb, 0, T)
            pe.wait_ge(S["cover_ok"], 1)
            fast = pe.value_load(covered[:, :], min_val=0, max_val=1)
            with pe.If(fast == 0):
                pe.wait_ge(S["psum_read"], LAST + 5)
                pe.wait_ge(S["e_const"], 1)
                pe.sem_inc(S["e_mm"], EU)
                pe.sem_inc(S["e_read"], 1)
                with pe.Fori(0, STEPS) as s:
                    for part, (t0, count) in enumerate(PARTS):
                        banks = [(b, min(512, count * D - b * 512)) for b in range((count + 1) // 2)] + [(7, count)]
                        pe.wait_ge(S["e_read"], 2 * s + (part + 1))
                        for b, n in banks:
                            te.matmul(ps[0:NP, b, 0:n], zeros_e[:, 0:NP], zeros_e[:, 0:n], start=True, stop=False)
                        with pe.Fori(0, EC // EU) as i:
                            for u in range(EU):
                                pe.wait_ge(S["e_oh"], s * (2 * EC) + i * EU + (part * EC + u + 1))
                                pe.wait_ge(e_gathered[u], s * (32 * EC // EU) + i * 16 + (part * 16 * EC // EU + 16))
                                for t in range(count):
                                    te.matmul(ps[0:NP, t // 2, t % 2 * D:(t % 2 + 1) * D], oh_e[u][:, t, :], rows_e[u], start=False, stop=False)
                                    last = te.matmul(ps[0:NP, 7, t:t + 1], oh_e[u][:, t, :], ones_e, start=False, stop=False)
                                last.then_inc(S["e_mm"], 1)
                        for b, n in banks:
                            last = te.matmul(ps[0:NP, b, 0:n], zeros_e[:, 0:NP], zeros_e[:, 0:n], start=False, stop=True)
                        last.then_inc(S["e_acc"], 1)
            pe.wait_ge(S["term_ok"], 1)
            pe.wait_ge(S["f_const"], 96)
            pe.wait_ge(S["pool_const"], 1)
            pe.wait_ge(S["psum_read"], LAST + 5)
            for kb in range(DK):
                for ob in range(DK):
                    last = te.transpose(ps[:, 7, (kb * DK + ob) * 128:(kb * DK + ob + 1) * 128],
                                        w_oraw[:, ob, kb * 128:(kb + 1) * 128], ident2)
            last.then_inc(S["w_oT_ps"], 1)
            pe.wait_ge(S["v_ready"], T * STEPS)

            def body(i, u, has):
                m = 5 * i + u
                n = LAST + m
                if has(0):
                    pe.wait_ge(S["psum_read"], n + 4)
                    for a in range(T):
                        last = te.matmul(ps[0:NP, RB[u], :], adj_t[:, bass.ds(m, 1), a, :].rearrange("b t p -> b (t p)"),
                                         vb[:, a, :], start=(a == 0), stop=(a == T - 1))
                    last.then_inc(S["tile_ps"], 1)
                if has(7):
                    pe.wait_ge(S["xn2_ok"], m - 6)
                    need(pe, S["xnT_ok"], m - 7)
                    for b in range(DK):
                        last = te.transpose(ps[:, 4, b * 128:b * 128 + NP], xn2[ring(7, u)][:, b * 128:(b + 1) * 128], ident2[0:NP, 0:NP])
                    last.then_inc(S["xnT_ps"], 1)
                if has(8):
                    pe.wait_ge(S["xnT_ok"], m - 7)
                    need(pe, S["lg_ok"], m - 8)
                    for b in range(DK):
                        last = te.matmul(ps[0:NP, 6, 0:NE], xnT[:, b, :], wr_sb[:, b, :], start=(b == 0), stop=(b == DK - 1))
                    last.then_inc(S["lg_ps"], 1)
                if has(2):
                    pe.wait_ge(S["vT_ok"], m - 1)
                    if isinstance(i, int) and m == 2:
                        pe.wait_ge(S["w_oT_ok"], 1)
                    need(pe, S["x1_ok"], m - 2)
                    for b in range(DK):
                        last = te.matmul(ps[0:NP, 5, 0:D], vT[:, b, :], w_outT[:, b, :], start=(b == 0), stop=(b == DK - 1))
                    last.then_inc(S["y_ps"], 1)
                if has(1):
                    pe.wait_ge(S["vfin_ok"], m)
                    need(pe, S["vT_ok"], m - 1)
                    for b in range(DK):
                        last = te.transpose(ps[:, 3, b * 128:b * 128 + NP], vfin[ring(1, u)][:, b * 128:(b + 1) * 128], ident2[0:NP, 0:NP])
                    last.then_inc(S["vT_ps"], 1)
            last_step(pe, body)
            pe.wait_ge(S["b1_in"], 32)
            pe.wait_ge(S["x1_ok"], T)
            te.transpose(ps[:, 5, 0:NE * HK], b1_rows, ident2[0:NE * HK, 0:NE * HK]).then_inc(S["b1T_ps"], 1)
            pe.wait_ge(S["cnt_in"], 1)
            te.matmul(ps[0:NP, 7, 0:NE], tri, per_p, start=True, stop=True)
            te.matmul(ps[:, 7, 8:8 + NE], ones2[0:NP, :], per_p, start=True, stop=True).then_inc(S["cnt_ok"], 1)
            pe.wait_ge(S["rt_done"], 1)
            for c in range(T * TOP):
                last = te.matmul(ps[:, 0, 0:PL], oh_pos[:, c, :], planes[:, c, :], start=(c == 0), stop=(c == T * TOP - 1))
            last.then_inc(S["tok_ps"], 1)
            pe.wait_ge(S["w_sq_ok"], 1)
            te.matmul(ps[:, 5, 0:NE * (DK + HK)], ones2, w_sq2[:, 0:NE * (DK + HK)], start=True, stop=True).then_inc(S["w_sum_ps"], 1)
            pe.wait_ge(S["w_sq_ok"], 2)
            te.matmul(ps[:, 5, 0:NE * HK], ones2, w_sq2[:, 0:NE * HK], start=True, stop=True).then_inc(S["w_sum_ps"], 1)
            pe.wait_ge(S["idx_ok"], 1)
            pe.wait_ge(S["w2_lo"], NE)

            def transposed(i, u):
                j = FU * i + u
                r = u % 2
                pe.wait_ge(g_in[u], 16 * (i + 1))
                need(pe, S["xgT_ok"], j - 1)
                for b in range(2 * DK):
                    last = te.transpose(ps[:, r, :].bitcast(F16)[:, b * 128:(b + 1) * 128], x_g[u][:, b * 128:(b + 1) * 128], ident16)
                last.then_inc(S["xg_T"], 1)

            def hidden(i, u, e):
                j = FU * i + u
                r = u % 2
                pe.wait_ge(S["xgT_ok"], j + 1)
                need(pe, S["gelu_ok"], j - 1)
                for b in range(HK):
                    for n, (w, part) in enumerate(((w1h, 0), (w1h, 1), (w1l, 0))):
                        for k in range(DK):
                            at = k * H + b * 128
                            last = te.matmul(ps[:, 2 + r, b * 128:(b + 1) * 128],
                                             w[:, bass.ds(e, 1), at:at + 128].rearrange("k a h -> k (a h)"),
                                             xT16[r][:, part * DK + k, :], start=(n == 0 and k == 0), stop=(n == 2 and k == DK - 1))
                last.then_inc(S["ffn_h"], 1)

            def result(i, u, e):
                j = FU * i + u
                r = u % 2
                pe.wait_ge(S["hs_ok"], j + 1)
                need(pe, S["y_ok"], j - 1)
                for b in range(HK):
                    for n, (hp, w) in enumerate(((h_hi, w2h), (h_hi, w2l), (h_lo, w2h))):
                        last = te.matmul(ps[:, 4 + r, 0:D], hp[u % FR][:, b, :],
                                         w[:, bass.ds(e, 1), b * D:(b + 1) * D].rearrange("h a d -> h (a d)"),
                                         start=(b == 0 and n == 0), stop=(b == HK - 1 and n == 2))
                last.then_inc(S["ffn_y"], 1)
            ffn_tiles(pe, FT, FU, LEAD, experts, transposed, hidden, result)


def ffn_tiles(eng, count, unroll, lead, experts, transposed, hidden, result):
    groups = count // unroll

    def group(i, first, last):
        es = experts(i, eng)
        for u in range(unroll):
            if not (last and u == unroll - 1):
                transposed(i + (u + 1) // unroll, (u + 1) % unroll)
            hidden(i, u, es[lead + u])
            if not (first and u < 2):
                result(i + (u - 2) // unroll, (u - 2) % unroll, es[lead + u - 2])
        if last:
            for u in (unroll - 2, unroll - 1):
                result(i, u, es[lead + u])

    transposed(0, 0)
    group(0, True, False)
    with eng.Fori(1, groups - 1) as i:
        group(i, False, False)
    group(groups - 1, False, True)


def newton(v, r, var, tmp):
    v.reciprocal(r, r)
    v.drain()
    v.tensor_tensor(tmp, r, r, ALU.mult)
    v.drain()
    v.tensor_tensor(tmp, tmp, var, ALU.mult)
    v.drain()
    v.tensor_scalar(tmp, tmp, -0.5, 1.5, ALU.mult, ALU.add)
    v.drain()
    v.tensor_tensor(r, r, tmp, ALU.mult)
    v.drain()


_INS = ["x", "src", "dst", "L0_gnn_W_in", "L0_gnn_b_in", "L0_gnn_W_out", "L0_gnn_b_out", "L0_ffn_gamma", "L0_ffn_beta",
        "L0_ffn_Wr", "L0_ffn_br", "L0_ffn_W1", "L0_ffn_b1", "L0_ffn_W2", "L0_ffn_b2"]


def kernel(**inputs):
    import numpy as np
    import concourse.bacc as bacc
    from concourse.bass_utils import run_bass_kernel_spmd

    nc = bacc.Bacc("TRN2", target_bir_lowering=False, num_devices=1)
    arrays, args = {}, []
    for name in _INS:
        a = np.ascontiguousarray(inputs[name])
        arrays[name] = a
        args.append(nc.dram_tensor(name, a.shape, mybir.dt.from_np(a.dtype), kind="ExternalInput").ap())
    out = nc.dram_tensor("out", inputs["x"].shape, F32, kind="ExternalOutput").ap()
    gnn_ffn(nc, *args, out)
    return run_bass_kernel_spmd(nc, [arrays], core_ids=[0]).results[0]["out"]
```

```python
from contextlib import ExitStack

import concourse.bass as bass
from concourse import mybir

F32 = mybir.dt.float32
F16 = mybir.dt.float16
I32 = mybir.dt.int32
I16 = mybir.dt.int16
ALU = mybir.AluOpType
ACT = mybir.ActivationFunctionType
AX = mybir.AxisListType

ROUND = 1.5 * 2.0**23


def gnn_ffn(nc, x, src, dst, W_in, b_in, W_out, b_out, gamma, beta, Wr, br, W1, b1, W2, b2, out):
    N, D = x.shape
    E = src.shape[0]
    NP = 125
    T = N // NP
    DK = D // 128
    WIN = 5
    NR = T // WIN
    Q = WIN * T
    SL = 2
    SLOTS = SL * NP
    GRAN = 25
    ROWS = (E - SLOTS) // GRAN + 1
    COARSE = E // GRAN // NP
    STEPS = 6
    XS = 2.0**11
    C = WIN * SL
    NB = T // WIN
    EARLY = T - WIN
    EC = E // NP
    TAIL = SLOTS - GRAN
    assert N < 2**15 and EC % GRAN == 0
    assert N == NP * T and E % (GRAN * NP) == 0 and (E - SLOTS) % GRAN == 0

    NE, _, H = W1.shape
    HK = H // 128
    TOP = 2
    WP = H // 128
    assert DK * H == WP * D and STEPS - 2 == NE // 2 and WP <= WIN and NE // 2 < WIN
    FT = (TOP * N + NE * 127) // 128
    CB = 10
    assert T * TOP % CB == 0
    FU = 8
    FR = 4
    EARLY_AT = 2
    XR = 4
    LAG = 3
    LEAD = 4
    assert FT % FU == 0

    EU = 5
    PARTS = ((0, (T + 1) // 2), ((T + 1) // 2, T // 2))
    assert EC % EU == 0 and PARTS[0][1] * D <= 7 * 512
    term_dram = nc.dram_tensor("term_dram", (N, D), F32, kind="Internal").ap()
    xs_dram = nc.dram_tensor("xs_dram", (N, 2 * D), F16, kind="Internal").ap()
    y_dram = nc.dram_tensor("y_dram", (TOP * N, D), F32, kind="Internal").ap()
    xs_v = xs_dram.rearrange("(p t) f -> p t f", t=T)
    y_v = y_dram.rearrange("(k p t) f -> k p t f", k=TOP, t=T)
    out_v = out.rearrange("(p t) f -> p t f", t=T)
    edge_rows = nc.dram_tensor("edge_rows", (ROWS, 2 * SLOTS), I16, kind="Internal").ap()
    early_dram = nc.dram_tensor("early_dram", (N, 2 * D), F16, kind="Internal").ap()
    h_dram = nc.dram_tensor("h_dram", (N, D), F32, kind="Internal").ap()
    x_v = x.rearrange("(p t) f -> p t f", t=T)
    h_v = h_dram.rearrange("(p t) f -> p t f", t=T)
    early_v = early_dram.rearrange("(p t) f -> p t f", t=T)
    term_v = term_dram.rearrange("(p t) f -> p t f", t=T)

    with ExitStack() as ctx:
        def sb(name, shape, dt):
            return ctx.enter_context(nc.sbuf_tensor(name, shape, dt))

        def sem(name):
            return ctx.enter_context(nc.semaphore(name))

        ADJ = T * T * NP
        REG = 3126
        adj = sb("adj", [128, T * REG], F16)
        v_a = sb("v_a", [128, T * 2 * D], F16)
        v_b = sb("v_b", [128, T * 2 * D], F16)
        ps = ctx.enter_context(nc.psum_tensor("ps", [128, 8, 512], F32))

        def over(buf, at, n, dt, parts=128):
            size = 4 if dt in (F32, I32) else 2
            assert at % size == 0
            v = buf[0:parts, at // 2:at // 2 + n * size // 2]
            return v if dt == F16 else v.bitcast(dt)

        def of_tile(flat, i, u, at, n):
            dt, size = flat.dtype, 2 if flat.dtype == F16 else 4
            tiles = flat.bitcast(mybir.dt.uint8).rearrange("p (i u b) -> p i u b", i=T // WIN, u=WIN)
            group = bass.ds(i, 1) if not isinstance(i, int) else slice(i, i + 1)
            return tiles[:, group, u, at * size:(at + n) * size].rearrange("p a b -> p (a b)").bitcast(dt)

        adj_w = adj[0:NP, 0:ADJ].rearrange("b (r q p) -> b r q p", r=NR, q=Q)
        va = v_a[0:NP, :].rearrange("p (t f) -> p t f", t=T)
        vb = v_b[0:NP, :].rearrange("p (t f) -> p t f", t=T)

        cinv = sb("cinv", [128, STEPS, T], F32)
        h_ring = sb("h_ring", [128, 2, D], F32)
        t_hi = sb("t_hi", [128, D], F32)
        w_piece = sb("w_piece", [128, D], F32)
        w_max = sb("w_max", [128, 2 * NE * WP], F32)
        scale = sb("scale", [128, 2], F32)

        in_windows = sb("in_windows", [128, 1], F32)
        ones_col = sb("ones_col", [128, 1], F32)
        covered = sb("covered", [1, 1], I32)

        at = (T - WIN) * T * NP * 2
        x_flat = over(adj, at, T * D, F32, NP)
        x_all = x_flat.rearrange("p (t f) -> p t f", t=T)
        at = 0
        def take(n, dt, parts=128):
            nonlocal at
            v = over(adj, at, n, dt, parts)
            at += (n * (4 if dt in (F32, I32) else 2) + 3) // 4 * 4
            return v

        src_i = take(EC + TAIL, I32, NP)
        dst_i32 = take(EC + TAIL, I32, NP)
        edges = take((EC + TAIL) * 2, F16, NP).bitcast(I16).rearrange("p (e k) -> p e k", k=2)
        w_raw = take(DK * D, F32).rearrange("o (b k) -> o b k", b=DK)
        w_sq = take(DK * D, F32).rearrange("o (b k) -> o b k", b=DK)
        x_n = [take(D, F32, NP) for _ in range(WIN)]
        assert at <= WIN * T * NP * 2
        at = (WIN * T * NP * 2 + 3) // 4 * 4
        above = take(COARSE * N // WIN, F16, NP).rearrange("p (j g) -> p j g", j=COARSE)
        iota_g = take(N // WIN, F16)
        key = take(COARSE, F32)
        key_t = take(COARSE, F32)
        ones16 = take(256 + 8, F16)
        starts = take(NR, F32)
        start_row = take(NR, I32)
        g_edges = take(NR * 2 * SLOTS, F16, NP).bitcast(I16).rearrange("p (r s k) -> p r s k", r=NR, k=2)
        e_b = take(NR * SLOTS, F16, NP).rearrange("p (r s) -> p r s", r=NR)
        e_k = take(NR * SLOTS, F16, NP).rearrange("p (r s) -> p r s", r=NR)
        e_q = take(NR * SLOTS, F32, NP).rearrange("p (r s) -> p r s", r=NR)
        e_d = take(NR * SLOTS, F32, NP).rearrange("p (r s) -> p r s", r=NR)
        win_base = take(NR, F32)
        dl_eq = take(T * SLOTS, F16, NP).rearrange("p (r d s) -> p r d s", r=NR, d=WIN)
        deg = take(T, F32)
        degc = take(T, F32)
        iota_row = take(128, F32)
        iota_col = take(1, F32)
        ident = take(128, F32)
        ident_16 = take(128, F16)
        w_inH = take(DK * D, F16)
        w_inL = take(DK * D, F16)
        b_row = take(D, F32)
        b_hi = take(D, F16)
        b_lo = take(D, F16)
        b_col = take(DK, F32)
        b_abs = take(DK, F32)
        b_sq = take(DK, F32)
        bound = take(DK, F32)
        bmax = take(2, F32)
        ball = take(2, F32)
        w_scale = take(1, F32)
        w_unscale = take(1, F32)
        exp_i = take(1, I32)
        exp_j = take(2, I32)
        exp_w = take(3, I32)
        stats = take(T * 6, F32).rearrange("p (t s) -> p t s", s=6)
        mv_flat = take(T * 2, F32)
        mv = mv_flat.rearrange("p (t s) -> p t s", s=2)
        rstd = take(T, F32)
        rtmp = take(T, F32)
        ve = take(T, F32)
        xT_hi = [take(DK * NP, F16).rearrange("k (b p) -> k b p", b=DK) for _ in range(3)]
        xT_lo = [take(DK * NP, F16).rearrange("k (b p) -> k b p", b=DK) for _ in range(3)]
        h_f = [take(D, F32) for _ in range(WIN)]
        assert at <= (T - WIN) * T * NP * 2, at

        at = 0

        def take_b(n, dt):
            nonlocal at
            v = over(v_b, at, n, dt, NP)
            at += n * 2
            return v

        iota_x = take_b(NP * C, F16).rearrange("e (x c) -> e x c", c=C)
        key_b = take_b(NP * C, F16).rearrange("e (r i k j) -> e r i k j", r=NR, k=SL, j=WIN)
        key_q = take_b(NP * C, F16).rearrange("e (r i k j) -> e r i k j", r=NR, k=SL, j=WIN)
        oh_b = [take_b(NP * C, F16).rearrange("e (x c) -> e x c", c=C) for _ in range(3)]
        oh_q = [take_b(NP * C, F16).rearrange("e (x c) -> e x c", c=C) for _ in range(3)]
        v_early = [take_b(2 * D, F16) for _ in range(3)]
        assert at <= T * 2 * D * 2

        x1 = adj[0:NP, :].bitcast(F32).rearrange("p (t r) -> p t r", t=T)[:, :, 0:D]
        XW = 2 * D
        EW = DK * H
        assert EW == HK * D and XW + 2 * EW + 2 * D <= REG
        ex8 = adj[:, :].bitcast(mybir.dt.uint8).rearrange("p (t r) -> p t r", t=T)
        ex16 = adj[:, :].rearrange("p (t r) -> p t r", t=T)
        ex32 = adj[:, :].bitcast(F32).rearrange("p (t r) -> p t r", t=T)
        PARTS_W = ((0, 1), (2, 4))
        PART_RAW = (4, 3)

        def w_part(part, low):
            return ex16[:, part, XW + low * EW:XW + (low + 1) * EW].rearrange("p a w -> p (a w)")

        def w_block(part, low, at, n):
            at = 2 * (XW + low * EW + at)
            return ex8[:, bass.ds(part, 1), at:at + 2 * n].rearrange("p a w -> p (a w)").bitcast(F16)

        def w_raw32(part):
            return ex32[:, part, XW // 2:XW // 2 + EW].rearrange("p a w -> p (a w)")

        def b2_part(part):
            at = XW // 2 + EW
            return ex32[:, part, at:at + D].rearrange("p a w -> p (a w)")

        def taker(buf):
            used = [0]

            def take(n, dt, parts=128):
                v = over(buf, used[0], n, dt, parts)
                used[0] += (n * (4 if dt in (F32, I32) else 2) + 3) // 4 * 4
                assert used[0] <= (T * REG * 2 if buf is adj else T * 2 * D * 2), used
                return v
            return take

        fa = taker(v_a)
        ident2 = fa(128, F32)
        ident16 = fa(128, F16)
        ones2 = fa(128, F32)
        w_outT = fa(DK * D, F32).rearrange("k (b o) -> k b o", b=DK)
        bo_bc, ga_bc, be_bc = fa(D, F32), fa(D, F32), fa(D, F32)
        wr_sb = fa(DK * NE, F32).rearrange("k (b e) -> k b e", b=DK)
        br_bc = fa(NE, F32)
        lg = fa(T * NE, F32, NP).rearrange("p (t e) -> p t e", t=T)
        stats2 = fa(6, F32, NP)
        mv_t = fa(2, F32, NP)
        mv2 = fa(2 * T, F32, NP).rearrange("p (t s) -> p t s", s=2)
        ve2, sd2, rt2 = (fa(WIN, F32, NP) for _ in range(3))
        rr = fa(T, F32, NP)
        gb_max = fa(2, F32)
        gb_sq = fa(2, F32)
        xn_sq = fa(2, F32)
        xs_scale = fa(2, F32)
        pow_i = fa(NE, I32)
        pow_j = fa(NE, I32)
        sw, iw = fa(2 * NE, F32), fa(2 * NE, F32)
        sh, ih, g1, g2 = (fa(NE, F32) for _ in range(4))
        w_top, w_all = fa(2 * NE, F32), fa(2 * NE, F32)
        b1T = fa(NE * HK, F32)
        b1_top, b1_all = fa(NE, F32), fa(NE, F32)
        pow_w, pow_v = fa(2 * NE, I32), fa(2 * NE, I32)
        tri = fa(NP, F32, NP)
        iota_e8 = fa(NE, F32, NP)
        tile_row = fa(FT, F32)
        p_plus1 = fa(1, F32)
        w_top1, w_top2 = fa(T, F32, NP), fa(T, F32, NP)
        idx_g, idx_s = fa(FT, I32), fa(FT, I32)
        exp_of, part1_of, part2_of = (over(adj, ((T - 1) * REG + XW) * 2 + 4 * D * FR + n * 4 * (FT + LEAD), FT + LEAD, I32)
                                      for n in range(3))
        vfin = [fa(D, F32, NP) for _ in range(3)]
        vT = fa(DK * NP, F32).rearrange("k (b p) -> k b p", b=DK)
        x_i = [fa(D, F32, NP) for _ in range(3)]
        xn2 = [fa(D, F32, NP) for _ in range(3)]
        xnT = fa(DK * NP, F32).rearrange("k (b p) -> k b p", b=DK)
        xs_f = fa(3 * 2 * D, F16)
        xs_r = [xs_f[0:NP, j * 2 * D:(j + 1) * 2 * D] for j in range(3)]
        w_oraw = xs_f[:, 0:2 * DK * D].bitcast(F32).rearrange("o (b k) -> o b k", b=DK)
        fb = taker(v_b)
        oh_pos = fb(T * TOP * 128, F16, NP).rearrange("p (n x c) -> p n x c", x=128, c=CB)
        oh1, oh2, tmp1, tmp2, both, sum_a, sum_b, pos = (fb(T * NE, F32, NP).rearrange("p (t e) -> p t e", t=T) for _ in range(8))
        per_p = fb(NE, F32, NP)
        totals, tiles_a, tiles_b, tiles_c = (fb(NE, F32) for _ in range(4))
        slot_base = fb(NE, F32, NP)
        s_all, s_tile, s_pin = (fb(T * TOP, F32, NP) for _ in range(3))
        tok_p, tok_b, dest, empty, expert = (fb(FT, F32) for _ in range(5))
        le_tiles = fb(FT * NE, F32).rearrange("p (j e) -> p j e", e=NE)
        assert XW + 128 * CB <= REG and NE // 2 * 5 < T - 1
        iota_xc = over(adj, ((T - 2) * REG + XW) * 2, 128 * CB, F16, NP).rearrange("p (x c) -> p x c", c=CB)
        pin16, tile16, chunk16 = (fb(T * TOP, F16, NP).rearrange("p (n c) -> p n c", c=CB) for _ in range(3))
        m1, m2, n1, ex2, den = (fb(T, F32, NP) for _ in range(5))
        PL = 2 * FT
        planes = over(v_a, T * 2 * D * 2 - T * TOP * PL * 2, T * TOP * PL, F16, NP).rearrange("p (n y c) -> p n y c", y=PL, c=CB)
        fc = taker(v_b)
        x_g = [fc(2 * D, F16) for _ in range(FU)]
        ig = [fc(1, I32) for _ in range(FU)]
        isc = [fc(1, I32) for _ in range(FR)]
        xT16 = [fc(2 * D, F16).rearrange("k (b s) -> k b s", b=2 * DK) for _ in range(XR)]
        h_g = [fc(H, F32) for _ in range(2)]
        h_hi = [fc(H, F16).rearrange("h (b s) -> h b s", b=HK) for _ in range(FR)]
        h_lo = [fc(H, F16).rearrange("h (b s) -> h b s", b=HK) for _ in range(FR)]
        at_y = ((T - 1) * REG + XW) * 2
        y_sb = [over(adj, at_y + r * D * 4, D, F32) for r in range(FR)]
        assert XW + 2 * WIN * D <= REG
        y_in = [[over(adj, ((TOP * i + k) * REG + XW) * 2, WIN * D, F32, NP).rearrange("p (t f) -> p t f", t=WIN) for k in range(TOP)]
                for i in range(NB)]

        fe = taker(adj)
        src_e, dst_i = fe(EC, I32, NP), fe(EC, I32, NP)
        dst_e = fe(EC, F32, NP)
        node = fe(N, F32, NP).rearrange("e (t p) -> e t p", t=T)
        oh_e = [fe(PARTS[0][1] * NP, F32, NP).rearrange("e (t p) -> e t p", p=NP) for _ in range(EU)]
        rows_e = [fe(D, F32, NP) for _ in range(EU)]
        src_col = [fe(1, I32, NP) for _ in range(EU)]
        ones_e, zeros_e = fe(1, F32, NP), fe(512, F32, 1)
        k_inv = fe(STEPS, F32, NP)
        deg_e = fe(T, F32, NP)
        term_e = fe(T * D, F32, NP).rearrange("p (t f) -> p t f", t=T)
        h_e = fe(T * D, F32, NP).rearrange("p (t f) -> p t f", t=T)

        names = """rows_made src_in dst_in edges_ok w_in_in iotas ident_ok above_ok count_ok start_ok deg_ok wscale_ok whi_ok
            xlo_ok b_ok early_back early_hi gathered digits_ok keys_ok keyT_ps keyT_q stats_ok std_ok wT_ps bound_ok ball_ok xn_ok xT_ps xT_ok h_ps
            h_act v_ready oh_ready win_ps win_out tile_ps hi_ok psum_read h_used f_const pool_const bo_mat w_oT_ps w_oT_ok
            vfin_ok vT_ps vT_ok y_ps xb_ok x1_ok ve_ok sd_ok z_ok xn2_ok xnT_ps xnT_ok lg_ps lg_ok xhi_ok xs_ok piece_in piece_used
            w_out_in b2_in w_top_ok w_all_ok w_hi w_lo wsc_ok ex_in ex_ok cnt_in cnt_ok rt_const rt_by_c rt_done tables_ok tok_ps idx_ok
            pool_turn cover_sum cover_ps cover_ok term_ok e_const e_in e_col e_oh e_mm e_acc e_read e_term e_rows ig_ok
            is_ok xg_T xgT_ok ffn_h gelu_ok hs_ok ffn_y y_ok y2_ok comb_ok""".split()
        S = {n: sem(n) for n in names}
        h_in = [sem(f"h_in{r}") for r in range(2)]
        h_out = [sem(f"h_out{r}") for r in range(3)]
        x_in = [sem(f"x_in{i}") for i in range(NB)]
        early_out = [sem(f"early_out{r}") for r in range(3)]
        xs_out = [sem(f"xs_out{r}") for r in range(3)]
        xi_in = [sem(f"xi_in{r}") for r in range(3)]
        w_raw_in = [sem(f"w_raw_in{layer}") for layer in range(2)]
        g_in = [sem(f"g_in{r}") for r in range(FU)]
        y_out = [sem(f"y_out{r}") for r in range(FR)]
        yc_in = [[sem(f"y{k}_in{i}") for i in range(NB)] for k in range(TOP)]
        out_sem = sem("out_sem")
        e_gathered = [sem(f"e_gathered{r}") for r in range(EU)]

        block = ctx.enter_context(nc.Block())
        RB = [0, 1, 2, 0, 1]
        AGE = [2, 2, 5, 3, 3]
        PRIOR = [(2, 0), (2, 0), (1, 0), (2, 1), (2, 1)]
        LAST = (STEPS - 1) * T

        def ring(d, u):
            return RB[(u - d) % WIN]

        def uses(i, u, d):
            w = (u - d) % WIN
            group = i + (u - d - w) // WIN
            return PRIOR[w][0] * group + PRIOR[w][1]

        def need(eng, s, value):
            if not (isinstance(value, int) and value <= 0):
                eng.wait_ge(s, value)

        def loaded(table, most):
            def load(i, eng, first, count):
                _, values = nc.values_load_multi_w_load_instructions(
                    table[0:1, bass.ds(FU * i + (LEAD + first), count)], engines=[eng.engine], min_val=0, max_val=most,
                    skip_runtime_bounds_check_because="a minimum with it made the table")
                return values
            return load
        experts = loaded(exp_of, NE - 1)
        parts1, parts2 = loaded(part1_of, T - 1), loaded(part2_of, T - 1)

        def has_unit(i, u):
            return u > 0 and (not isinstance(i, int) or 1 <= i <= NE // 2)

        def win_cells(slot):
            return ps[0:NP, 2 * slot:2 * slot + 2, :].rearrange("b k c -> b (k c)")[:, 0:WIN * 128]

        def key_block(r, which):
            in_bank = 8 // SL
            at = r % in_bank * SL * 128
            return ps[0:NP, which * 3 + r // in_bank, :].bitcast(F16)[:, at:at + SL * 128].rearrange("e (k p) -> e k p", k=SL)

        def keys_T(r, which):
            return key_block(r, which)[:, :, 0:NP].rearrange("e k (i j) -> e k i j", j=WIN)

        def early_bank(w):
            return 6 + w % WIN % 2

        def with_lag(eng, lag, body):
            def group(i):
                for u in range(WIN if i is not NB else lag):
                    body(i, u, lambda d: not isinstance(i, int) or 0 <= WIN * i + u - d < T)
            group(0)
            with eng.Fori(1, NB) as i:
                group(i)
            group(NB)

        def feature_tiles(eng, transposed, features):
            def tile(i, u, has):
                if has(0):
                    transposed(i, u)
                if has(2):
                    features(i + (u - 2) // WIN, (u - 2) % WIN)
            with_lag(eng, 2, tile)

        def loop(eng, first, end, body):
            if end - first == 1:
                body(first)
            else:
                with eng.Fori(first, end) as i:
                    body(i)

        def step_groups(eng, s, t0, t1, tiles):
            first, end = t0 // WIN, t1 // WIN
            if s > 0:
                loop(eng, first, NE // 2, lambda i: tiles(i, True))
                first = NE // 2
            loop(eng, first, end, lambda i: tiles(i, False))

        def early_step(eng, body):
            def group(i):
                for u in range(WIN):
                    body(i, u, lambda d: not isinstance(i, int) or 0 <= WIN * i + u - d < EARLY)
            group(0)
            with eng.Fori(1, EARLY // WIN) as i:
                group(i)
            group(EARLY // WIN)

        def last_step(eng, body):
            def peeled(i):
                for u in range(WIN):
                    body(i, u, lambda d: 0 <= WIN * i + u - d < T)
            peeled(0)
            peeled(1)
            with eng.Fori(2, NB) as i:
                for u in range(WIN):
                    body(i, u, lambda d: True)
            peeled(NB)
            peeled(NB + 1)

        @block.sync
        def _(sp):
            for a, on_chip, s in ((dst, dst_i32, "dst_in"), (src, src_i, "src_in")):
                sp.dma_start(on_chip[0:NP - 1, :], bass.AP(a.tensor, 0, [[EC, NP - 1], [1, EC + TAIL]])).then_inc(S[s], 16)
                sp.dma_start(on_chip[NP - 1:NP, 0:EC], bass.AP(a.tensor, (NP - 1) * EC, [[EC, 1], [1, EC]])).then_inc(S[s], 16)
            sp.wait_ge(S["edges_ok"], 1)
            whole = (NP - 1) * COARSE
            flat = edges.rearrange("p e k -> p (e k)")

            def rows(parts, count):
                v = flat[parts, 0:2 * SLOTS]
                return bass.AP(v.tensor, v.offset, [list(v.ap[0]), [2 * GRAN, count], [1, 2 * SLOTS]])
            sp.dma_start(edge_rows[0:whole, :].rearrange("(p j) s -> p j s", j=COARSE),
                         rows(slice(0, NP - 1), COARSE)).then_inc(S["rows_made"], 16)
            sp.dma_start(edge_rows[whole:ROWS, :].rearrange("(p j) s -> p j s", p=1),
                         rows(slice(NP - 1, NP), ROWS - whole)).then_inc(S["rows_made"], 16)
            with sp.Fori(0, NB) as i:
                for u in range(WIN):
                    sp.wait_ge(S["h_act"], 5 * i + u + 1)
                    sp.dma_start(h_v[:, bass.ds(5 * i + u, 1), :].rearrange("p a f -> p (a f)"), h_f[u][0:NP, :]).then_inc(h_out[RB[u]], 16)
            for slot, per in enumerate((2, 2, 1)):
                sp.wait_ge(h_out[slot], 16 * per * NB)

            def step(s, t0, t1):
                def tiles(i, pieces):
                    for u in range(WIN):
                        n = s * T + WIN * i + u
                        if u == 0:
                            sp.wait_ge(S["h_used"], n + 2)
                        elif u > 1:
                            sp.wait_ge(S["h_used"], n + 1)
                        sp.dma_start(h_ring[0:NP, u % 2, :],
                                     h_v[:, bass.ds(WIN * i + u, 1), :].rearrange("p a f -> p (a f)")).then_inc(h_in[u % 2], 16)
                        if pieces and u < WP:
                            e = (s - 1) % 2 * NE // 2 + i
                            sp.wait_ge(S["piece_used"], (s - 1) * NE // 2 * WP + i * WP + (u + 1))
                            if s <= 2:
                                rows, cols = (u // 2) * 128, (u % 2) * D
                                piece = W1[bass.ds(e, 1), rows:rows + 128, cols:cols + D]
                            else:
                                piece = W2[bass.ds(e, 1), u * 128:(u + 1) * 128, :]
                            sp.dma_start(w_piece[:, :], piece.rearrange("a k h -> k (a h)")).then_inc(S["piece_in"], 16)
                step_groups(sp, s, t0, t1, tiles)

            def early(i, u, has):
                n = WIN * i + u
                if has(0):
                    if u == 0:
                        sp.wait_ge(S["h_used"], n + 2)
                    elif u > 1:
                        sp.wait_ge(S["h_used"], n + 1)
                    sp.dma_start(h_ring[0:NP, u % 2, :],
                                 h_v[:, bass.ds(n, 1), :].rearrange("p a f -> p (a f)")).then_inc(h_in[u % 2], 16)
                if has(2):
                    sp.wait_ge(S["v_ready"], T + n - 1)
                    sp.dma_start(early_v[:, bass.ds(n - 2, 1), :].rearrange("p a f -> p (a f)"),
                                 v_early[ring(2, u)]).then_inc(early_out[ring(2, u)], 16)
            early_step(sp, early)
            for r, per in enumerate((2, 2, 1)):
                sp.wait_ge(early_out[r], 16 * per * (EARLY // WIN))
            sp.wait_ge(S["win_ps"], NR * T + 2)
            sp.dma_start(vb[:, 0:EARLY, :], early_v[:, 0:EARLY, :]).then_inc(S["early_back"], 16)
            step(0, EARLY, T)
            for s in range(1, STEPS - 1):
                step(s, 0, T)
            sp.wait_ge(S["term_ok"], 1)

            def bc(v, n):
                return bass.AP(v.tensor, 0, [[0, 128], [1, n]])
            sp.dma_start(w_oraw, W_out.rearrange("(b o) k -> o b k", o=128)).then_inc(S["w_out_in"], 16)
            sp.dma_start(bo_bc, bc(b_out, D)).then_inc(S["f_const"], 16)
            sp.dma_start(ga_bc, bc(gamma, D)).then_inc(S["f_const"], 16)
            sp.dma_start(be_bc, bc(beta, D)).then_inc(S["f_const"], 16)
            sp.dma_start(wr_sb, Wr.rearrange("(b k) e -> k b e", k=128)).then_inc(S["f_const"], 16)
            sp.dma_start(br_bc, bc(br, NE)).then_inc(S["f_const"], 16)
            sp.dma_start(b1T, b1.rearrange("e (b h) -> h (e b)", h=128), allow_slow_non_contiguous=True).then_inc(S["f_const"], 16)

            def body(i, u, has):
                m = 5 * i + u
                n = LAST + m
                if has(0):
                    if u == 0:
                        sp.wait_ge(S["h_used"], n + 2)
                    elif u > 1:
                        sp.wait_ge(S["h_used"], n + 1)
                    sp.dma_start(h_ring[0:NP, u % 2, :],
                                 h_v[:, bass.ds(m, 1), :].rearrange("p a f -> p (a f)")).then_inc(h_in[u % 2], 16)
                if has(1):
                    need(sp, S["x1_ok"], m - 2)
                    sp.dma_start(x_i[ring(1, u)], x_v[:, bass.ds(m - 1, 1), :].rearrange("p a f -> p (a f)")).then_inc(xi_in[ring(1, u)], 16)
                if has(8):
                    sp.wait_ge(S["xs_ok"], m - 7)
                    sp.dma_start(xs_v[:, bass.ds(m - 8, 1), :].rearrange("p a f -> p (a f)"), xs_r[ring(8, u)]).then_inc(xs_out[ring(8, u)], 16)
            last_step(sp, body)
            for r in range(FR):
                sp.wait_ge(y_out[r], 16 * (FT // FR))
            for i in range(NB):
                sp.dma_start(y_in[i][0], y_v[0, :, i * WIN:(i + 1) * WIN, :]).then_inc(yc_in[0][i], 16)
            for i in range(NB):
                sp.wait_ge(S["comb_ok"], i + 1)
                sp.dma_start(out_v[:, i * WIN:(i + 1) * WIN, :], x1[:, i * WIN:(i + 1) * WIN, :]).then_inc(out_sem, 16)
            sp.wait_ge(out_sem, 16 * NB)

        @block.gpsimd
        def _(pool):
            g = nc.gpsimd
            g.iota(iota_g, [[1, N // WIN]], base=0, channel_multiplier=0, allow_small_or_imprecise_dtypes=True)
            g.iota(iota_row, [[1, 128]], base=0, channel_multiplier=0, allow_small_or_imprecise_dtypes=True)
            g.iota(iota_col, [[0, 1]], base=0, channel_multiplier=1, allow_small_or_imprecise_dtypes=True)
            g.memset(ones_col[:, :], 1.0)
            g.memset(ones16[:, 0:128], 1.0)
            g.memset(ones16[:, 256:264], 0.0)
            g.memset(ones16[:, 128:256], XS).then_inc(S["iotas"], 1)
            g.iota(win_base, [[T * WIN, NR]], base=0, channel_multiplier=T * T, allow_small_or_imprecise_dtypes=True)
            g.iota(iota_x, [[1, NP], [0, C]], base=0, channel_multiplier=0,
                   allow_small_or_imprecise_dtypes=True).then_inc(S["iotas"], 1)
            pool.wait_ge(S["bound_ok"], 1)
            g.partition_all_reduce(ball, bmax, 128, bass.bass_isa.ReduceOp.max).then_inc(S["ball_ok"], 1)
            pool.wait_ge(S["rows_made"], 32)
            pool.wait_ge(S["start_ok"], 1)
            for r in range(NR):
                g.indirect_dma_start(g_edges[:, r, :, :].rearrange("p s k -> p (s k)"), None, edge_rows,
                                     bass.IndirectOffsetOnAxis(ap=start_row[0:NP, r:r + 1], axis=0),
                                     ).then_inc(S["gathered"], 16)
            pool.wait_ge(S["gathered"], 16 * NR)
            pool.wait_ge(S["iotas"], 2)
            gs, gd = g_edges[:, :, :, 0], g_edges[:, :, :, 1]
            g.tensor_scalar(e_q, gs, 1.0 / T, 0.5 / T - 0.5, ALU.mult, ALU.add)
            for r in range(NR):
                g.tensor_scalar(e_d[:, r, :], gd[:, r, :], float(T), win_base[0:NP, r:r + 1], ALU.mult, ALU.subtract)
            g.drain()
            g.tensor_scalar(e_b, e_q, ROUND, ROUND, ALU.add, ALU.subtract)
            g.drain()
            g.tensor_scalar(e_q, gs, 1.0, None, ALU.mult)
            g.drain()
            g.tensor_tensor(e_q, e_d, e_q, ALU.add).then_inc(S["digits_ok"], 1)
            for d in range(WIN):
                last = g.tensor_scalar(dl_eq[:, :, d, :], e_d, float(T * d), None, ALU.is_equal)
            last.then_inc(S["deg_ok"], 1)
            pool.wait_ge(S["cover_ok"], 1)
            fast = pool.value_load(covered[:, :], min_val=0, max_val=1)
            with pool.If(fast == 0):
                pool.wait_ge(S["v_ready"], T * STEPS)
                for slot, per in enumerate((2, 2, 1)):
                    pool.wait_ge(h_out[slot], 16 * per * NB)
                g.dma_start(src_e, src.rearrange("(p e) -> p e", p=NP)).then_inc(S["e_in"], 16)
                g.dma_start(dst_i, dst.rearrange("(p e) -> p e", p=NP)).then_inc(S["e_in"], 16)
                g.dma_start(h_e, h_v).then_inc(S["e_in"], 16)
                g.dma_start(term_v, h_v).then_inc(S["e_rows"], 16)
                g.iota(node, [[1, T], [T, NP]], base=0, channel_multiplier=0, allow_small_or_imprecise_dtypes=True)
                g.memset(ones_e, 1.0)
                for s in range(STEPS):
                    g.memset(k_inv[:, s:s + 1], 1.0 / (STEPS - s))
                g.memset(zeros_e, 0.0).then_inc(S["e_const"], 1)
                pool.wait_ge(S["e_in"], 48)
                with pool.Fori(0, STEPS) as s:
                    pool.wait_ge(S["e_rows"], s * 16 + 16)
                    pool.sem_inc(S["pool_turn"], 1)
                    for part in range(2):
                        with pool.Fori(0, EC // EU) as i:
                            for u in range(EU):
                                n = s * (2 * EC) + i * EU + (part * EC + u)
                                pool.wait_ge(S["e_mm"], n + 1)
                                pool.sem_inc(S["pool_turn"], 1)
                                g.tensor_copy(src_col[u], src_e[:, bass.ds(i * EU + u, 1)]).then_inc(S["e_col"], 1)
                                pool.wait_ge(S["e_col"], n + 1)
                                pool.sem_inc(S["pool_turn"], 1)
                                g.indirect_dma_start(rows_e[u], None, term_dram,
                                                     bass.IndirectOffsetOnAxis(ap=src_col[u], axis=0)).then_inc(e_gathered[u], 16)
                    pool.wait_ge(S["e_term"], s + 1)
                    pool.sem_inc(S["pool_turn"], 1)
                    g.dma_start(term_v, term_e).then_inc(S["e_rows"], 16)
                pool.wait_ge(S["e_rows"], 16 * (STEPS + 1))
                g.dma_start(h_v, term_e).then_inc(S["e_rows"], 16)
            pool.wait_ge(S["term_ok"], 1)
            g.memset(ident2, 0.0)
            g.memset(ident16, 0.0)
            g.memset(ones2, 1.0)
            g.memset(tri, 1.0)
            g.iota(iota_e8, [[1, NE]], base=-NE, channel_multiplier=0, allow_small_or_imprecise_dtypes=True)
            g.iota(tile_row, [[1, FT]], base=0, channel_multiplier=0, allow_small_or_imprecise_dtypes=True)
            g.iota(p_plus1, [[0, 1]], base=1, channel_multiplier=1, allow_small_or_imprecise_dtypes=True).then_inc(S["bo_mat"], 1)
            pool.wait_ge(S["bo_mat"], 1)
            g.affine_select(out=ident2, in_=ident2, compare_op=ALU.not_equal, fill=1.0, base=0, pattern=[[-1, 128]], channel_multiplier=1)
            g.affine_select(out=ident16, in_=ident16, compare_op=ALU.not_equal, fill=1.0, base=0, pattern=[[-1, 128]], channel_multiplier=1)
            g.affine_select(out=tri, in_=tri, compare_op=ALU.is_gt, fill=0.0, base=0, pattern=[[1, NP]],
                            channel_multiplier=-1).then_inc(S["pool_const"], 1)
            pool.wait_ge(S["f_const"], 96)

            def body(i, u, has):
                m = 5 * i + u
                if has(7):
                    pool.wait_ge(S["z_ok"], m - 6)
                    g.tensor_tensor(xn2[ring(7, u)], xn2[ring(7, u)], be_bc[0:NP, :], ALU.add).then_inc(S["xn2_ok"], 1)
                if has(1):
                    pool.wait_ge(xi_in[ring(1, u)], 16 * (uses(i, u, 1) + 1))
                    g.tensor_tensor(x_i[ring(1, u)], x_i[ring(1, u)], bo_bc[0:NP, :], ALU.add).then_inc(S["xb_ok"], 1)
                if isinstance(i, int) and m == WIN - 1:
                    pool.wait_ge(S["w_top_ok"], 1)
                    g.partition_all_reduce(w_all, w_top, 128, bass.bass_isa.ReduceOp.max)
                    g.partition_all_reduce(b1_all, b1_top, 128, bass.bass_isa.ReduceOp.max).then_inc(S["w_all_ok"], 1)
            last_step(pool, body)
            pool.wait_ge(S["tile_ps"], LAST + T)
            g.iota(iota_xc, [[1, 128], [0, CB]], base=0, channel_multiplier=0, allow_small_or_imprecise_dtypes=True)
            g.iota(chunk16, [[CB, T * TOP // CB], [1, CB]], base=0, channel_multiplier=0,
                   allow_small_or_imprecise_dtypes=True).then_inc(S["rt_const"], 1)
            for r, per in enumerate((2, 2, 1)):
                pool.wait_ge(xs_out[r], 16 * per * NB)
            pool.wait_ge(S["idx_ok"], 1)

            def gather(i, u):
                j = FU * i + u
                need(pool, g_in[u], 16 * i)
                pool.sem_inc(S["pool_turn"], 1)
                g.tensor_copy(ig[u], idx_g[:, bass.ds(j, 1)]).then_inc(S["ig_ok"], 1)
                need(pool, S["xg_T"], j - FU + 1)
                pool.wait_ge(S["ig_ok"], j + 1)
                pool.sem_inc(S["pool_turn"], 1)
                g.indirect_dma_start(x_g[u], None, xs_dram, bass.IndirectOffsetOnAxis(ap=ig[u], axis=0)).then_inc(g_in[u], 16)

            def scatter(i, u):
                j = FU * i + u
                r = u % FR
                need(pool, y_out[r], 16 * (FU // FR * i + u // FR))
                pool.sem_inc(S["pool_turn"], 1)
                g.tensor_copy(isc[r], idx_s[:, bass.ds(j, 1)]).then_inc(S["is_ok"], 1)
                pool.wait_ge(S["y_ok"], j + 1)
                pool.wait_ge(S["is_ok"], j + 1)
                pool.sem_inc(S["pool_turn"], 1)
                g.indirect_dma_start(y_dram, bass.IndirectOffsetOnAxis(ap=isc[r], axis=0), y_sb[r], None,
                                     bounds_check=TOP * N - 1, oob_is_err=False).then_inc(y_out[r], 16)

            def tiles(i, last):
                for u in range(FU):
                    if not (last and u):
                        gather(i + (u + FU - 1) // FU, (u + FU - 1) % FU)
                    scatter(i, u)
            for u in range(FU - 1):
                gather(0, u)
            tiles(0, False)
            with pool.Fori(1, FT // FU - 1) as i:
                tiles(i, False)
            tiles(FT // FU - 1, True)

        @block.scalar
        def _(act):
            a = nc.scalar
            act.dma_start(w_raw, W_in.rearrange("(b o) k -> o b k", o=128)).then_inc(S["w_in_in"], 16)
            act.dma_start(b_row[0:1, :], b_in[None, :]).then_inc(S["w_in_in"], 16)
            act.dma_start(b_col, b_in.rearrange("(b o) -> o b", o=128), allow_slow_non_contiguous=True).then_inc(S["w_in_in"], 16)
            for i in range(NB):
                act.dma_start(x_all[:, i * WIN:(i + 1) * WIN, :], x_v[:, i * WIN:(i + 1) * WIN, :]).then_inc(x_in[i], 16)
            act.wait_ge(S["wT_ps"], 1)
            act.wait_ge(S["wscale_ok"], 1)
            a.activation(w_inH, ps[:, 7, :], ACT.Copy, scale=w_scale[:, 0:1])
            a.activation(b_hi[0:1, :], b_row[0:1, :], ACT.Copy, scale=w_scale[0:1, 0:1]).then_inc(S["whi_ok"], 1)
            act.wait_ge(S["stats_ok"], 1)
            a.activation(rstd[0:NP, :], ve[0:NP, :], ACT.Sqrt).then_inc(S["std_ok"], 1)

            def transposed(i, u):
                n = WIN * i + u
                act.wait_ge(S["xT_ps"], n + 1)
                need(act, S["h_ps"], n - AGE[u] + 1)
                a.activation(xT_hi[RB[u]], ps[:, RB[u], 0:DK * 128].rearrange("k (b p) -> k b p", b=DK)[:, :, 0:NP],
                             ACT.Copy).then_inc(S["xT_ok"], 1)

            def features(i, u):
                n = WIN * i + u
                act.wait_ge(S["h_ps"], n + 1)
                need(act, S["v_ready"], n - AGE[u] + 1)
                need(act, h_out[RB[u]], 16 * uses(i, u, 0))
                a.activation(h_f[u][0:NP, :], ps[0:NP, 3 + RB[u], 0:D], ACT.Silu, scale=w_unscale[0:NP, 0:1])
                a.drain()
                a.activation(of_tile(v_a[0:NP, :], i, u, 0, D), h_f[u][0:NP, :], ACT.Copy,
                             scale=scale[0:NP, 0:1]).then_inc(S["h_act"], 1)
            feature_tiles(act, transposed, features)
            act.wait_ge(S["keyT_ps"], 1)
            for r in range(NR):
                a.activation(key_q[:, r, :, :, :].rearrange("e i k j -> e k i j"), keys_T(r, 1), ACT.Copy).then_inc(S["keyT_q"], 1)

            def window(r, i, u):
                bt = T * r + WIN * i + u
                act.wait_ge(S["win_ps"], bt + 1 + 2)
                cells = win_cells(RB[u]).rearrange("b (c q) -> b c q", q=128)[:, :, 0:Q]
                row = bass.ds(r, 1) if not isinstance(r, int) else slice(r, r + 1)
                a.activation(adj_w[:, row, :, bass.ds(T * i + WIN * u, WIN)].rearrange("b o q p -> b (o q) p"),
                             cells.rearrange("b c q -> b q c"), ACT.Copy).then_inc(S["win_out"], 1)

            def high(n0, s, i, u, bank):
                n = n0 + WIN * i + u
                act.wait_ge(S["tile_ps"], n + 1)
                act.wait_ge(S["v_ready"], T + n)
                a.activation(t_hi[0:NP, :], ps[0:NP, bank, 0:D], ACT.Copy,
                             scale=cinv[0:NP, s, bass.ds(WIN * i + u, 1)]).then_inc(S["hi_ok"], 1)

            def early_high(i, u):
                act.wait_ge(S["h_used"], 2 + WIN * i + u + 1)
                a.activation(v_early[RB[u]][:, 0:D], t_hi[0:NP, :], ACT.Copy).then_inc(S["early_hi"], 1)
            with act.Fori(0, NB) as i:
                for u in range(WIN):
                    window(0, i, u)
            for slot, per in enumerate((2, 2, 1)):
                act.wait_ge(h_out[slot], 16 * per * NB)

            def group(r):
                for w in range(WIN):
                    has_early = not (isinstance(r, int) and r == 1 and w == 0)
                    if has_early:
                        high(0, 0, r - 1 + (w - 1) // WIN, (w - 1) % WIN, early_bank(w - 1))
                    for u in range(WIN):
                        window(r, w, u)
                        if has_early and u == EARLY_AT:
                            early_high(r - 1 + (w - 1) // WIN, (w - 1) % WIN)
            group(1)
            with act.Fori(2, NR) as r:
                group(r)
            high(0, 0, NR - 2, WIN - 1, early_bank(-1))
            early_high(NR - 2, WIN - 1)

            def step(n0, s, t0, t1):
                def tiles(i):
                    for u in range(WIN):
                        high(n0, s, i, u, u)
                loop(act, t0 // WIN, t1 // WIN, tiles)
            step(0, 0, EARLY, T)
            for s in range(1, STEPS - 1):
                step(s * T, s, 0, T)
            act.wait_ge(S["w_oT_ps"], 1)
            a.activation(w_outT, ps[:, 7, :].rearrange("k (b o) -> k b o", b=DK), ACT.Copy).then_inc(S["w_oT_ok"], 1)

            def body(i, u, has):
                m = 5 * i + u
                n = LAST + m
                if isinstance(i, int) and m == WIN:
                    act.wait_ge(S["wsc_ok"], 1)
                if has_unit(i, u):
                    e, layer = (u - 1) // 2, (u - 1) % 2
                    unit = WP * (i - 1) + u - 1
                    act.wait_ge(w_raw_in[layer], 16 * (2 * (i - 1) + e + 1))
                    if u == WP:
                        act.wait_ge(S["w_lo"], unit)
                    a.activation(w_part(bass.ds(WIN * i - WIN + PARTS_W[e][layer], 1), 0), w_raw32(bass.ds(WIN * i - WIN + PART_RAW[layer], 1)),
                                 ACT.Copy, scale=sw[:, bass.ds(layer * NE + 2 * i - 2 + e, 1)]).then_inc(S["w_hi"], 1)

                def v_T():
                    act.wait_ge(S["vT_ps"], m)
                    need(act, S["y_ps"], m - 1)
                    a.activation(vT, ps[:, 3, 0:DK * 128].rearrange("k (b p) -> k b p", b=DK)[:, :, 0:NP], ACT.Copy).then_inc(S["vT_ok"], 1)
                if not has(0) and has(1):
                    v_T()
                if u == 2 and has(7):
                    act.wait_ge(S["ve_ok"], i)
                    a.activation(sd2, ve2, ACT.Sqrt).then_inc(S["sd_ok"], 1)
                if has(7):
                    act.wait_ge(S["xn2_ok"], m - 6)
                    need(act, xs_out[ring(7, u)], 16 * uses(i, u, 7))
                    a.activation(xs_r[ring(7, u)][:, 0:D], xn2[ring(7, u)], ACT.Copy, scale=xs_scale[0:NP, 0:1]).then_inc(S["xhi_ok"], 1)
                if has(0):
                    act.wait_ge(S["tile_ps"], n + 1)
                    act.wait_ge(S["h_used"], n + 2)
                    a.activation(t_hi[0:NP, :], ps[0:NP, RB[u], 0:D], ACT.Copy,
                                 scale=cinv[0:NP, STEPS - 1, bass.ds(m, 1)]).then_inc(S["hi_ok"], 1)
                if has(8):
                    act.wait_ge(S["xnT_ps"], m - 7)
                    need(act, S["lg_ps"], m - 8)
                    a.activation(xnT, ps[:, 4, 0:DK * 128].rearrange("k (b p) -> k b p", b=DK)[:, :, 0:NP], ACT.Copy).then_inc(S["xnT_ok"], 1)
                if has(0) and has(1):
                    v_T()
                if u == 0 and has_unit(i, 1):
                    act.wait_ge(S["tile_ps"], n)
                    for k in range(2):
                        e = b2[bass.ds(2 * i - 2 + k, 1), :].broadcast_to([128, D])
                        act.dma_start(b2_part(bass.ds(WIN * i - WIN + PARTS_W[k][0], 1)), e).then_inc(S["b2_in"], 16)
                if u in (0, 2, 3) and has_unit(i, 1):
                    for layer in ((0, 1) if u == 0 else (u - 2,)):
                        if u > 0:
                            act.wait_ge(S["w_lo"], WP * (i - 1) + layer + 1)
                        e = bass.ds(2 * i - 2 + (u > 0), 1)
                        weights = (W1[e, :, :].rearrange("a (b k) h -> k (a b) h", k=128) if layer == 0 else
                                   W2[e, :, :].rearrange("a (b h) d -> h (a b) d", h=128))
                        act.dma_start(w_raw32(bass.ds(WIN * i - WIN + PART_RAW[layer], 1)).rearrange("p (b w) -> p b w", b=DK if layer == 0 else HK),
                                     weights).then_inc(w_raw_in[layer], 16)
            last_step(act, body)
            act.wait_ge(S["ex_in"], 1)
            a.activation(ex2, m2, ACT.Exp).then_inc(S["ex_ok"], 1)
            for n in range(T * TOP // CB):
                act.wait_ge(S["rt_by_c"], n + 1)
                by_p = planes[:, n, 0:FT, :]
                a.activation(by_p, by_p, ACT.Copy, scale=p_plus1[0:NP, 0:1]).then_inc(S["rt_done"], 1)
            a.activation(gb_max, gb_max, ACT.Gelu)
            act.wait_ge(S["tables_ok"], 1)

            def tile(i, u, e):
                j = FU * i + u
                r = u % 2
                act.wait_ge(S["ffn_h"], j + 1)
                need(act, S["hs_ok"], j - 1)
                for b in range(HK):
                    last = a.activation(h_g[r][:, b * 128:(b + 1) * 128], ps[:, 2 + r, b * 128:(b + 1) * 128], ACT.Gelu,
                                        bias=b1T[:, bass.ds(e * HK + b, 1)], scale=g1[:, bass.ds(e, 1)])
                last.then_inc(S["gelu_ok"], 1)

            def group(i):
                es = experts(i, act, 0, FU)
                for u in range(FU):
                    tile(i, u, es[u])
            group(0)
            with act.Fori(1, FT // FU) as i:
                group(i)
            for r in range(FR):
                act.wait_ge(y_out[r], 16 * (FT // FR))
            for i in range(NB):
                act.dma_start(y_in[i][1], y_v[1, :, i * WIN:(i + 1) * WIN, :]).then_inc(yc_in[1][i], 16)
            for i in range(NB):
                act.wait_ge(yc_in[1][i], 16)
                for t in range(WIN):
                    n = i * WIN + t
                    last = a.activation(y_in[i][1][:, t, :], y_in[i][1][:, t, :], ACT.Copy, scale=w_top2[:, n:n + 1])
                last.then_inc(S["y2_ok"], 1)

        @block.vector
        def _(dve):
            v = nc.vector
            dve.wait_ge(S["dst_in"], 32)
            v.tensor_scalar(key_t[0:NP, :], dst_i32[:, 0:EC].rearrange("p (j g) -> p j g", g=GRAN)[:, :, 0], 1.0 / WIN, 0.5 / WIN - 0.5,
                            ALU.mult, ALU.add)
            v.drain()
            v.tensor_scalar(key[0:NP, :], key_t[0:NP, :], ROUND, ROUND, ALU.add, ALU.subtract)
            dve.wait_ge(S["src_in"], 32)
            for k, ids in enumerate((src_i, dst_i32)):
                v.tensor_copy(edges[:, 0:EC, k], ids[:, 0:EC])
                v.tensor_copy(edges[0:NP - 1, EC:EC + TAIL, k], ids[0:NP - 1, EC:EC + TAIL])
            v.drain().then_inc(S["edges_ok"], 1)
            dve.wait_ge(S["iotas"], 1)
            v.drain()
            for j in range(COARSE):
                v.tensor_scalar(above[:, j, :], iota_g[0:NP, :], key[0:NP, j:j + 1], None, ALU.is_gt).then_inc(S["above_ok"], 1)
            v.tensor_scalar(ident_16, iota_row, iota_col, None, ALU.is_equal)
            v.tensor_scalar(ident, iota_row, iota_col, None, ALU.is_equal).then_inc(S["ident_ok"], 1)
            dve.wait_ge(S["w_in_in"], 48)
            v.tensor_tensor(w_sq, w_raw, w_raw, ALU.mult)
            v.tensor_tensor(b_sq, b_col, b_col, ALU.mult)
            v.tensor_reduce(b_abs, w_raw, AX.X, ALU.max, apply_absolute_value=True)
            v.drain()
            v.tensor_reduce(bound, w_sq, AX.X, ALU.add)
            v.tensor_tensor(b_abs, b_abs, b_abs, ALU.mult)
            v.drain()
            v.tensor_tensor(b_abs, b_abs, b_sq, ALU.max)
            v.scalar_tensor_tensor(bound, bound, float(D), b_sq, ALU.mult, ALU.add)
            v.drain()
            v.tensor_reduce(bmax[:, 1:2], b_abs, AX.X, ALU.max)
            v.tensor_reduce(bmax[:, 0:1], bound, AX.X, ALU.max)
            v.drain().then_inc(S["bound_ok"], 1)
            for t in range(T):
                if t % WIN == 0:
                    dve.wait_ge(x_in[t // WIN], 16)
                v.bn_stats(stats[0:NP, t, :], x_all[:, t, :])
            v.drain()
            for t in range(T):
                v.bn_aggr(mv[0:NP, t, :], stats[0:NP, t, :])
            v.drain()
            v.tensor_scalar(ve[0:NP, :], mv[0:NP, :, 1], 1e-5, None, ALU.add).then_inc(S["stats_ok"], 1)
            dve.wait_ge(S["count_ok"], 1)
            v.tensor_scalar(starts[0:NP, :], ps[0:NP, 6, 0:NR], -1.0, 0.0, ALU.add, ALU.max)
            v.drain()
            v.tensor_scalar(start_row[0:NP, :], starts[0:NP, :], float(ROWS - 1), None, ALU.min).then_inc(S["start_ok"], 1)
            dve.wait_ge(S["ball_ok"], 1)
            v.tensor_scalar(bmax, ball, 2.0, None, ALU.mult)
            v.drain()
            v.tensor_scalar(exp_i, bmax.bitcast(I32)[:, 0:1], 24, None, ALU.logical_shift_right)
            v.tensor_scalar(exp_w[:, 0:1], bmax.bitcast(I32)[:, 1:2], 24, None, ALU.logical_shift_right)
            v.drain()
            v.tensor_scalar(exp_j[:, 0:1], exp_i, -1.0, 202.0, ALU.mult, ALU.add)
            v.tensor_scalar(exp_j[:, 1:2], exp_i, 52.0, None, ALU.add)
            v.tensor_scalar(exp_w[:, 1:2], exp_w[:, 0:1], -1.0, 203.0, ALU.mult, ALU.add)
            v.tensor_scalar(exp_w[:, 2:3], exp_w[:, 0:1], 51.0, None, ALU.add)
            v.drain()
            v.tensor_scalar(scale[:, :].bitcast(I32), exp_j, 23, None, ALU.logical_shift_left)
            v.tensor_scalar(w_scale.bitcast(I32), exp_w[:, 1:2], 23, None, ALU.logical_shift_left)
            v.tensor_scalar(w_unscale.bitcast(I32), exp_w[:, 2:3], 23, None, ALU.logical_shift_left)
            v.drain()
            v.tensor_scalar(w_unscale, w_unscale, 1.0 / XS, None, ALU.mult)
            v.drain().then_inc(S["wscale_ok"], 1)
            dve.wait_ge(S["whi_ok"], 1)
            v.scalar_tensor_tensor(w_inL, ps[:, 7, :], w_scale[:, 0:1], w_inH, ALU.mult, ALU.subtract)
            v.scalar_tensor_tensor(b_lo[0:1, :], b_row[0:1, :], w_scale[0:1, 0:1], b_hi[0:1, :], ALU.mult, ALU.subtract)
            v.drain().then_inc(S["b_ok"], 1)
            dve.wait_ge(S["std_ok"], 1)
            newton(v, rstd[0:NP, :], ve[0:NP, :], rtmp[0:NP, :])
            v.tensor_scalar(rstd[0:NP, :], rstd[0:NP, :], XS, None, ALU.mult)
            v.drain()

            def normalise(i, u):
                v.tensor_scalar(x_n[u], of_tile(x_flat, i, u, 0, D), of_tile(mv_flat[0:NP, :], i, u, 0, 1),
                                of_tile(rstd[0:NP, :], i, u, 0, 1),
                                ALU.subtract, ALU.mult).then_inc(S["xn_ok"], 1)

            def transposed(i, u):
                n = WIN * i + u
                dve.wait_ge(S["xT_ok"], n + 1)
                v.tensor_tensor(xT_lo[RB[u]], ps[:, RB[u], 0:DK * 128].rearrange("k (b p) -> k b p", b=DK)[:, :, 0:NP],
                                xT_hi[RB[u]], ALU.subtract).then_inc(S["xlo_ok"], 1)

            def features(i, u):
                n = WIN * i + u
                dve.wait_ge(S["h_act"], n + 1)
                hi, lo = (of_tile(v_a[0:NP, :], i, u, k * D, D) for k in range(2))
                v.scalar_tensor_tensor(lo, h_f[u][0:NP, :], scale[0:NP, 0:1], hi, ALU.mult, ALU.subtract).then_inc(S["v_ready"], 1)

            def tile(i, u, has):
                if has(0):
                    normalise(i, u)
                if has(3):
                    transposed(i + (u - 3) // WIN, (u - 3) % WIN)
                if has(5):
                    features(i - 1, u)
            with_lag(dve, 5, tile)

            dve.wait_ge(S["iotas"], 2)
            dve.wait_ge(S["digits_ok"], 1)
            v.scalar_tensor_tensor(e_q, e_b, -float(T), e_q, ALU.mult, ALU.add)
            v.drain()
            v.tensor_scalar(e_k, e_q, -1.0, float(Q), ALU.max, ALU.min)
            v.drain().then_inc(S["keys_ok"], 1)
            dve.wait_ge(S["keyT_ps"], 1)
            for r in range(NR):
                v.tensor_copy(key_b[:, r, :, :, :].rearrange("e i k j -> e k i j"), keys_T(r, 0))
            dve.wait_ge(S["keyT_q"], NR)
            v.drain()
            kb = key_b.rearrange("e r i k j -> e (r i) (k j)")
            kq = key_q.rearrange("e r i k j -> e (r i) (k j)")

            def one_hots(r, i, u):
                bt = T * r + WIN * i + u
                dve.wait_ge(S["win_ps"], bt + 1)
                v.tensor_tensor(oh_b[RB[u]], iota_x, kb[:, bass.ds(bt, 1), :].broadcast_to([NP, NP, C]), ALU.is_equal)
                v.tensor_tensor(oh_q[RB[u]], iota_x, kq[:, bass.ds(bt, 1), :].broadcast_to([NP, NP, C]),
                                ALU.is_equal).then_inc(S["oh_ready"], 1)

            def total(n0, s, i, u, bank):
                t = WIN * i + u
                n = n0 + t
                dve.wait_ge(S["hi_ok"], n + 1)
                v.scalar_tensor_tensor(t_hi[0:NP, :], ps[0:NP, bank, D:2 * D], cinv[0:NP, s, bass.ds(t, 1)], t_hi[0:NP, :],
                                       ALU.mult, ALU.add).then_inc(S["psum_read"], 1)
                v.drain()
                if u % 2 == 0:
                    dve.wait_ge(h_in[0], 16 * (3 * (s * NB + i) + u // 2 + 1))
                else:
                    dve.wait_ge(h_in[1], 16 * (2 * (s * NB + i) + u // 2 + 1))
                v.scalar_tensor_tensor(t_hi[0:NP, :], h_ring[0:NP, u % 2, :], scale[0:NP, 0:1], t_hi[0:NP, :],
                                       ALU.mult, ALU.add).then_inc(S["h_used"], 1)

            def result(s, i, u, dest):
                t = WIN * i + u
                hi, lo = (dest[:, bass.ds(t, 1), k * D:(k + 1) * D].rearrange("p a f -> p (a f)") for k in range(2))
                total(s * T, s, i, u, u)
                v.drain()
                v.tensor_copy(hi, t_hi[0:NP, :])
                v.drain()
                v.tensor_tensor(lo, t_hi[0:NP, :], hi, ALU.subtract).then_inc(S["v_ready"], 1)
                v.drain()

            with dve.Fori(0, NB) as i:
                for u in range(WIN):
                    one_hots(0, i, u)
            dve.wait_ge(S["deg_ok"], 1)
            v.tensor_reduce(deg[0:NP, :].rearrange("p (r d) -> p r d", d=WIN), dl_eq, AX.X, ALU.add)
            v.drain()
            v.tensor_scalar(degc[0:NP, :], deg[0:NP, :], 1.0, None, ALU.max)
            v.tensor_reduce(in_windows[0:NP, :], deg[0:NP, :], AX.X, ALU.add)
            v.drain()
            v.reciprocal(degc[0:NP, :], degc[0:NP, :])
            v.drain()
            for s in range(STEPS):
                v.tensor_scalar(cinv[0:NP, s, :], degc[0:NP, :], 1.0 / (STEPS - s), None, ALU.mult)
            v.drain().then_inc(S["cover_sum"], 1)
            dve.sem_inc(S["psum_read"], 5)
            dve.sem_inc(S["h_used"], 2)

            def early(i, u):
                need(dve, early_out[RB[u]], 16 * uses(i, u, 0))
                total(0, 0, i, u, early_bank(u))

            def early_low(i, u):
                dve.wait_ge(S["early_hi"], WIN * i + u + 1)
                v.tensor_tensor(v_early[RB[u]][:, D:2 * D], t_hi[0:NP, :], v_early[RB[u]][:, 0:D], ALU.subtract).then_inc(S["v_ready"], 1)

            def group(r):
                for w in range(WIN):
                    for u in range(WIN):
                        one_hots(r, w, u)
                        if not (isinstance(r, int) and r == 1 and w == 0):
                            if u == EARLY_AT:
                                early(r - 1 + (w - 1) // WIN, (w - 1) % WIN)
                            if u == WIN - 1:
                                early_low(r - 1 + (w - 1) // WIN, (w - 1) % WIN)
            group(1)
            with dve.Fori(2, NR) as r:
                group(r)
            early(NR - 2, WIN - 1)
            early_low(NR - 2, WIN - 1)

            def step(s, dest, t0, t1):
                def tiles(i, pieces):
                    for u in range(WIN):
                        result(s, i, u, dest)
                        if pieces and u < WP:
                            count = (s - 1) * NE // 2 * WP + i * WP + u
                            dve.wait_ge(S["piece_in"], 16 * count + 16)
                            v.tensor_reduce(w_max[:, bass.ds(count, 1)], w_piece[:, :], AX.X, ALU.max,
                                            apply_absolute_value=True).then_inc(S["piece_used"], 1)
                step_groups(dve, s, t0, t1, tiles)
            dve.wait_ge(S["cover_ps"], 1)
            v.tensor_scalar(covered[:, :], ps[0:1, 7, 0:1], float(E), None, ALU.is_equal)
            v.drain().then_inc(S["cover_ok"], 1)
            fast = dve.value_load(covered[:, :], min_val=0, max_val=1)
            for r, per in enumerate((2, 2, 1)):
                dve.wait_ge(early_out[r], 16 * per * (EARLY // WIN))
            dve.sem_inc(S["piece_used"], 1)
            step(0, vb, EARLY, T)
            for s in range(1, STEPS - 1):
                step(s, vb if s % 2 == 0 else va, 0, T)
            with dve.If(fast == 0):
                dve.wait_ge(S["e_const"], 1)
                dve.wait_ge(S["e_in"], 48)
                v.tensor_copy(dst_e, dst_i)
                v.drain()
                with dve.Fori(0, STEPS) as s:
                    for part, (t0, count) in enumerate(PARTS):
                        with dve.Fori(0, EC // EU) as i:
                            for u in range(EU):
                                dve.wait_ge(S["e_mm"], s * (2 * EC) + i * EU + (part * EC + u + 1))
                                v.tensor_scalar(oh_e[u][:, 0:count, :], node[:, t0:t0 + count, :], dst_e[:, bass.ds(i * EU + u, 1)], None,
                                                ALU.is_equal).then_inc(S["e_oh"], 1)
                        dve.wait_ge(S["e_acc"], 2 * s + (part + 1))
                        dve.wait_ge(S["e_rows"], s * 16 + 16)
                        v.tensor_scalar(deg_e[:, t0:t0 + count], ps[0:NP, 7, 0:count], 1.0, None, ALU.max)
                        v.drain()
                        v.reciprocal(deg_e[:, t0:t0 + count], deg_e[:, t0:t0 + count])
                        v.drain()
                        v.tensor_scalar(deg_e[:, t0:t0 + count], deg_e[:, t0:t0 + count], k_inv[:, bass.ds(s, 1)], None, ALU.mult)
                        v.drain()
                        for t in range(count):
                            v.scalar_tensor_tensor(term_e[:, t0 + t, :], ps[0:NP, t // 2, t % 2 * D:(t % 2 + 1) * D],
                                                   deg_e[:, t0 + t:t0 + t + 1], h_e[:, t0 + t, :], ALU.mult, ALU.add)
                        v.drain().then_inc(S["e_read"], 1)
                    dve.sem_inc(S["e_term"], 1)
                dve.wait_ge(S["e_rows"], 16 * (STEPS + 2))
                v.memset(adj[:, :], 0.0)
                v.memset(v_b[:, :], 0.0)
                v.memset(cinv[:, STEPS - 1, :], 0.0)
                v.drain()
            v.drain().then_inc(S["term_ok"], 1)

            def pow2(scale_out, inv_out, square, pi, pj):
                v.tensor_scalar(pi, square.bitcast(I32), 24, None, ALU.logical_shift_right)
                v.drain()
                v.tensor_scalar(pj, pi, -1.0, 203.0, ALU.mult, ALU.add)
                v.tensor_scalar(pi, pi, 51.0, None, ALU.add)
                v.drain()
                v.tensor_scalar(scale_out.bitcast(I32), pj, 23, None, ALU.logical_shift_left)
                v.tensor_scalar(inv_out.bitcast(I32), pi, 23, None, ALU.logical_shift_left)
                v.drain()

            def scales():
                dve.wait_ge(S["f_const"], 96)
                v.tensor_reduce(w_top, w_max[:, :].rearrange("p (e b) -> p e b", b=WP), AX.X, ALU.max)
                v.tensor_reduce(b1_top, b1T.rearrange("p (e b) -> p e b", e=NE), AX.X, ALU.max, apply_absolute_value=True)
                v.drain().then_inc(S["w_top_ok"], 1)
                v.tensor_reduce(gb_max[:, 0:1], ga_bc, AX.X, ALU.max, apply_absolute_value=True)
                v.tensor_reduce(gb_max[:, 1:2], be_bc, AX.X, ALU.max, apply_absolute_value=True)
                v.drain()
                v.tensor_tensor(gb_sq, gb_max, gb_max, ALU.mult)
                v.drain()
                v.tensor_scalar(xn_sq[:, 0:1], gb_sq[:, 0:1], float(D), gb_sq[:, 1:2], ALU.mult, ALU.add)
                v.tensor_tensor(xn_sq[:, 1:2], gb_sq[:, 0:1], gb_sq[:, 1:2], ALU.add)
                v.drain()
                v.tensor_scalar(xn_sq[:, 0:1], xn_sq[:, 0:1], 2.0, None, ALU.mult)
                v.tensor_scalar(xn_sq[:, 1:2], xn_sq[:, 1:2], 2.0 * D, None, ALU.mult)
                v.drain()
                pow2(xs_scale[:, 0:1], xs_scale[:, 1:2], xn_sq[:, 0:1], pow_i[:, 0:1], pow_j[:, 0:1])
                dve.wait_ge(S["w_all_ok"], 1)
                v.tensor_tensor(w_all, w_all, w_all, ALU.mult)
                v.tensor_tensor(b1_all, b1_all, b1_all, ALU.mult)
                v.drain()
                pow2(sw, iw, w_all, pow_w, pow_v)
                v.tensor_scalar(w_top[:, 0:NE], w_all[:, 0:NE], xn_sq[:, 1:2], 2.0 * D, ALU.mult, ALU.mult)
                v.tensor_scalar(g1, iw[:, 0:NE], xs_scale[:, 1:2], None, ALU.mult)
                v.drain()
                v.scalar_tensor_tensor(w_top[:, 0:NE], b1_all, 2.0, w_top[:, 0:NE], ALU.mult, ALU.add)
                v.drain()
                pow2(sh, ih, w_top[:, 0:NE], pow_i, pow_j)
                v.tensor_tensor(g2, ih, iw[:, NE:2 * NE], ALU.mult)
                v.drain().then_inc(S["wsc_ok"], 1)

            def body(i, u, has):
                m = 5 * i + u
                n = LAST + m

                def logits():
                    w = m - 10
                    dve.wait_ge(S["lg_ps"], w + 1)
                    v.tensor_tensor(lg[:, bass.ds(w, 1), :].rearrange("p a e -> p (a e)"), ps[0:NP, 6, 0:NE], br_bc[0:NP, :],
                                    ALU.add).then_inc(S["lg_ok"], 1)
                if has(10) and has(0):
                    logits()
                if has(3):
                    xt = x1[:, bass.ds(m - 3, 1), :].rearrange("p a f -> p (a f)")
                    dve.wait_ge(S["y_ps"], m - 2)
                    dve.wait_ge(S["xb_ok"], m - 2)
                    v.scalar_tensor_tensor(xt, ps[0:NP, 5, 0:D], scale[0:NP, 1:2], x_i[ring(3, u)], ALU.mult, ALU.add).then_inc(S["x1_ok"], 1)
                    v.drain()
                    v.bn_stats(stats2, xt)
                    v.drain()
                    v.bn_aggr(mv_t, stats2)
                    v.drain()
                    v.tensor_copy(mv2[:, bass.ds(m - 3, 1), :].rearrange("p a f -> p (a f)"), mv_t)
                    v.drain()
                if u == 2 and has(7):
                    v.tensor_scalar(ve2, mv2[:, bass.ds(5 * (i - 1), WIN), 1], 1 + 1e-5, 1e-5 ** 2, ALU.mult, ALU.add)
                    v.drain().then_inc(S["ve_ok"], 1)
                    dve.wait_ge(S["sd_ok"], i)
                    newton(v, sd2, ve2, rt2)
                    v.tensor_copy(rr[:, bass.ds(5 * (i - 1), WIN)], sd2)
                    v.drain()
                if has(7):
                    w = m - 7
                    v.drain()
                    need(dve, S["xnT_ps"], w - 1)
                    need(dve, S["xhi_ok"], w - 1)
                    v.tensor_scalar(xn2[ring(7, u)], x1[:, bass.ds(w, 1), :].rearrange("p a f -> p (a f)"),
                                    mv2[:, bass.ds(w, 1), 0], rr[:, bass.ds(w, 1)], ALU.subtract, ALU.mult)
                    v.drain()
                    v.tensor_tensor(xn2[ring(7, u)], xn2[ring(7, u)], ga_bc[0:NP, :], ALU.mult).then_inc(S["z_ok"], 1)
                if has(8):
                    w = m - 8
                    dve.wait_ge(S["xhi_ok"], w + 1)
                    xs = xs_r[ring(8, u)]
                    v.scalar_tensor_tensor(xs[:, D:2 * D], xn2[ring(8, u)], xs_scale[0:NP, 0:1], xs[:, 0:D],
                                           ALU.mult, ALU.subtract).then_inc(S["xs_ok"], 1)
                if has(10) and not has(0):
                    logits()
                if has_unit(i, u):
                    e, layer = (u - 1) // 2, (u - 1) % 2
                    part = bass.ds(WIN * i - WIN + PARTS_W[e][layer], 1)
                    dve.wait_ge(S["w_hi"], WP * (i - 1) + u)
                    v.scalar_tensor_tensor(w_part(part, 1), w_raw32(bass.ds(WIN * i - WIN + PART_RAW[layer], 1)),
                                           sw[:, bass.ds(layer * NE + 2 * i - 2 + e, 1)], w_part(part, 0),
                                           ALU.mult, ALU.subtract).then_inc(S["w_lo"], 1)
                if has(0):
                    dve.wait_ge(S["hi_ok"], n + 1)
                    v.scalar_tensor_tensor(t_hi[0:NP, :], ps[0:NP, RB[u], D:2 * D], cinv[0:NP, STEPS - 1, bass.ds(m, 1)], t_hi[0:NP, :],
                                           ALU.mult, ALU.add).then_inc(S["psum_read"], 1)
                    v.drain()
                    if u % 2 == 0:
                        dve.wait_ge(h_in[0], 16 * (3 * ((STEPS - 1) * NB + i) + u // 2 + 1))
                    else:
                        dve.wait_ge(h_in[1], 16 * (2 * ((STEPS - 1) * NB + i) + u // 2 + 1))
                    need(dve, S["vT_ps"], m - 1)
                    v.scalar_tensor_tensor(vfin[RB[u]], h_ring[0:NP, u % 2, :], scale[0:NP, 0:1], t_hi[0:NP, :],
                                           ALU.mult, ALU.add).then_inc(S["h_used"], 1)
                    v.drain().then_inc(S["vfin_ok"], 1)
                if isinstance(i, int) and m == WIN - 1:
                    scales()
            last_step(dve, body)
            v.drain()
            bte = [NP, T, NE]
            e8 = iota_e8[:, None, :].broadcast_to(bte)
            v.tensor_reduce(m1, lg, AX.X, ALU.max)
            v.drain()

            def one_hot(out_, logits, m):
                v.tensor_tensor(tmp1, logits, m[:, :, None].broadcast_to(bte), ALU.is_equal)
                v.drain()
                v.tensor_tensor(tmp1, tmp1, e8, ALU.mult)
                v.drain()
                v.tensor_reduce(n1, tmp1, AX.X, ALU.min)
                v.drain()
                v.tensor_tensor(out_, e8, n1[:, :, None].broadcast_to(bte), ALU.is_equal)
                v.drain()
            one_hot(oh1, lg, m1)
            v.scalar_tensor_tensor(tmp2, oh1, -3e38, lg, ALU.mult, ALU.add)
            v.drain()
            v.tensor_reduce(m2, tmp2, AX.X, ALU.max)
            v.drain()
            one_hot(oh2, tmp2, m2)
            v.tensor_tensor(m2, m2, m1, ALU.subtract)
            v.drain().then_inc(S["ex_in"], 1)
            v.tensor_tensor(both, oh1, oh2, ALU.add)
            v.drain()
            v.tensor_reduce(per_p, both.rearrange("p t e -> p e t"), AX.X, ALU.add).then_inc(S["cnt_in"], 1)
            src_, d = both, 1
            bufs = [sum_a, sum_b]
            while d < T:
                dst_ = bufs[0]
                v.tensor_tensor(dst_[:, d:T, :], src_[:, d:T, :], src_[:, 0:T - d, :], ALU.add)
                v.tensor_copy(dst_[:, 0:d, :], src_[:, 0:d, :])
                v.drain()
                src_, d = dst_, 2 * d
                bufs = bufs[::-1]
            v.tensor_tensor(pos, src_, both, ALU.subtract)
            dve.wait_ge(S["cnt_ok"], 1)
            v.tensor_scalar(totals, ps[:, 7, 8:8 + NE], 127.0, 1.0 / 128, ALU.add, ALU.mult)
            v.drain()
            v.tensor_scalar(totals, totals, 1.0 / 256 - 0.5, None, ALU.add)
            v.drain()
            v.tensor_scalar(tiles_a, totals, ROUND, ROUND, ALU.add, ALU.subtract)
            v.drain()
            src_, d = tiles_a, 1
            bufs = [tiles_b, tiles_c]
            while d < NE:
                dst_ = bufs[0]
                v.tensor_tensor(dst_[:, d:NE], src_[:, d:NE], src_[:, 0:NE - d], ALU.add)
                v.tensor_copy(dst_[:, 0:d], src_[:, 0:d])
                v.drain()
                src_, d = dst_, 2 * d
                bufs = bufs[::-1]
            ends = src_
            v.tensor_tensor(totals, ends, tiles_a, ALU.subtract)
            v.drain()
            v.scalar_tensor_tensor(slot_base, totals[0:NP, :], 128.0, ps[0:NP, 7, 0:NE], ALU.mult, ALU.add)
            v.drain()
            v.tensor_tensor(pos, pos, slot_base[:, None, :].broadcast_to(bte), ALU.add)
            v.drain()
            for k, oh in enumerate((oh1, oh2)):
                v.tensor_tensor(tmp1, oh, pos, ALU.mult)
                v.drain()
                v.tensor_reduce(s_all[:, k * T:(k + 1) * T], tmp1, AX.X, ALU.add)
                v.drain()
            v.tensor_scalar(s_tile, s_all, 1.0 / 128, 1.0 / 256 - 0.5, ALU.mult, ALU.add)
            v.drain()
            v.tensor_scalar(s_tile, s_tile, ROUND, ROUND, ALU.add, ALU.subtract)
            v.drain()
            v.scalar_tensor_tensor(s_pin, s_tile, -128.0, s_all, ALU.mult, ALU.add)
            for r, per in enumerate((2, 2, 1)):
                dve.wait_ge(xs_out[r], 16 * per * NB)
            v.drain()
            v.tensor_copy(pin16.rearrange("p n c -> p (n c)"), s_pin)
            v.tensor_copy(tile16.rearrange("p n c -> p (n c)"), s_tile)
            dve.wait_ge(S["rt_const"], 1)
            v.drain()
            for n in range(T * TOP // CB):
                def along(row, width):
                    return row[:, n:n + 1, :].broadcast_to([NP, width, CB])
                by_p, by_c = planes[:, n, 0:FT, :], planes[:, n, FT:PL, :]
                v.tensor_tensor(by_p, iota_xc[:, 0:FT, :], along(tile16, FT), ALU.is_equal)
                v.tensor_tensor(oh_pos[:, n, :, :], iota_xc, along(pin16, 128), ALU.is_equal)
                v.drain()
                v.tensor_tensor(by_c, by_p, along(chunk16, FT), ALU.mult).then_inc(S["rt_by_c"], 1)
            dve.wait_ge(S["ex_ok"], 1)
            v.tensor_scalar(den, ex2, 1.0, None, ALU.add)
            v.drain()
            v.reciprocal(w_top1, den)
            v.drain()
            v.tensor_tensor(w_top2, ex2, w_top1, ALU.mult)
            v.tensor_tensor(le_tiles, tile_row[:, :, None].broadcast_to([128, FT, NE]),
                            ends[:, None, :].broadcast_to([128, FT, NE]), ALU.is_ge)
            v.drain()
            v.tensor_reduce(expert, le_tiles, AX.X, ALU.add)
            v.drain()
            dve.wait_ge(S["tok_ps"], 1)
            v.tensor_scalar(tok_p, ps[:, 0, 0:FT], -1.0, float(T), ALU.add, ALU.mult)
            v.tensor_scalar(empty, ps[:, 0, 0:FT], 0.0, 4.0 * TOP * N, ALU.is_equal, ALU.mult)
            v.tensor_copy(tok_b, ps[:, 0, FT:PL])
            v.drain()
            v.tensor_tensor(tok_p, tok_p, tok_b, ALU.add)
            v.tensor_scalar(tok_b, tok_b, float(T), None, ALU.is_ge)
            v.drain()
            v.scalar_tensor_tensor(tok_p, tok_b, -float(T), tok_p, ALU.mult, ALU.add)
            v.drain()
            v.scalar_tensor_tensor(dest, tok_b, float(N), tok_p, ALU.mult, ALU.add)
            v.tensor_scalar(idx_g, tok_p, 0.0, None, ALU.max)
            v.drain()
            v.tensor_tensor(dest, dest, empty, ALU.add)
            v.drain()
            v.tensor_copy(idx_s, dest)
            v.drain().then_inc(S["idx_ok"], 1)
            v.memset(exp_of[:, 0:LEAD], 0)
            v.memset(part1_of[:, 0:LEAD], 0)
            v.memset(part2_of[:, 0:LEAD], 0)
            v.tensor_scalar(expert, expert, float(NE - 1), None, ALU.min)
            v.drain()
            v.tensor_copy(exp_of[:, LEAD:], expert)
            v.tensor_scalar(tok_p, expert, 0.5, -0.25, ALU.mult, ALU.add)
            v.drain()
            v.tensor_scalar(tok_p, tok_p, ROUND, ROUND, ALU.add, ALU.subtract)
            v.drain()
            v.scalar_tensor_tensor(part1_of[:, LEAD:], expert, 2.0, tok_p, ALU.mult, ALU.add)
            v.tensor_scalar(tok_b, expert, 3.0, 1.0, ALU.mult, ALU.add)
            v.drain()
            v.tensor_tensor(part2_of[:, LEAD:], tok_b, tok_p, ALU.subtract)
            v.drain().then_inc(S["tables_ok"], 1)
            dve.wait_ge(S["b2_in"], 16 * NE)

            def transposed(i, u):
                j = FU * i + u
                r = u % 2
                dve.wait_ge(S["xg_T"], j + 1)
                need(dve, S["ffn_h"], j - XR + 1)
                v.tensor_copy(xT16[u % XR], ps[:, r, :].bitcast(F16)[:, 0:2 * D].rearrange("k (b s) -> k b s", b=2 * DK)).then_inc(S["xgT_ok"], 1)

            def hidden(i, u, b, e):
                j = FU * i + u
                r = u % 2
                dve.wait_ge(S["gelu_ok"], j + 1)
                need(dve, S["ffn_y"], j - FR + 1)
                hh, hl = h_hi[u % FR].rearrange("h b s -> h (b s)"), h_lo[u % FR].rearrange("h b s -> h (b s)")
                v.tensor_scalar(hh, h_g[r], sh[:, bass.ds(e, 1)], None, ALU.mult)
                v.drain()
                v.scalar_tensor_tensor(hl, h_g[r], sh[:, bass.ds(e, 1)], hh, ALU.mult, ALU.subtract).then_inc(S["hs_ok"], 1)

            def result(i, u, b, e, part, alone=False):
                j = FU * i + u
                r = u % 2
                dve.wait_ge(S["ffn_y"], j + 1)
                need(dve, y_out[u % FR], 16 * (FU // FR * i + u // FR))
                v.scalar_tensor_tensor(y_sb[u % FR], ps[:, 4 + r, 0:D], g2[:, bass.ds(e, 1)], b2_part(bass.ds(part, 1)),
                                       ALU.mult, ALU.add).then_inc(S["y_ok"], 1)
            ffn_tiles(dve, FT, FU, LAG, (experts,), (experts, parts1), 1, transposed, hidden, result)
            for i in range(NB):
                dve.wait_ge(yc_in[0][i], 16)
                for t in range(WIN):
                    n = i * WIN + t
                    v.scalar_tensor_tensor(x1[:, n, :], y_in[i][0][:, t, :], w_top1[:, n:n + 1], x1[:, n, :], ALU.mult, ALU.add)
                dve.wait_ge(S["y2_ok"], i + 1)
                v.drain()
                group = x1[:, i * WIN:(i + 1) * WIN, :]
                v.tensor_tensor(group, group, y_in[i][1], ALU.add).then_inc(S["comb_ok"], 1)

        @block.tensor
        def _(pe):
            te = nc.tensor
            pe.wait_ge(S["iotas"], 1)
            count = ps[0:NP, 6, 0:NR]
            te.matmul(count, ones16[0:NP, 0:NP], ones16[0:NP, 256:256 + NR], start=True, stop=False)
            for j in range(COARSE):
                pe.wait_ge(S["above_ok"], j + 1)
                for r in range(NR):
                    last = te.matmul(count[:, r:r + 1], above[:, j, :].rearrange("p (g r) -> p g r", r=NR)[:, :, r],
                                     ones16[0:NP, 0:1], start=False, stop=(j == COARSE - 1 and r == NR - 1))
            last.then_inc(S["count_ok"], 1)
            pe.wait_ge(S["ident_ok"], 1)
            pe.wait_ge(S["w_in_in"], 48)
            for kb in range(DK):
                for ob in range(DK):
                    last = te.transpose(ps[:, 7, (kb * DK + ob) * 128:(kb * DK + ob + 1) * 128],
                                        w_raw[:, ob, kb * 128:(kb + 1) * 128], ident)
            last.then_inc(S["wT_ps"], 1)
            pe.wait_ge(S["b_ok"], 1)

            def transposed(i, u):
                n = WIN * i + u
                pe.wait_ge(S["xn_ok"], n + 1)
                need(pe, S["xlo_ok"], n - AGE[u] + 1)
                for b in range(DK):
                    last = te.transpose(ps[:, RB[u], b * 128:b * 128 + NP], x_n[u][:, b * 128:(b + 1) * 128], ident[0:NP, 0:NP])
                last.then_inc(S["xT_ps"], 1)

            def features(i, u):
                n = WIN * i + u
                pe.wait_ge(S["xlo_ok"], n + 1)
                need(pe, S["h_act"], n - AGE[u] + 1)
                bank = ps[0:NP, 3 + RB[u], 0:D]
                te.matmul(bank, ones16[0:1, 128:128 + NP], b_hi[0:1, :], start=True, stop=False)
                te.matmul(bank, ones16[0:1, 128:128 + NP], b_lo[0:1, :], start=False, stop=False)
                for part, (xp, w) in enumerate(((xT_hi, w_inH), (xT_hi, w_inL), (xT_lo, w_inH))):
                    for b in range(DK):
                        last = te.matmul(bank, xp[RB[u]][:, b, :], w[:, b * D:(b + 1) * D],
                                         start=False, stop=(part == 2 and b == DK - 1))
                last.then_inc(S["h_ps"], 1)
            feature_tiles(pe, transposed, features)
            pe.wait_ge(S["h_act"], T)
            pe.wait_ge(S["keys_ok"], 1)
            for r in range(NR):
                for which, keys in enumerate((e_b, e_k)):
                    for k in range(SL):
                        last = te.transpose(key_block(r, which)[:, k, 0:NP], keys[:, r, k * NP:(k + 1) * NP], ident_16[0:NP, 0:NP])
            last.then_inc(S["keyT_ps"], 1)
            pe.sem_inc(S["win_ps"], 2)

            def windows(r, i, u):
                bt = T * r + WIN * i + u
                pe.wait_ge(S["oh_ready"], bt + 1)
                need(pe, S["win_out"], bt - 1)
                cells = win_cells(RB[u])
                for j in range(WIN):
                    for k in range(SL):
                        last = te.matmul(cells[:, j * 128:j * 128 + Q], oh_b[RB[u]][:, :, k * WIN + j], oh_q[RB[u]][:, :, k * WIN + j],
                                         start=(k == 0), stop=(k == SL - 1))
                last.then_inc(S["win_ps"], 1)

            def windows_only(i):
                for u in range(WIN):
                    windows(0, i, u)
            windows_only(0)
            with pe.Fori(1, NB) as i:
                windows_only(i)
            pe.wait_ge(S["v_ready"], T)

            def group(r):
                for w in range(WIN):
                    n = WIN * (r - 1) + w
                    for u in range(WIN):
                        windows(r, w, u)
                        parts = (0, 0, 0, 8, 16, T) if w == 0 else (0, 5, 10, 15, 20, T)
                        if parts[u] == 0 and parts[u + 1] > 0:
                            if w == 0:
                                pe.wait_ge(S["win_out"], T * r)
                            pe.wait_ge(S["psum_read"], n + 5 if w == 0 else n + 4)
                        for a in range(parts[u], parts[u + 1]):
                            last = te.matmul(ps[0:NP, early_bank(w), :], of_tile(adj[0:NP, 0:ADJ], r - 1, w, a * NP, NP),
                                             va[:, a, :], start=(a == 0), stop=(a == T - 1))
                    last.then_inc(S["tile_ps"], 1)
            group(1)
            with pe.Fori(2, NR) as r:
                group(r)
            pe.wait_ge(S["cover_sum"], 1)
            te.matmul(ps[0:1, 7, 0:1], in_windows[0:NP, :], ones_col[0:NP, :], start=True, stop=True).then_inc(S["cover_ps"], 1)
            pe.wait_ge(S["win_out"], NR * T)

            def step(n0, s, source, t0, t1):
                def tiles(i):
                    for u in range(WIN):
                        t = WIN * i + u
                        n = n0 + t
                        pe.wait_ge(S["psum_read"], n + 1)
                        pe.wait_ge(S["v_ready"], T * (s + 1) - 1)
                        for a in range(T):
                            if a == T - 1:
                                pe.wait_ge(S["v_ready"], T * (s + 1))
                            last = te.matmul(ps[0:NP, u, :], of_tile(adj[0:NP, 0:ADJ], i, u, a * NP, NP),
                                             source[:, a, :], start=(a == 0), stop=(a == T - 1))
                        last.then_inc(S["tile_ps"], 1)
                loop(pe, t0 // WIN, t1 // WIN, tiles)
            step(0, 0, va, EARLY, T)
            pe.wait_ge(S["cover_ok"], 1)
            fast = pe.value_load(covered[:, :], min_val=0, max_val=1)
            pe.wait_ge(S["early_back"], 16)
            for s in range(1, STEPS - 1):
                step(s * T, s, va if s % 2 == 0 else vb, 0, T)
            with pe.If(fast == 0):
                pe.wait_ge(S["psum_read"], LAST + 5)
                pe.wait_ge(S["e_const"], 1)
                pe.sem_inc(S["e_mm"], EU)
                pe.sem_inc(S["e_read"], 1)
                with pe.Fori(0, STEPS) as s:
                    for part, (t0, count) in enumerate(PARTS):
                        banks = [(b, min(512, count * D - b * 512)) for b in range((count + 1) // 2)] + [(7, count)]
                        pe.wait_ge(S["e_read"], 2 * s + (part + 1))
                        for b, n in banks:
                            te.matmul(ps[0:NP, b, 0:n], zeros_e[:, 0:NP], zeros_e[:, 0:n], start=True, stop=False)
                        with pe.Fori(0, EC // EU) as i:
                            for u in range(EU):
                                pe.wait_ge(S["e_oh"], s * (2 * EC) + i * EU + (part * EC + u + 1))
                                pe.wait_ge(e_gathered[u], s * (32 * EC // EU) + i * 16 + (part * 16 * EC // EU + 16))
                                for t in range(count):
                                    te.matmul(ps[0:NP, t // 2, t % 2 * D:(t % 2 + 1) * D], oh_e[u][:, t, :], rows_e[u], start=False, stop=False)
                                    last = te.matmul(ps[0:NP, 7, t:t + 1], oh_e[u][:, t, :], ones_e, start=False, stop=False)
                                last.then_inc(S["e_mm"], 1)
                        for b, n in banks:
                            last = te.matmul(ps[0:NP, b, 0:n], zeros_e[:, 0:NP], zeros_e[:, 0:n], start=False, stop=True)
                        last.then_inc(S["e_acc"], 1)
            pe.wait_ge(S["term_ok"], 1)
            pe.wait_ge(S["psum_read"], LAST + 5)

            def body(i, u, has):
                m = 5 * i + u
                n = LAST + m
                if has(0):
                    pe.wait_ge(S["psum_read"], n + 4)
                    for a in range(T):
                        last = te.matmul(ps[0:NP, RB[u], :], of_tile(adj[0:NP, 0:ADJ], i, u, a * NP, NP),
                                         vb[:, a, :], start=(a == 0), stop=(a == T - 1))
                    last.then_inc(S["tile_ps"], 1)
                if isinstance(i, int) and m == 0:
                    pe.wait_ge(S["w_out_in"], 16)
                    pe.wait_ge(S["pool_const"], 1)
                    for kb in range(DK):
                        for ob in range(DK):
                            last = te.transpose(ps[:, 7, (kb * DK + ob) * 128:(kb * DK + ob + 1) * 128],
                                                w_oraw[:, ob, kb * 128:(kb + 1) * 128], ident2)
                    last.then_inc(S["w_oT_ps"], 1)

                def graph_out():
                    pe.wait_ge(S["vT_ok"], m - 1)
                    if isinstance(i, int) and m == 2:
                        pe.wait_ge(S["w_oT_ok"], 1)
                    need(pe, S["x1_ok"], m - 2)
                    for b in range(DK):
                        last = te.matmul(ps[0:NP, 5, 0:D], vT[:, b, :], w_outT[:, b, :], start=(b == 0), stop=(b == DK - 1))
                    last.then_inc(S["y_ps"], 1)

                def v_T():
                    pe.wait_ge(S["vfin_ok"], m)
                    need(pe, S["vT_ok"], m - 1)
                    for b in range(DK):
                        last = te.transpose(ps[:, 3, b * 128:b * 128 + NP], vfin[ring(1, u)][:, b * 128:(b + 1) * 128], ident2[0:NP, 0:NP])
                    last.then_inc(S["vT_ps"], 1)

                if not has(0) and has(1):
                    v_T()
                if not has(0) and has(2):
                    graph_out()
                if has(8):
                    pe.wait_ge(S["xn2_ok"], m - 7)
                    need(pe, S["xnT_ok"], m - 8)
                    for b in range(DK):
                        last = te.transpose(ps[:, 4, b * 128:b * 128 + NP], xn2[ring(8, u)][:, b * 128:(b + 1) * 128], ident2[0:NP, 0:NP])
                    last.then_inc(S["xnT_ps"], 1)
                if has(9):
                    pe.wait_ge(S["xnT_ok"], m - 8)
                    if isinstance(i, int) and m == 9:
                        pe.wait_ge(S["f_const"], 96)
                    need(pe, S["lg_ok"], m - 9)
                    for b in range(DK):
                        last = te.matmul(ps[0:NP, 6, 0:NE], xnT[:, b, :], wr_sb[:, b, :], start=(b == 0), stop=(b == DK - 1))
                    last.then_inc(S["lg_ps"], 1)
                if has(0) and has(2):
                    graph_out()
                if has(0) and has(1):
                    v_T()
            last_step(pe, body)
            pe.wait_ge(S["cnt_in"], 1)
            te.matmul(ps[0:NP, 7, 0:NE], tri, per_p, start=True, stop=True)
            te.matmul(ps[:, 7, 8:8 + NE], ones2[0:NP, :], per_p, start=True, stop=True).then_inc(S["cnt_ok"], 1)
            for c in range(T * TOP):
                if c % CB == 0:
                    pe.wait_ge(S["rt_done"], c // CB + 1)
                last = te.matmul(ps[:, 0, 0:PL], oh_pos[:, c // CB, :, c % CB], planes[:, c // CB, :, c % CB],
                                 start=(c == 0), stop=(c == T * TOP - 1))
            last.then_inc(S["tok_ps"], 1)
            pe.wait_ge(S["tables_ok"], 1)
            pe.wait_ge(S["w_lo"], 2 * NE)

            def transposed(i, u):
                j = FU * i + u
                r = u % 2
                pe.wait_ge(g_in[u], 16 * (i + 1))
                if isinstance(i, int) and 2 <= j < 2 + LAG:
                    pe.wait_ge(S["xgT_ok"], j - 1)
                for b in range(2 * DK):
                    last = te.transpose(ps[:, r, :].bitcast(F16)[:, b * 128:(b + 1) * 128], x_g[u][:, b * 128:(b + 1) * 128], ident16)
                last.then_inc(S["xg_T"], 1)

            def hidden(i, u, b, part1):
                j = FU * i + u
                r = u % 2
                if b == 0:
                    if isinstance(i, int) and j < LAG:
                        pe.wait_ge(S["xgT_ok"], j + 1)
                    need(pe, S["gelu_ok"], j - 1)
                for n, (low, part) in enumerate(((0, 0), (0, 1), (1, 0))):
                    for k in range(DK):
                        at = k * H + b * 128
                        last = te.matmul(ps[:, 2 + r, b * 128:(b + 1) * 128],
                                         w_block(part1, low, at, 128),
                                         xT16[u % XR][:, part * DK + k, :], start=(n == 0 and k == 0), stop=(n == 2 and k == DK - 1))
                if b == HK - 1:
                    last.then_inc(S["ffn_h"], 1)

            def result(i, u, b, part2, alone=False):
                j = FU * i + u
                r = u % 2
                if b == 0 and alone:
                    pe.wait_ge(S["hs_ok"], j + 1)
                    pe.wait_ge(S["y_ok"], j - 1)
                elif b == 0:
                    pe.wait_ge(S["xgT_ok"], j + LAG + 1)
                for n, (hp, low) in enumerate(((h_hi, 0), (h_hi, 1), (h_lo, 0))):
                    last = te.matmul(ps[:, 4 + r, 0:D], hp[u % FR][:, b, :],
                                     w_block(part2, low, b * D, D),
                                     start=(b == 0 and n == 0), stop=(b == HK - 1 and n == 2))
                if b == HK - 1:
                    last.then_inc(S["ffn_y"], 1)
            ffn_tiles(pe, FT, FU, LAG, (parts1,), (parts2,), HK, transposed, hidden, result)


def ffn_tiles(eng, count, unroll, lag, hidden_tables, result_tables, steps, transposed, hidden, result):
    groups = count // unroll

    def entries(tables, i, first, tiles):
        return list(zip(*(load(i, eng, first, tiles) for load in tables)))

    def group(i, first, last):
        now, before = entries(hidden_tables, i, 0, unroll), entries(result_tables, i, -lag, unroll)
        for u in range(unroll):
            for b in range(steps):
                if not (first and u < lag):
                    result(i + (u - lag) // unroll, (u - lag) % unroll, b, *before[u])
                if b == 0 and not (last and u >= unroll - 2):
                    transposed(i + (u + 2) // unroll, (u + 2) % unroll)
                hidden(i, u, b, *now[u])
        if last:
            for u, values in enumerate(entries(result_tables, groups, -lag, lag)):
                for b in range(steps):
                    result(i, unroll - lag + u, b, *values, alone=True)

    transposed(0, 0)
    transposed(0, 1)
    group(0, True, False)
    with eng.Fori(1, groups - 1) as i:
        group(i, False, False)
    group(groups - 1, False, True)


def newton(v, r, var, tmp):
    v.reciprocal(r, r)
    v.drain()
    v.tensor_tensor(tmp, r, r, ALU.mult)
    v.drain()
    v.tensor_tensor(tmp, tmp, var, ALU.mult)
    v.drain()
    v.tensor_scalar(tmp, tmp, -0.5, 1.5, ALU.mult, ALU.add)
    v.drain()
    v.tensor_tensor(r, r, tmp, ALU.mult)
    v.drain()


_INS = ["x", "src", "dst", "L0_gnn_W_in", "L0_gnn_b_in", "L0_gnn_W_out", "L0_gnn_b_out", "L0_ffn_gamma", "L0_ffn_beta",
        "L0_ffn_Wr", "L0_ffn_br", "L0_ffn_W1", "L0_ffn_b1", "L0_ffn_W2", "L0_ffn_b2"]


def kernel(**inputs):
    import numpy as np
    import concourse.bacc as bacc
    from concourse.bass_utils import run_bass_kernel_spmd

    nc = bacc.Bacc("TRN2", target_bir_lowering=False, num_devices=1)
    arrays, args = {}, []
    for name in _INS:
        a = np.ascontiguousarray(inputs[name])
        arrays[name] = a
        args.append(nc.dram_tensor(name, a.shape, mybir.dt.from_np(a.dtype), kind="ExternalInput").ap())
    out = nc.dram_tensor("out", inputs["x"].shape, F32, kind="ExternalOutput").ap()
    gnn_ffn(nc, *args, out)
    return run_bass_kernel_spmd(nc, [arrays], core_ids=[0]).results[0]["out"]
```
